# Optimizing a Trainium2 kernel written in Bass

```python
import numpy as np
import jax
import jax.numpy as jnp

def _softmax(x, axis=-1):
    return jax.nn.softmax(x, axis=axis)

def _gelu(x):
    return jax.nn.gelu(x, approximate=True)

def _silu(x):
    return jax.nn.silu(x)

def _sigmoid(x):
    return jax.nn.sigmoid(x)

def _layernorm(x, axis=-1, eps=1e-05):
    m = jnp.mean(x, axis=axis, keepdims=True)
    v = jnp.var(x, axis=axis, keepdims=True)
    return (x - m) / jnp.sqrt(v + eps)

def _scatter_add(tgt, idx, src, axis=0):
    return tgt.at[idx].add(src)

def _segment_sum(src, seg, n):
    return jax.ops.segment_sum(src, seg, n)
kernel_name = 'mk_lm_tower_d1_tok_ids768_r4_78cf5c'

def setup_inputs(seed: int=0):
    np.random.seed(seed)
    _w = jnp.asarray

    def _rec_inputs():
        import jax
        import jax.numpy as jnp
        _rk = jax.random.key(seed)
        x = jax.random.randint(jax.random.fold_in(_rk, 1), (8, 512), 0, 8000, jnp.int32)
        return x
    x = _rec_inputs()

    def _L0_tok_setup():
        import jax, jax.numpy as jnp
        import numpy as np
        N_QUBITS = 6
        N_LAYERS = 3
        DIM = 1 << N_QUBITS
        VOCAB = 8000
        EMBED = 192
        B, S = (16, 1024)

        def _cnot_perm(control, target):
            idx = np.arange(DIM)
            cbit = idx >> N_QUBITS - 1 - control & 1
            flipped = idx ^ 1 << N_QUBITS - 1 - target
            return np.where(cbit == 1, flipped, idx)
        _idx = np.arange(DIM)
        Z_SIGNS = np.stack([1.0 - 2.0 * (_idx >> N_QUBITS - 1 - q & 1) for q in range(N_QUBITS)], axis=1).astype(np.float32)

        def _apply_ry(state, theta, q):
            T = state.shape[0]
            left, right = (1 << q, 1 << N_QUBITS - 1 - q)
            s = state.reshape(T, left, 2, right)
            c = jnp.cos(theta * 0.5)[:, None, None]
            sn = jnp.sin(theta * 0.5)[:, None, None]
            a0, a1 = (s[:, :, 0, :], s[:, :, 1, :])
            out = jnp.stack([c * a0 - sn * a1, sn * a0 + c * a1], axis=2)
            return out.reshape(T, DIM)

        def _apply_rz(state, theta, q):
            T = state.shape[0]
            left, right = (1 << q, 1 << N_QUBITS - 1 - q)
            s = state.reshape(T, left, 2, right)
            ph = jnp.exp(1j * (theta * 0.5)).astype(state.dtype)[:, None, None]
            out = jnp.stack([jnp.conj(ph) * s[:, :, 0, :], ph * s[:, :, 1, :]], axis=2)
            return out.reshape(T, DIM)

        def _circuit_expvals(params):
            T = params.shape[0]
            state = jnp.zeros((T, DIM), dtype=jnp.complex64).at[:, 0].set(1.0)
            for layer in range(N_LAYERS):
                for q in range(N_QUBITS):
                    state = _apply_ry(state, params[:, layer, q, 0], q)
                    state = _apply_rz(state, params[:, layer, q, 1], q)
                if layer < N_LAYERS - 1:
                    for q in range(N_QUBITS - 1):
                        state = state[:, _cnot_perm(q, q + 1)]
                    if N_QUBITS > 2:
                        state = state[:, _cnot_perm(N_QUBITS - 1, 0)]
            probs = state.real ** 2 + state.imag ** 2
            return probs @ jnp.asarray(Z_SIGNS)
        key = jax.random.key(seed)
        k1, k2, k3, k4 = jax.random.split(key, 4)
        token_ids = jax.random.randint(k1, (B, S), 0, VOCAB)
        quantum_params = jax.random.normal(k2, (VOCAB, N_LAYERS, N_QUBITS, 2), dtype=jnp.float32) * 0.1
        post_w = jax.random.normal(k3, (EMBED, N_QUBITS), dtype=jnp.float32) / np.sqrt(N_QUBITS)
        post_b = jax.random.normal(k4, (EMBED,), dtype=jnp.float32) * 0.01
        return {'token_ids': token_ids, 'quantum_params': quantum_params, 'post_w': post_w, 'post_b': post_b}
    _L0_tok_all = _L0_tok_setup()
    _L0_tok_in = {k: v for k, v in _L0_tok_all.items() if k in ('quantum_params', 'post_w', 'post_b')}
    del _L0_tok_all

    def _L0_attn_setup():
        import math
        import jax, jax.numpy as jnp
        import numpy as np
        B, N, D_IN, D_OUT = (8, 512, 192, 192)
        key = jax.random.key(seed)
        k1, k2, k3 = jax.random.split(key, 3)
        x = jax.random.normal(k1, (B, N, D_IN), dtype=jnp.float32)
        W_qkv = jax.random.normal(k2, (D_IN, 3 * D_OUT), dtype=jnp.float32) * (1.0 / math.sqrt(D_IN))
        b_qkv = jax.random.normal(k3, (3 * D_OUT,), dtype=jnp.float32) * 0.02
        return {'x': x, 'W_qkv': W_qkv, 'b_qkv': b_qkv}
    _L0_attn_all = _L0_attn_setup()
    _L0_attn_in = {k: v for k, v in _L0_attn_all.items() if k in ('W_qkv', 'b_qkv')}
    del _L0_attn_all

    def _L0_ffn_setup():
        import jax, jax.numpy as jnp
        import numpy as np
        B, S, D, H, E, K = (1, 512, 192, 384, 8, 2)
        key = jax.random.key(seed)
        ks = jax.random.split(key, 6)
        scale_d = 1.0 / np.sqrt(D)
        scale_h = 1.0 / np.sqrt(H)
        return {'x': jax.random.normal(ks[0], (B, S, D), dtype=jnp.float32), 'Wg': jax.random.uniform(ks[1], (D, E), minval=-scale_d, maxval=scale_d, dtype=jnp.float32), 'W1': jax.random.uniform(ks[2], (E, D, H), minval=-scale_d, maxval=scale_d, dtype=jnp.float32), 'b1': jax.random.uniform(ks[3], (E, H), minval=-scale_d, maxval=scale_d, dtype=jnp.float32), 'W2': jax.random.uniform(ks[4], (E, H, D), minval=-scale_h, maxval=scale_h, dtype=jnp.float32), 'b2': jax.random.uniform(ks[5], (E, D), minval=-scale_h, maxval=scale_h, dtype=jnp.float32)}
    _L0_ffn_all = _L0_ffn_setup()
    _L0_ffn_in = {k: v for k, v in _L0_ffn_all.items() if k in ('Wg', 'W1', 'b1', 'W2', 'b2')}
    del _L0_ffn_all
    return {'x': x, 'L0_tok_quantum_params': _L0_tok_in['quantum_params'], 'L0_tok_post_w': _L0_tok_in['post_w'], 'L0_tok_post_b': _L0_tok_in['post_b'], 'L0_attn_W_qkv': _L0_attn_in['W_qkv'], 'L0_attn_b_qkv': _L0_attn_in['b_qkv'], 'L0_ffn_Wg': _L0_ffn_in['Wg'], 'L0_ffn_W1': _L0_ffn_in['W1'], 'L0_ffn_b1': _L0_ffn_in['b1'], 'L0_ffn_W2': _L0_ffn_in['W2'], 'L0_ffn_b2': _L0_ffn_in['b2']}

def reference(x, L0_tok_quantum_params, L0_tok_post_w, L0_tok_post_b, L0_attn_W_qkv, L0_attn_b_qkv, L0_ffn_Wg, L0_ffn_W1, L0_ffn_b1, L0_ffn_W2, L0_ffn_b2):
    import jax
    import jax.numpy as jnp

    def _L0_tok_ref(token_ids, quantum_params, post_w, post_b):
        import jax, jax.numpy as jnp
        import numpy as np
        N_QUBITS = 6
        N_LAYERS = 3
        DIM = 1 << N_QUBITS
        VOCAB = 8000
        EMBED = 192
        B, S = (16, 1024)

        def _cnot_perm(control, target):
            idx = np.arange(DIM)
            cbit = idx >> N_QUBITS - 1 - control & 1
            flipped = idx ^ 1 << N_QUBITS - 1 - target
            return np.where(cbit == 1, flipped, idx)
        _idx = np.arange(DIM)
        Z_SIGNS = np.stack([1.0 - 2.0 * (_idx >> N_QUBITS - 1 - q & 1) for q in range(N_QUBITS)], axis=1).astype(np.float32)

        def _apply_ry(state, theta, q):
            T = state.shape[0]
            left, right = (1 << q, 1 << N_QUBITS - 1 - q)
            s = state.reshape(T, left, 2, right)
            c = jnp.cos(theta * 0.5)[:, None, None]
            sn = jnp.sin(theta * 0.5)[:, None, None]
            a0, a1 = (s[:, :, 0, :], s[:, :, 1, :])
            out = jnp.stack([c * a0 - sn * a1, sn * a0 + c * a1], axis=2)
            return out.reshape(T, DIM)

        def _apply_rz(state, theta, q):
            T = state.shape[0]
            left, right = (1 << q, 1 << N_QUBITS - 1 - q)
            s = state.reshape(T, left, 2, right)
            ph = jnp.exp(1j * (theta * 0.5)).astype(state.dtype)[:, None, None]
            out = jnp.stack([jnp.conj(ph) * s[:, :, 0, :], ph * s[:, :, 1, :]], axis=2)
            return out.reshape(T, DIM)

        def _circuit_expvals(params):
            T = params.shape[0]
            state = jnp.zeros((T, DIM), dtype=jnp.complex64).at[:, 0].set(1.0)
            for layer in range(N_LAYERS):
                for q in range(N_QUBITS):
                    state = _apply_ry(state, params[:, layer, q, 0], q)
                    state = _apply_rz(state, params[:, layer, q, 1], q)
                if layer < N_LAYERS - 1:
                    for q in range(N_QUBITS - 1):
                        state = state[:, _cnot_perm(q, q + 1)]
                    if N_QUBITS > 2:
                        state = state[:, _cnot_perm(N_QUBITS - 1, 0)]
            probs = state.real ** 2 + state.imag ** 2
            return probs @ jnp.asarray(Z_SIGNS)
        b, s = token_ids.shape
        params = quantum_params[token_ids.reshape(-1)]
        ev = _circuit_expvals(params)
        emb = ev @ post_w.T + post_b
        return emb.reshape(b, s, -1)

    def _L0_attn_ref(x, W_qkv, b_qkv):
        import math
        import jax, jax.numpy as jnp
        import numpy as np
        B, N, D_IN, D_OUT = (8, 512, 192, 192)
        d_out = D_OUT
        qkv = jnp.einsum('bnd,de->bne', x, W_qkv) + b_qkv
        q = qkv[:, :, :d_out]
        k = qkv[:, :, d_out:2 * d_out]
        v = qkv[:, :, 2 * d_out:3 * d_out]
        scale = 1.0 / math.sqrt(d_out)
        scores = jnp.einsum('bqd,bkd->bqk', q, k) * scale
        attn = jax.nn.softmax(scores, axis=-1)
        context = jnp.einsum('bqk,bkd->bqd', attn, v)
        return context

    def _L0_ffn_ref(x, Wg, W1, b1, W2, b2):
        import jax, jax.numpy as jnp
        import numpy as np
        B, S, D, H, E, K = (1, 512, 192, 384, 8, 2)
        gate_scores = jnp.einsum('bsd,de->bse', x, Wg)
        topk_scores, topk_idx = jax.lax.top_k(gate_scores, K)
        topk_probs = jax.nn.softmax(topk_scores, axis=-1)
        h = jax.nn.gelu(jnp.einsum('bsd,edh->bseh', x, W1) + b1, approximate=False)
        y = jnp.einsum('bseh,eho->bseo', h, W2) + b2
        y_sel = jnp.take_along_axis(y, topk_idx[..., None], axis=2)
        return jnp.sum(topk_probs[..., None] * y_sel, axis=2)
    h = _L0_tok_ref(x, L0_tok_quantum_params, L0_tok_post_w, L0_tok_post_b)
    h = h + _L0_attn_ref(_layernorm(h, axis=-1), L0_attn_W_qkv, L0_attn_b_qkv)
    h = h + _L0_ffn_ref(_layernorm(h, axis=-1), L0_ffn_Wg, L0_ffn_W1, L0_ffn_b1, L0_ffn_W2, L0_ffn_b2)
    return h

_drawn_inputs = setup_inputs


def setup_inputs(seed=0):
    import zlib

    import numpy as np

    out = dict(_drawn_inputs(seed))
    spreads = {}
    factors = {'L0_tok_quantum_params': 3.93,
     'L0_tok_post_b': 5.867,
     'L0_attn_b_qkv': 3.886,
     'L0_ffn_b1': 7.289,
     'L0_ffn_b2': 3.471}
    for name, (base, spread) in spreads.items():
        noise = np.random.default_rng([zlib.crc32(name.encode()), seed]).standard_normal(out[name].shape)
        drawn = base * np.exp(spread * noise) if base else spread * noise
        out[name] = jnp.asarray(drawn.astype(out[name].dtype))
    for name, factor in factors.items():
        out[name] = (out[name] * factor).astype(out[name].dtype)
    return out
```

```python
import itertools
import math
from contextlib import ExitStack

import numpy as np
import concourse.bass as bass
from concourse import mybir

ALU = mybir.AluOpType
ACT = mybir.ActivationFunctionType
AX = mybir.AxisListType
F32 = mybir.dt.float32
I32 = mybir.dt.int32
U32 = mybir.dt.uint32
BF16 = mybir.dt.bfloat16

QUBITS = 6
LAYERS = 3
ANGLES = LAYERS * QUBITS * 2
EPS = 1e-5
ROUNDER = 1.5 * 2.0 ** 23
TWO_PI_HIGH = 6.28125
TWO_PI_LOW = 2 * math.pi - TWO_PI_HIGH
PI_BELOW = 3.1415925
REDUCED = 10
TABLES_READY = 24
X_DONE = 52
CHAIN = 43


Z_SUPPORT = [list(range(1, QUBITS))] + [list(range(q + 1)) for q in range(1, QUBITS)]
X_SUPPORT = [[q, q + 1] for q in range(QUBITS - 1)] + [[QUBITS - 1, 0, 1]]
PAULI_CODE = {"I": 0, "Z": 1, "X": 2, "Y": 3}


def pauli_string(choice):
    x_all, z_all, phase = 0, 0, 0
    for j, name in choice:
        x = sum(1 << k for k in X_SUPPORT[j]) if name in "XY" else 0
        z = sum(1 << k for k in Z_SUPPORT[j]) if name in "ZY" else 0
        phase += (name == "Y") + 2 * bin(z_all & x).count("1")
        x_all, z_all = x_all ^ x, z_all ^ z
    names = ""
    for k in range(QUBITS):
        xk, zk = x_all >> k & 1, z_all >> k & 1
        names += "IXZY"[xk + 2 * zk]
        phase -= xk and zk
    assert phase % 2 == 0
    return names, 1 - phase % 4


def table_place(choice):
    names, sign = pauli_string(choice)
    low = sum(PAULI_CODE[names[k]] * 4 ** k for k in range(3))
    high = sum(PAULI_CODE[names[3 + k]] * 4 ** k for k in range(3))
    return low + (0 if sign > 0 else 64), high


def boxes(shape, place, most=3):
    left = set(itertools.product(*[range(s) for s in shape]))
    kinds = []
    for k in range(most, -1, -1):
        for dims in itertools.combinations(range(len(shape)), k):
            runs = [[(s, n, t) for t in (1, 2) for s in range(shape[d]) for n in range(shape[d], 1, -1)
                     if s + (n - 1) * t < shape[d]] for d in dims]
            for run in itertools.product(*runs):
                kinds.append((int(np.prod([n for _, n, _ in run])), dims, run))
    kinds.sort(key=lambda kind: -kind[0])
    found = []
    for size, dims, run in kinds:
        for base in sorted(left):
            if base not in left or any(base[d] != r[0] for d, r in zip(dims, run)):
                continue
            points = {}
            for step in itertools.product(*[range(r[1]) for r in run]):
                p = list(base)
                for d, r, o in zip(dims, run, step):
                    p[d] += r[2] * o
                points[step] = tuple(p)
            if not all(p in left for p in points.values()):
                continue
            origin = place(base)
            units = [tuple(int(j == i) for j in range(len(dims))) for i in range(len(dims))]
            slope = [tuple(a - b for a, b in zip(place(points[u]), origin)) for u in units]
            if all(place(p) == tuple(origin[h] + sum(o * s[h] for o, s in zip(step, slope)) for h in (0, 1))
                   for step, p in points.items()):
                found.append((base, [(d, r[1], r[2]) for d, r in zip(dims, run)], origin, slope))
                left -= set(points.values())
    assert not left
    return found


Z_BLOCK, at = {}, 0
for _q in list(range(1, QUBITS)) + [0]:
    Z_BLOCK[_q] = at
    at += 2 ** len(Z_SUPPORT[_q])
Z_STRINGS = at
PAIRS = QUBITS - 1
X_STRINGS = 9 * PAIRS + 27


def gather_products(eng, out, tables, n, shape, names, support, base, strides, log):
    def place(index):
        return table_place([(j, names[i]) for j, i in zip(support, index)])

    for first, dims, (low, high), slope in boxes(shape, place):
        at = base + sum(i * s for i, s in zip(first, strides))
        part_out, part_tab = out.ap[0][0], tables.ap[0][0]
        run = [(strides[d] * step, count) for d, count, step in dims]
        o = bass.AP(out.tensor, out.offset + at * n, [[part_out, 128]] + [[s * n, c] for s, c in run] + [[1, n]])
        a = bass.AP(tables.tensor, tables.offset + low * n,
                    [[part_tab, 128]] + [[s[0] * n, c] for s, (_, c) in zip(slope, run)] + [[1, n]])
        b = bass.AP(tables.tensor, tables.offset + (128 + high) * n,
                    [[part_tab, 128]] + [[s[1] * n, c] for s, (_, c) in zip(slope, run)] + [[1, n]])
        log(eng.tensor_tensor(o, a, b, ALU.mult))


def build(nc, token_ids, angles, emb_w, qkv_w, gate_w, up_w, down_w, down_b, out):
    P = 128
    TOKENS = token_ids.shape[0] * token_ids.shape[1]
    BATCHES, SEQ = token_ids.shape
    D = qkv_w.shape[1] // 3
    D0, D1 = P, D - P
    K1 = D1 + 1
    TILES = SEQ // P
    T = TOKENS // P
    E = gate_w.shape[1]
    HID = up_w.shape[1] // E
    HC = HID // P
    SCALE = 1.0 / math.sqrt(D)
    REGION = TOKENS + P
    PAD_ROW = E * REGION
    WIDTH = D + 5
    NO_TOKEN = 1.0e6
    UNROLL = 4
    ROWS_KEPT = 3
    BLOCKS = -(-(2 * TOKENS // P + E - 1) // UNROLL) * UNROLL
    EV_STRIDE = P // TILES

    routed = nc.dram_tensor("routed", (PAD_ROW + P, WIDTH), F32, kind="Internal").ap()
    ids_view = token_ids.rearrange("b (p j) -> p b j", j=TILES)
    out_rows = out.rearrange("b s d -> (b s) d")
    out_view = out.rearrange("b (p j) d -> b p (j d)", j=TILES)

    ctx = ExitStack()
    with ctx:
        def sb(name, shape, dt=F32):
            return ctx.enter_context(nc.sbuf_tensor(name, shape, dt))

        def bank(name):
            return ctx.enter_context(nc.psum_tensor(name, [P, 512], F32))

        def sem(name):
            return ctx.enter_context(nc.semaphore(name))

        ids = sb("ids", [P, BATCHES, TILES], I32)
        theta = sb("theta", [P, T, ANGLES])
        turns = sb("turns", [P, T, ANGLES])
        turned = sb("turned", [P, T, ANGLES])
        folded = sb("folded", [P, T, ANGLES])
        sine = sb("sine", [P, ANGLES, T])
        cosine = sb("cosine", [P, ANGLES, T])
        half_pi = sb("half_pi", [P, 1])
        bloch = sb("bloch", [P, QUBITS, 4, T])
        pair = sb("pair", [P, 2, 16, T])
        tables = sb("tables", [P, 192, T])
        ry = sb("ry", [P, QUBITS, 2, T])
        rzy = sb("rzy", [P, QUBITS, 3, T])
        z_both = sb("z_both", [P, 2, Z_STRINGS, T])
        z_coef = z_both[:, 0]
        z_str = z_both[:, 1]
        z_part = sb("z_part", [P, 28, T])
        x_str = sb("x_str", [P, X_STRINGS, T])
        x_sum = sb("x_sum", [P, X_STRINGS // 3, T])
        x_sum2 = sb("x_sum2", [P, X_STRINGS // 9, T])
        z_exp = sb("z_exp", [P, QUBITS, T])
        x_exp = sb("x_exp", [P, QUBITS, T])
        ev = sb("ev", [P, T, EV_STRIDE])
        ident = sb("ident", [P, P])
        ones = sb("ones", [P, P])
        before_f = sb("before_f", [P, P])
        before = sb("before", [P, P], BF16)
        ones_b = sb("ones_b", [P, P], BF16)
        minus_half = sb("minus_half", [P, TILES])
        tok_i = sb("tok_i", [P, T], I32)
        tok = sb("tok", [P, T])
        blk_i = sb("blk_i", [P, BLOCKS], I32)
        blk = sb("blk", [P, BLOCKS])
        exp_i = sb("exp_i", [P, E], I32)
        exp_f = sb("exp_f", [P, E])
        region_f = sb("region_f", [P, E])
        pad_rows = sb("pad_rows", [P, WIDTH])
        wz = sb("wz", [P, TILES, D])
        wqkv0 = sb("wqkv0", [P, 3 * D])
        wqkv1 = sb("wqkv1", [K1, 3 * D])
        wg0 = sb("wg0", [P, E])
        wg1 = sb("wg1", [D1, E])
        wqk_t0 = sb("wqk_t0", [P, 2, D + 1])
        wqk_t1 = sb("wqk_t1", [D1, 2, D + 1])
        score_w0 = sb("score_w0", [P, D + 1])
        score_w1 = sb("score_w1", [K1, D + 1])
        up0 = sb("up0", [P, E * HID])
        up1 = sb("up1", [K1, E * HID])
        spare = tables[:, :, :].rearrange("p f t -> p (f t)")
        down = spare[:, 0:E * HC * D]
        down_bias = spare[:, E * HC * D:E * HC * D + E * D]
        z_flat = z_both[:, :, :, :].rearrange("p a k t -> p (a k t)")
        taken = [0]

        def behind_circuit(pattern, **sizes):
            size = int(np.prod(list(sizes.values())))
            view = z_flat[:, taken[0]:taken[0] + size].rearrange(pattern, **sizes)
            taken[0] += size
            return view

        hres = behind_circuit("p (t d) -> p t d", t=T, d=D)
        ev_b = sb("ev_b", [P, P])
        ev_t = sb("ev_t", [P, P])
        bn1 = sb("bn1", [P, TILES, 6])
        mv1 = sb("mv1", [P, TILES, 2])
        ve1 = sb("ve1", [P, TILES])
        rs1 = sb("rs1", [P, TILES])
        x1 = behind_circuit("p (j d) -> p j d", j=TILES, d=D)
        xt0 = sb("xt0", [P, SEQ])
        xt1 = sb("xt1", [K1, SEQ])
        tq0 = sb("tq0", [P, SEQ])
        tq1 = sb("tq1", [K1, SEQ])
        val = behind_circuit("p (j d) -> p j d", j=TILES, d=D)
        nmax = sb("nmax", [P, 2])
        rsum = sb("rsum", [P, 2])
        rinv = sb("rinv", [P, 2])
        prob = behind_circuit("p (c k) -> p c k", c=2, k=SEQ)
        prob_t = behind_circuit("p (c k) -> p c k", c=2, k=SEQ)
        bn2 = sb("bn2", [P, 2, 6])
        mv2 = sb("mv2", [P, 2, 2])
        ve2 = sb("ve2", [P, 2])
        rs2 = sb("rs2", [P, 2])
        x2 = sb("x2", [P, ROWS_KEPT, TILES, WIDTH])
        x2t0 = sb("x2t0", [P, P])
        x2t1 = sb("x2t1", [D1, P])
        logit = sb("logit", [P, TILES, E])
        top = sb("top", [P, TILES, E])
        top_i = sb("top_i", [P, TILES, E], U32)
        gap = sb("gap", [P, TILES])
        gap_e = sb("gap_e", [P, TILES])
        gap_1 = sb("gap_1", [P, TILES])
        mask = sb("mask", [P, 2, TILES, E])
        both = sb("both", [P, TILES, E])
        ahead = sb("ahead", [P, TILES, E])
        here = sb("here", [P, E])
        here_b = sb("here_b", [P, E], BF16)
        so_far = sb("so_far", [P, E], BF16)
        rank = sb("rank", [P, E])
        place = sb("place", [P, TILES, E])
        slot_e = sb("slot_e", [P, 2, TILES, E])
        slot_f = sb("slot_f", [P, 2, TILES])
        slot = sb("slot", [P, ROWS_KEPT, 2, TILES], I32)
        count = sb("count", [P, E])
        count_i = sb("count_i", [P, E], I32)
        nblk_i = sb("nblk_i", [P, E], I32)
        nblk = sb("nblk", [P, E])
        cum = sb("cum", [P, 2, E])
        skip = sb("skip", [P, E])
        ge = sb("ge", [P, E, BLOCKS])
        ge_w = sb("ge_w", [P, E - 1, BLOCKS])
        t_exp = sb("t_exp", [P, BLOCKS])
        t_row = sb("t_row", [P, BLOCKS])
        t_first = sb("t_first", [P, BLOCKS])
        t_i = sb("t_i", [P, 3, BLOCKS], I32)
        xb = sb("xb", [P, UNROLL, WIDTH])
        xbt0 = sb("xbt0", [P, P])
        xbt1 = sb("xbt1", [K1, P])
        hid = sb("hid", [P, 2, HID])
        hid_t = sb("hid_t", [P, HID])
        share = sb("share", [P, UNROLL])
        share_w = sb("share_w", [P, UNROLL, 2])
        dest = sb("dest", [P, UNROLL], I32)
        y_raw = sb("y_raw", [P, 2, D])
        y = sb("y", [P, UNROLL, D])

        b0, b1, b2, b3, b4, b5, b6, b7 = [bank(f"bank{i}") for i in range(8)]

        ids_in = sem("ids_in")
        angles_in = sem("angles_in")
        small_in = sem("small_in")
        up_in = sem("up_in")
        down_in = sem("down_in")
        const_done = sem("const_done")
        dve_step = sem("dve_step")
        trig_done = sem("trig_done")
        x_step = sem("x_step")
        pool_step = sem("pool_step")
        wt_done = sem("wt_done")
        wt_copied = sem("wt_copied")
        sw_done = sem("sw_done")
        ev_done = sem("ev_done")
        ev_copied = sem("ev_copied")
        evt_done = sem("evt_done")
        evt_copied = sem("evt_copied")
        emb_done = sem("emb_done")
        emb_copied = sem("emb_copied")
        var1_done = sem("var1_done")
        x1_done = sem("x1_done")
        rs1_done = sem("rs1_done")
        rs2_done = sem("rs2_done")
        rows_free = sem("rows_free")
        xt_done = sem("xt_done")
        xt_copied = sem("xt_copied")
        tq_done = sem("tq_done")
        tq_copied = sem("tq_copied")
        val_done = sem("val_done")
        val_copied = sem("val_copied")
        score_done = sem("score_done")
        max_done = sem("max_done")
        exp_done = sem("exp_done")
        pt_done = sem("pt_done")
        pt_copied = sem("pt_copied")
        pv_done = sem("pv_done")
        h2_done = sem("h2_done")
        var2_done = sem("var2_done")
        x2_done = sem("x2_done")
        x2t_done = sem("x2t_done")
        x2t_copied = sem("x2t_copied")
        logit_done = sem("logit_done")
        logit_copied = sem("logit_copied")
        gap_done = sem("gap_done")
        gap_exp = sem("gap_exp")
        mask_done = sem("mask_done")
        rank_done = sem("rank_done")
        rank_copied = sem("rank_copied")
        slot_done = sem("slot_done")
        scattered = sem("scattered")
        h2_out = sem("h2_out")
        count_done = sem("count_done")
        count_copied = sem("count_copied")
        table_done = sem("table_done")
        pads_out = sem("pads_out")
        block_in = [sem(f"block_in{i}") for i in range(UNROLL)]
        xbt_done = sem("xbt_done")
        xbt_copied = sem("xbt_copied")
        up_done = sem("up_done")
        gelu_done = sem("gelu_done")
        ht_done = sem("ht_done")
        ht_copied = sem("ht_copied")
        share_done = sem("share_done")
        y_mm = sem("y_mm")
        y_read = sem("y_read")
        y_done = sem("y_done")
        added = [sem(f"added{i}") for i in range(UNROLL)]
        passed = sem("passed")

        def hold(eng):
            eng.sem_inc(passed, 1)

        block = ctx.enter_context(nc.Block())

        @block.sync
        def _(sp):
            sp.dma_start(ids[:, :, :], ids_view).then_inc(ids_in, 16)
            sp.dma_start(wqkv0[:, :], qkv_w[0:P, :]).then_inc(small_in, 16)
            sp.dma_start(wqkv1[:, :], qkv_w[P:D + 1, :]).then_inc(small_in, 16)
            sp.dma_start(wz[:, :, :], emb_w.rearrange("p (j d) -> p j d", j=TILES)).then_inc(small_in, 16)
            sp.dma_start(wg0[:, :], gate_w[0:P, :]).then_inc(small_in, 16)
            sp.dma_start(wg1[:, :], gate_w[P:D, :]).then_inc(small_in, 16)
            sp.dma_start(up0[:, :], up_w[0:P, :]).then_inc(up_in, 16)
            sp.dma_start(up1[:, :], up_w[P:D + 1, :]).then_inc(up_in, 16)
            sp.wait_ge(const_done, 1)
            sp.dma_start(routed[PAD_ROW:PAD_ROW + P, :], pad_rows[:, :]).then_inc(pads_out, 16)
            sp.wait_ge(ev_done, 1)
            sp.dma_start(down, down_w).then_inc(down_in, 16)
            sp.dma_start(down_bias, down_b.partition_broadcast(P)).then_inc(down_in, 16)
            with sp.Fori(0, BATCHES) as b:
                sp.wait_ge(h2_done, b * TILES + TILES)
                sp.dma_start(out_view[bass.ds(b, 1)].rearrange("o p f -> (o p) f"),
                             hres[:, bass.ds(b * TILES, TILES), :].rearrange("p j d -> p (j d)")).then_inc(h2_out, 16)
            sp.wait_ge(count_copied, 2)
            for e in range(E):
                rows = sp.value_load(count_i[0:1, e:e + 1], min_val=0, max_val=TOKENS)
                sp.dma_start(routed[bass.ds(rows + e * REGION, P), :], pad_rows[:, :]).then_inc(pads_out, 16)
            sp.wait_ge(pads_out, 16 * E + 16)
            sp.wait_ge(scattered, 16 * 2 * T)
            sp.wait_ge(table_done, 1)
            for n in range(UNROLL):
                row = sp.value_load(t_i[0:1, 1, n:n + 1], min_val=0, max_val=PAD_ROW)
                sp.dma_start(xb[:, n, :], routed[bass.ds(row, P), :]).then_inc(block_in[n], 16)
            with sp.Fori(0, BLOCKS // UNROLL - 1) as it:
                for n in range(UNROLL):
                    row = sp.value_load(t_i[0:1, 1, bass.ds((it + 1) * UNROLL + n, 1)], min_val=0, max_val=PAD_ROW)
                    sp.wait_ge(xbt_done, it * UNROLL + n + 1)
                    sp.wait_ge(share_done, (it * UNROLL + n) * 2 + 2)
                    sp.dma_start(xb[:, n, :], routed[bass.ds(row, P), :]).then_inc(block_in[n], 16)
            sp.wait_ge(h2_out, 16 * BATCHES)
            for n in range(UNROLL):
                sp.wait_ge(added[n], 16 * (BLOCKS // UNROLL) + 16)

        @block.gpsimd
        def _(pool):
            steps = [0]

            def step(instruction):
                steps[0] += 1
                instruction.then_inc(pool_step, 1)

            def join():
                pool.wait_ge(pool_step, steps[0])

            step(pool.memset(pad_rows[:, :], 0.0))
            join()
            pool.memset(pad_rows[:, WIDTH - 1:WIDTH], NO_TOKEN).then_inc(const_done, 1)
            pool.wait_ge(ids_in, 16)
            for t in range(T):
                b, j = divmod(t, TILES)
                pool.indirect_dma_start(out=theta[:, t, :], out_offset=None, in_=angles,
                                        in_offset=bass.IndirectOffsetOnAxis(ids[:, b, j:j + 1], 0)
                                        ).then_inc(angles_in, 16)
            step(pool.memset(ident[:, :], 0.0))
            step(pool.memset(ones[:, :], 1.0))
            step(pool.memset(minus_half[:, :], -0.5))
            step(pool.memset(ones_b[:, :], 1.0))
            step(pool.memset(so_far[:, :], 0.0))
            step(pool.iota(tok_i[:, :], [[SEQ, BATCHES], [1, TILES]], base=0, channel_multiplier=TILES))
            step(pool.iota(blk_i[:, :], [[1, BLOCKS]], base=0, channel_multiplier=0))
            step(pool.iota(exp_i[:, :], [[1, E]], base=0, channel_multiplier=0))
            join()
            step(pool.affine_select(out=ident[:, :], in_=ident[:, :], compare_op=ALU.not_equal, fill=1.0, base=0,
                                    pattern=[[-1, P]], channel_multiplier=1))
            step(pool.affine_select(out=before_f[:, :], in_=ones[:, :], compare_op=ALU.is_gt, fill=0.0, base=0,
                                    pattern=[[1, P]], channel_multiplier=-1))
            step(pool.tensor_copy(tok[:, :], tok_i[:, :]))
            step(pool.tensor_copy(blk[:, :], blk_i[:, :]))
            step(pool.tensor_copy(exp_f[:, :], exp_i[:, :]))
            join()
            step(pool.tensor_copy(before[:, :], before_f[:, :]))
            step(pool.tensor_scalar(region_f[:, :], exp_f[:, :], float(REGION), None, ALU.mult))
            join()
            pool.tensor_copy(exp_f[:, :], exp_i[:, :]).then_inc(const_done, 1)

            xsteps = [0]

            def xstep(instruction):
                xsteps[0] += 1
                instruction.then_inc(x_step, 1)

            def xjoin():
                pool.wait_ge(x_step, xsteps[0])

            pool.wait_ge(dve_step, TABLES_READY)
            for q in range(PAIRS):
                gather_products(pool, x_str[:, :, :], tables[:, :, :], T, [3, 3], "XYZ", X_SUPPORT[q], 9 * q, [3, 1],
                                xstep)
            gather_products(pool, x_str[:, :, :], tables[:, :, :], T, [3, 3, 3], "XYZ", X_SUPPORT[PAIRS], 9 * PAIRS,
                            [9, 3, 1], xstep)
            xjoin()
            pairs = x_str[:, 0:9 * PAIRS].rearrange("p (q a b) t -> p q a b t", q=PAIRS, a=3)
            for q in range(PAIRS):
                xstep(pool.tensor_tensor(pairs[:, q], pairs[:, q],
                                         rzy[:, q + 1].unsqueeze(1).to_broadcast([P, 3, 3, T]), ALU.mult))
            triple = x_str[:, 9 * PAIRS:X_STRINGS].rearrange("p (a b) t -> p a b t", b=3)
            xstep(pool.tensor_tensor(triple, triple, rzy[:, 1].unsqueeze(1).to_broadcast([P, 9, 3, T]), ALU.mult))
            xjoin()
            by3 = x_str[:, :, :].rearrange("p (a b) t -> p a b t", b=3)
            xstep(pool.tensor_tensor(x_sum[:, :, :], by3[:, :, 0], by3[:, :, 1], ALU.add))
            xjoin()
            xstep(pool.tensor_tensor(x_sum[:, :, :], x_sum[:, :, :], by3[:, :, 2], ALU.add))
            xjoin()
            xstep(pool.tensor_tensor(x_sum[:, 0:3 * PAIRS], x_sum[:, 0:3 * PAIRS],
                                     rzy[:, 0:PAIRS].rearrange("p q a t -> p (q a) t"), ALU.mult))
            triple2 = x_sum[:, 3 * PAIRS:].rearrange("p (a b) t -> p a b t", b=3)
            xstep(pool.tensor_tensor(triple2, triple2, rzy[:, 0].unsqueeze(1).to_broadcast([P, 3, 3, T]), ALU.mult))
            xjoin()
            sum_by3 = x_sum[:, :, :].rearrange("p (a b) t -> p a b t", b=3)
            xstep(pool.tensor_tensor(x_sum2[:, :, :], sum_by3[:, :, 0], sum_by3[:, :, 1], ALU.add))
            xjoin()
            xstep(pool.tensor_tensor(x_sum2[:, :, :], x_sum2[:, :, :], sum_by3[:, :, 2], ALU.add))
            xjoin()
            xstep(pool.tensor_copy(x_exp[:, 0:PAIRS], x_sum2[:, 0:PAIRS]))
            xstep(pool.tensor_tensor(x_sum2[:, PAIRS:], x_sum2[:, PAIRS:], rzy[:, PAIRS], ALU.mult))
            xjoin()
            xstep(pool.tensor_tensor(x_exp[:, PAIRS], x_sum2[:, PAIRS], x_sum2[:, PAIRS + 1], ALU.add))
            xjoin()
            xstep(pool.tensor_tensor(x_exp[:, PAIRS], x_exp[:, PAIRS], x_sum2[:, PAIRS + 2], ALU.add))
            assert xsteps[0] == X_DONE, xsteps

            def copy_ev(b):
                if not (isinstance(b, int) and b == 0):
                    pool.wait_ge(evt_done, b)
                pool.tensor_copy(ev_b[:, :], ev[:, bass.ds(b * TILES, TILES), :].rearrange("p j e -> p (j e)")
                                 ).then_inc(ev_copied, 1)

            def rstd1(b):
                pool.wait_ge(var1_done, b + 1)
                pool.tensor_tensor(rs1[:, :], ve1[:, :], minus_half[:, :], ALU.pow).then_inc(rs1_done, 1)

            def rstd2(b, s):
                pool.wait_ge(var2_done, b * TILES + s + 1)
                pool.tensor_tensor(rs2[:, s % 2:s % 2 + 1], ve2[:, s % 2:s % 2 + 1], minus_half[:, 0:1], ALU.pow
                                   ).then_inc(rs2_done, 1)

            def scatter(b, kept):
                pool.wait_ge(slot_done, b + 1)
                hold(pool)
                for j in range(TILES):
                    for k in range(2):
                        pool.indirect_dma_start(out=routed, out_offset=bass.IndirectOffsetOnAxis(
                            slot[:, kept, k, j:j + 1], 0), in_=x2[:, kept, j, :], in_offset=None).then_inc(scattered, 16)
                pool.wait_ge(scattered, (b + 1) * (16 * 2 * TILES))
                pool.sem_inc(rows_free, 1)

            step(pool.memset(dest[:, :], TOKENS))
            step(pool.memset(y[:, :, :], 0.0))
            join()
            for n in range(UNROLL):
                pool.indirect_dma_start(out=out_rows, out_offset=bass.IndirectOffsetOnAxis(dest[:, n:n + 1], 0),
                                        in_=y[:, n, :], in_offset=None, bounds_check=TOKENS - 1,
                                        oob_is_err=False, compute_op=ALU.add).then_inc(added[n], 16)
            pool.sem_inc(rows_free, ROWS_KEPT - 1)
            pool.wait_ge(ev_done, 1)
            copy_ev(0)
            rstd1(0)

            def batch(b, kept, first=False, last=False):
                if not last:
                    copy_ev(b + 1)
                rstd2(b, 0)
                if not last:
                    rstd1(b + 1)
                rstd2(b, 1)
                rstd2(b, 2)
                rstd2(b, 3)
                if not first:
                    scatter(b - 1, (kept - 1) % ROWS_KEPT)

            batch(0, 0, first=True)
            with pool.Fori(0, (BATCHES - 2) // ROWS_KEPT) as i:
                for k in range(ROWS_KEPT):
                    batch(ROWS_KEPT * i + k + 1, (k + 1) % ROWS_KEPT)
            batch(BATCHES - 1, (BATCHES - 1) % ROWS_KEPT, last=True)
            scatter(BATCHES - 1, (BATCHES - 1) % ROWS_KEPT)

            pool.wait_ge(h2_out, 16 * BATCHES)
            pool.wait_ge(table_done, 1)
            with pool.Fori(0, BLOCKS // UNROLL) as it:
                for n in range(UNROLL):
                    m = it * UNROLL + n
                    first_of_expert = pool.value_load(t_i[0:1, 2, bass.ds(m, 1)], min_val=0, max_val=BLOCKS)
                    pool.wait_ge(y_done, m + 1)
                    for k in range(UNROLL):
                        pool.wait_ge(added[k], (first_of_expert + (UNROLL - 1 - k)) // UNROLL * 16 + 16)
                    hold(pool)
                    pool.indirect_dma_start(out=out_rows, out_offset=bass.IndirectOffsetOnAxis(dest[:, n:n + 1], 0),
                                            in_=y[:, n, :], in_offset=None, bounds_check=TOKENS - 1,
                                            oob_is_err=False, compute_op=ALU.add).then_inc(added[n], 16)

        @block.vector
        def _(dve):
            steps = [0]

            def step(instruction):
                steps[0] += 1
                instruction.then_inc(dve_step, 1)

            def join():
                dve.wait_ge(dve_step, steps[0])

            step(dve.memset(ev[:, :, :], 0.0))
            step(dve.memset(half_pi[:, :], math.pi / 2))
            dve.memset(xt1[D1:K1, :], 1.0)
            dve.memset(xbt1[D1:K1, :], 1.0)
            step(dve.memset(bloch[:, :, 0, :], 1.0))
            join()
            step(dve.memset(ev[:, :, QUBITS:QUBITS + 1], 1.0))
            dve.wait_ge(angles_in, 16 * T)
            step(dve.tensor_scalar(turns[:, :, :], theta[:, :, :], 1 / (2 * math.pi), ROUNDER, ALU.mult, ALU.add))
            join()
            step(dve.tensor_scalar(turned[:, :, :], turns[:, :, :], ROUNDER, TWO_PI_HIGH, ALU.subtract, ALU.mult))
            step(dve.tensor_scalar(folded[:, :, :], turns[:, :, :], ROUNDER, TWO_PI_LOW, ALU.subtract, ALU.mult))
            join()
            step(dve.tensor_tensor(theta[:, :, :], theta[:, :, :], turned[:, :, :], ALU.subtract))
            join()
            step(dve.tensor_tensor(theta[:, :, :], theta[:, :, :], folded[:, :, :], ALU.subtract))
            join()
            step(dve.tensor_scalar(turned[:, :, :], theta[:, :, :], PI_BELOW, -PI_BELOW, ALU.min, ALU.max))
            join()
            assert steps[0] == REDUCED
            step(dve.scalar_tensor_tensor(folded[:, :, :], turned[:, :, :], -1.0, turned[:, :, :], ALU.mult, ALU.max))

            def sin_of(layer, gate):
                first = (layer * QUBITS * 2) + gate
                return sine[:, first:first + 2 * QUBITS - 1:2, :]

            def cos_of(layer, gate):
                first = (layer * QUBITS * 2) + gate
                return cosine[:, first:first + 2 * QUBITS - 1:2, :]

            dve.wait_ge(trig_done, 2)
            step(dve.tensor_copy(bloch[:, :, 1, :], cos_of(0, 0)))
            step(dve.tensor_tensor(bloch[:, :, 2, :], sin_of(0, 0), cos_of(0, 1), ALU.mult))
            step(dve.tensor_tensor(bloch[:, :, 3, :], sin_of(0, 0), sin_of(0, 1), ALU.mult))
            step(dve.tensor_copy(ry[:, :, 0, :], cos_of(1, 0)))
            step(dve.tensor_scalar(ry[:, :, 1, :], sin_of(1, 0), -1.0, None, ALU.mult))
            step(dve.tensor_tensor(rzy[:, :, 0, :], cos_of(1, 1), cos_of(1, 0), ALU.mult))
            step(dve.tensor_scalar(rzy[:, :, 1, :], sin_of(1, 1), -1.0, None, ALU.mult))
            step(dve.tensor_tensor(rzy[:, :, 2, :], cos_of(1, 1), sin_of(1, 0), ALU.mult))
            join()
            for h in range(2):
                step(dve.tensor_tensor(pair[:, h].rearrange("p (a b) t -> p a b t", a=4),
                                       bloch[:, 3 * h + 1].unsqueeze(2).to_broadcast([P, 4, 4, T]),
                                       bloch[:, 3 * h].unsqueeze(1).to_broadcast([P, 4, 4, T]), ALU.mult))
            join()
            for h, at in ((0, 0), (1, 128)):
                step(dve.tensor_tensor(tables[:, at:at + 64].rearrange("p (a b) t -> p a b t", a=4),
                                       bloch[:, 3 * h + 2].unsqueeze(2).to_broadcast([P, 4, 16, T]),
                                       pair[:, h].unsqueeze(1).to_broadcast([P, 4, 16, T]), ALU.mult))
            join()
            step(dve.tensor_scalar(tables[:, 64:128], tables[:, 0:64], -1.0, None, ALU.mult))
            join()
            assert steps[0] == TABLES_READY, steps

            def times_qubit(result, at, q, factors, first, n):
                step(dve.tensor_tensor(result[:, at:at + 2 * n].rearrange("p (a b) t -> p a b t", a=2),
                                       ry[:, q].unsqueeze(2).to_broadcast([P, 2, n, T]),
                                       factors[:, first:first + n].unsqueeze(1).to_broadcast([P, 2, n, T]), ALU.mult))

            times_qubit(z_coef, Z_BLOCK[1], 1, ry[:, 0], 0, 2)
            times_qubit(z_part, 0, 2, ry[:, 1], 0, 2)
            join()
            times_qubit(z_coef, Z_BLOCK[2], 2, z_coef, Z_BLOCK[1], 4)
            times_qubit(z_part, 4, 3, z_part, 0, 4)
            join()
            times_qubit(z_coef, Z_BLOCK[3], 3, z_coef, Z_BLOCK[2], 8)
            times_qubit(z_part, 12, 4, z_part, 4, 8)
            join()
            times_qubit(z_coef, Z_BLOCK[4], 4, z_coef, Z_BLOCK[3], 16)
            times_qubit(z_coef, Z_BLOCK[0], 5, z_part, 12, 16)
            join()
            times_qubit(z_coef, Z_BLOCK[5], 5, z_coef, Z_BLOCK[4], 32)
            for q in range(QUBITS):
                k = len(Z_SUPPORT[q])
                gather_products(dve, z_str[:, :, :], tables[:, :, :], T, [2] * k, "ZX", Z_SUPPORT[q], Z_BLOCK[q],
                                [2 ** i for i in range(k)], step)
            join()
            step(dve.tensor_tensor(z_str[:, :, :], z_str[:, :, :], z_coef[:, :, :], ALU.mult))
            join()
            for q in range(QUBITS):
                k = 2 ** len(Z_SUPPORT[q])
                step(dve.tensor_reduce(z_exp[:, q], z_str[:, Z_BLOCK[q]:Z_BLOCK[q] + k].rearrange("p k t -> p t k"),
                                       AX.X, ALU.add))
            join()
            step(dve.tensor_tensor(z_exp[:, :, :], z_exp[:, :, :], cos_of(2, 0), ALU.mult))
            dve.wait_ge(x_step, X_DONE)
            step(dve.tensor_tensor(x_exp[:, :, :], x_exp[:, :, :], sin_of(2, 0), ALU.mult))
            join()
            dve.tensor_tensor(ev[:, :, 0:QUBITS].rearrange("p t q -> p q t"), z_exp[:, :, :], x_exp[:, :, :],
                              ALU.subtract).then_inc(ev_done, 1)

            for i in range(4):
                dve.wait_ge(wt_done, i + 1)
                src, dst = [(b4, wqk_t0), (b5, wqk_t1), (b6, wqk_t0), (b7, wqk_t1)][i]
                rows = P if i % 2 == 0 else D1
                dve.tensor_copy(dst[0:rows, i // 2, :], src[0:rows, 0:D + 1]).then_inc(wt_copied, 1)
            dve.wait_ge(sw_done, 2)
            dve.tensor_scalar(score_w0[:, :], b0[:, 0:D + 1], SCALE, None, ALU.mult)
            dve.tensor_scalar(score_w1[:, :], b1[0:K1, 0:D + 1], SCALE, None, ALU.mult).then_inc(wt_copied, 1)

            base = steps[0]

            class Chain:
                def __init__(self, per):
                    self.per, self.start, self.n = per, 0, 0

                def begin(self, b):
                    self.start, self.n = b * self.per + base, 0

                def step(self, instruction):
                    self.n += 1
                    instruction.then_inc(dve_step, 1)

                def join(self):
                    dve.wait_ge(dve_step, self.start + self.n)

                def join_held(self):
                    self.join()
                    hold(dve)

                def end(self):
                    assert self.n == self.per, self.n

            chain = Chain(CHAIN)

            def emb_copy(b, half):
                dve.wait_ge(emb_done, 2 * b + half + 1)
                dve.tensor_copy(hres[:, bass.ds(b * TILES + 2 * half, 2), :],
                                b0[:, 0:2 * D].rearrange("p (j d) -> p j d", j=2)).then_inc(emb_copied, 1)

            def stats1(b):
                dve.wait_ge(emb_copied, 2 * b + 2)
                hold(dve)
                for j in range(TILES):
                    chain.step(dve.bn_stats(bn1[:, j, :], hres[:, bass.ds(b * TILES + j, 1), :].rearrange("p o d -> p (o d)")))
                chain.join_held()
                for j in range(TILES):
                    chain.step(dve.bn_aggr(mv1[:, j, :], bn1[:, j, :]))
                chain.join()
                dve.tensor_scalar(ve1[:, :], mv1[:, :, 1], EPS, None, ALU.add).then_inc(var1_done, 1)

            def norm1(b):
                dve.wait_ge(rs1_done, b + 1)
                if not (isinstance(b, int) and b == 0):
                    dve.wait_ge(xt_done, b)
                for j in range(TILES):
                    last = dve.tensor_scalar(x1[:, j, :], hres[:, bass.ds(b * TILES + j, 1), :].rearrange(
                        "p o d -> p (o d)"), mv1[:, j, 0:1], rs1[:, j:j + 1], ALU.subtract, ALU.mult)
                last.then_inc(x1_done, 1)

            def norm2(b, kept, s):
                i = b * TILES + s
                dve.wait_ge(rs2_done, i + 1)
                dve.tensor_scalar(x2[:, kept, s, 0:D], hres[:, bass.ds(i, 1), :].rearrange("p o d -> p (o d)"),
                                  mv2[:, s % 2, 0:1], rs2[:, s % 2:s % 2 + 1], ALU.subtract, ALU.mult
                                  ).then_inc(x2_done, 1)

            def val_copy(b, half):
                dve.wait_ge(val_done, 2 * b + half + 1)
                dve.tensor_copy(val[:, 2 * half:2 * half + 2, :],
                                b0[:, 0:2 * D].rearrange("p (j d) -> p j d", j=2)).then_inc(val_copied, 1)

            def row_max(b, s):
                i = b * TILES + s
                dve.wait_ge(score_done, i + 1)
                if not (isinstance(b, int) and b == 0 and s < 2):
                    dve.wait_ge(exp_done, i - 1)
                dve.tensor_reduce(nmax[:, s % 2:s % 2 + 1], (b4, b5)[s % 2][:, :], AX.X, ALU.max, negate=True
                                  ).then_inc(max_done, 1)

            def pt_copy(b, s):
                dve.wait_ge(pt_done, b * TILES + s + 1)
                dve.tensor_copy(prob_t[:, s % 2, :], b6[:, :]).then_inc(pt_copied, 1)

            def residual(b, s):
                i = b * TILES + s
                c = s % 2
                chain.step(dve.reciprocal(rinv[:, c:c + 1], rsum[:, c:c + 1]))
                dve.wait_ge(pv_done, i + 1)
                chain.join()
                row = hres[:, bass.ds(i, 1), :].rearrange("p o d -> p (o d)")
                dve.scalar_tensor_tensor(row, b7[:, 0:D], rinv[:, c:c + 1], row, ALU.mult, ALU.add).then_inc(h2_done, 1)
                dve.wait_ge(h2_done, i + 1)
                hold(dve)
                chain.step(dve.bn_stats(bn2[:, c, :], row))
                chain.join_held()
                chain.step(dve.bn_aggr(mv2[:, c, :], bn2[:, c, :]))
                chain.join()
                dve.tensor_scalar(ve2[:, c:c + 1], mv2[:, c, 1:2], EPS, None, ALU.add).then_inc(var2_done, 1)

            def logit_copy(b):
                dve.wait_ge(logit_done, b * TILES + TILES)
                dve.tensor_copy(logit[:, :, :].rearrange("p j e -> p (j e)"),
                                b1[:, 256:256 + TILES * E]).then_inc(logit_copied, 1)

            def route_a(b, par):
                dve.wait_ge(logit_copied, b + 1)
                hold(dve)
                for j in range(TILES):
                    chain.step(dve.max(top[:, j, :], logit[:, j, :]))
                chain.join_held()
                for j in range(TILES):
                    chain.step(dve.max_index(top_i[:, j, :], top[:, j, :], logit[:, j, :]))
                dve.tensor_tensor(gap[:, :], top[:, :, 1], top[:, :, 0], ALU.subtract).then_inc(gap_done, 1)
                chain.join()
                chain.step(dve.tensor_copy(x2[:, par, :, D:D + 2], top_i[:, :, 0:2]))
                chain.step(dve.tensor_copy(x2[:, par, :, D + 4], tok[:, bass.ds(b * TILES, TILES)]))
                chain.join()
                chain.step(dve.tensor_tensor(
                    mask[:, :, :, :], x2[:, par, :, D:D + 2].rearrange("p j k -> p k j").unsqueeze(3).to_broadcast([P, 2, TILES, E]),
                    exp_f[:, :].unsqueeze(1).unsqueeze(1).to_broadcast([P, 2, TILES, E]), ALU.is_equal))
                chain.join()
                chain.step(dve.tensor_tensor(both[:, :, :], mask[:, 0], mask[:, 1], ALU.add))
                chain.join()
                chain.step(dve.tensor_copy(ahead[:, 1, :], both[:, 0, :]))
                chain.step(dve.tensor_tensor(ahead[:, 2, :], both[:, 0, :], both[:, 1, :], ALU.add))
                chain.join()
                chain.step(dve.tensor_tensor(ahead[:, 3, :], ahead[:, 2, :], both[:, 2, :], ALU.add))
                chain.join()
                chain.step(dve.tensor_tensor(here[:, :], ahead[:, 3, :], both[:, 3, :], ALU.add))
                chain.join()
                dve.tensor_copy(here_b[:, :], here[:, :]).then_inc(mask_done, 1)

            def rank_copy(b):
                dve.wait_ge(rank_done, b + 1)
                dve.tensor_tensor(rank[:, :], b1[:, 288:288 + E], region_f[:, :], ALU.add).then_inc(rank_copied, 1)

            def route_b(b, par):
                dve.wait_ge(gap_exp, b + 1)
                chain.step(dve.tensor_scalar(gap_1[:, :], gap_e[:, :], 1.0, None, ALU.add))
                chain.join()
                chain.step(dve.reciprocal(x2[:, par, :, D + 2], gap_1[:, :]))
                chain.join()
                chain.step(dve.tensor_tensor(x2[:, par, :, D + 3], x2[:, par, :, D + 2], gap_e[:, :], ALU.mult))
                chain.step(dve.tensor_tensor(so_far[:, :], so_far[:, :], here[:, :], ALU.add))
                dve.wait_ge(rank_copied, b + 1)
                chain.step(dve.tensor_tensor(place[:, :, :], ahead[:, :, :],
                                             rank[:, :].unsqueeze(1).to_broadcast([P, TILES, E]), ALU.add))
                chain.join()
                chain.step(dve.tensor_tensor(slot_e[:, :, :, :], mask[:, :, :, :],
                                             place[:, :, :].unsqueeze(1).to_broadcast([P, 2, TILES, E]), ALU.mult))
                chain.join()
                chain.step(dve.tensor_reduce(slot_f[:, :, :], slot_e[:, :, :, :], AX.X, ALU.add))
                chain.join()
                dve.tensor_copy(slot[:, par, :, :], slot_f[:, :, :]).then_inc(slot_done, 1)

            dve.memset(ahead[:, 0, :], 0.0).then_inc(const_done, 1)
            dve.wait_ge(const_done, 3)
            chain.begin(0)
            emb_copy(0, 0)
            emb_copy(0, 1)
            stats1(0)
            norm1(0)
            base = base + chain.n
            val_copy(0, 0)
            row_max(0, 0)
            val_copy(0, 1)

            def batch(b, kept, first=False, last=False):
                before_kept = (kept - 1) % ROWS_KEPT
                chain.begin(b)
                if not first:
                    dve.wait_ge(rows_free, b)
                for s in range(TILES):
                    if s < TILES - 1:
                        row_max(b, s + 1)
                    if s > 0:
                        norm2(b, kept, s - 1)
                    elif not first:
                        norm2(b - 1, before_kept, TILES - 1)
                    if s == 1 and not last:
                        emb_copy(b + 1, 1)
                    pt_copy(b, s)
                    if s == 1 and not first:
                        logit_copy(b - 1)
                    if s == 0 and not last:
                        emb_copy(b + 1, 0)
                    if s == 1 and not last:
                        stats1(b + 1)
                    if s == 2 and not first:
                        rank_copy(b - 1)
                    if s == 2 and not last:
                        norm1(b + 1)
                    residual(b, s)
                    if s == 1 and not first:
                        route_a(b - 1, before_kept)
                    if s == 3 and not first:
                        route_b(b - 1, before_kept)
                if not last:
                    val_copy(b + 1, 0)
                    row_max(b + 1, 0)
                    val_copy(b + 1, 1)

            batch(0, 0, first=True)
            base = base + chain.n - CHAIN
            with dve.Fori(0, (BATCHES - 2) // ROWS_KEPT) as i:
                for k in range(ROWS_KEPT):
                    batch(ROWS_KEPT * i + k + 1, (k + 1) % ROWS_KEPT)
                    chain.end()
            batch(BATCHES - 1, (BATCHES - 1) % ROWS_KEPT, last=True)
            norm2(BATCHES - 1, (BATCHES - 1) % ROWS_KEPT, TILES - 1)
            logit_copy(BATCHES - 1)
            route_a(BATCHES - 1, (BATCHES - 1) % ROWS_KEPT)
            rank_copy(BATCHES - 1)
            route_b(BATCHES - 1, (BATCHES - 1) % ROWS_KEPT)

            dve.wait_ge(count_done, 1)
            dve.tensor_copy(count[:, :], b1[:, 304:304 + E]).then_inc(count_copied, 1)
            dve.tensor_copy(count_i[:, :], b1[:, 304:304 + E]).then_inc(count_copied, 1)
            dve.wait_ge(count_copied, 2)
            chain.step(dve.tensor_scalar(count[:, :], count[:, :], float(P - 1), None, ALU.add))
            chain.join()
            chain.step(dve.tensor_copy(nblk_i[:, :], count[:, :]))
            chain.join()
            chain.step(dve.tensor_scalar(nblk_i[:, :], nblk_i[:, :], 7, None, ALU.arith_shift_right))
            chain.join()
            chain.step(dve.tensor_copy(nblk[:, :], nblk_i[:, :]))
            chain.join()
            chain.step(dve.tensor_copy(cum[:, 0, :], nblk[:, :]))
            chain.step(dve.tensor_scalar(skip[:, :], nblk[:, :], -float(P), float(REGION), ALU.mult, ALU.add))
            chain.join()
            c = 0
            for shift in (1, 2, 4):
                chain.step(dve.tensor_copy(cum[:, 1 - c, 0:shift], cum[:, c, 0:shift]))
                chain.step(dve.tensor_tensor(cum[:, 1 - c, shift:E], cum[:, c, shift:E], cum[:, c, 0:E - shift], ALU.add))
                chain.join()
                c = 1 - c
            chain.step(dve.tensor_tensor(ge[:, :, :], blk[:, :].unsqueeze(1).to_broadcast([P, E, BLOCKS]),
                                         cum[:, c, :].unsqueeze(2).to_broadcast([P, E, BLOCKS]), ALU.is_ge))
            chain.join()
            past = ge[:, 0:E - 1, :]
            chain.step(dve.tensor_reduce(t_exp[:, :], past.rearrange("p e m -> p m e"), AX.X, ALU.add))
            for values, result in ((skip, t_row), (nblk, t_first)):
                chain.step(dve.tensor_tensor(ge_w[:, :, :], past, values[:, 0:E - 1].unsqueeze(2).to_broadcast(
                    [P, E - 1, BLOCKS]), ALU.mult))
                chain.join()
                chain.step(dve.tensor_reduce(result[:, :], ge_w[:, :, :].rearrange("p e m -> p m e"), AX.X, ALU.add))
                chain.join()
            chain.step(dve.scalar_tensor_tensor(t_row[:, :], blk[:, :], float(P), t_row[:, :], ALU.mult, ALU.add))
            chain.join()
            chain.step(dve.tensor_scalar(t_row[:, :], t_row[:, :], -float(PAD_ROW), None, ALU.add))
            chain.join()
            chain.step(dve.tensor_tensor(ge_w[:, 0, :], t_row[:, :], ge[:, E - 1, :], ALU.mult))
            chain.join()
            chain.step(dve.tensor_tensor(t_row[:, :], t_row[:, :], ge_w[:, 0, :], ALU.subtract))
            chain.join()
            chain.step(dve.tensor_scalar(t_row[:, :], t_row[:, :], float(PAD_ROW), None, ALU.add))
            chain.join()
            dve.tensor_copy(t_i[:, 0, :], t_exp[:, :])
            dve.tensor_copy(t_i[:, 2, :], t_first[:, :])
            dve.tensor_copy(t_i[:, 1, :], t_row[:, :]).then_inc(table_done, 1)

            def share_of(m, n, round_of):
                dve.wait_ge(block_in[n], round_of * 16)
                dve.scalar_tensor_tensor(share_w[:, n, :], xb[:, n, D:D + 2], t_exp[:, bass.ds(m, 1)],
                                         xb[:, n, D + 2:D + 4], ALU.is_equal, ALU.mult,
                                         accum_out=share[:, n:n + 1]).then_inc(share_done, 1)
                dve.tensor_copy(dest[:, n:n + 1], xb[:, n, D + 4:D + 5]).then_inc(share_done, 1)

            def ht_copy(m):
                dve.wait_ge(ht_done, m + 1)
                dve.tensor_copy(hid_t[:, :], b3[:, 0:HID]).then_inc(ht_copied, 1)

            def finish(m, n, e):
                dve.wait_ge(y_mm, m + 1)
                dve.tensor_tensor(y_raw[:, n % 2, :], (b5, b6)[n % 2][:, 0:D],
                                  down_bias[:, bass.ds(e * D, D)], ALU.add).then_inc(y_read, 1)
                dve.wait_ge(y_read, m + 1)
                dve.wait_ge(share_done, m * 2 + 2)
                dve.tensor_scalar(y[:, n, :], y_raw[:, n % 2, :], share[:, n:n + 1], None, ALU.mult
                                  ).then_inc(y_done, 1)

            dve.wait_ge(down_in, 32)
            dve.wait_ge(table_done, 1)
            dve.wait_ge(added[0], 16)
            share_of(0, 0, 1)

            def expert_block(m, n, it, more, first):
                e = dve.value_load(t_i[0:1, 0, bass.ds(m, 1)], min_val=0, max_val=E - 1)
                ht_copy(m)
                if more:
                    dve.wait_ge(added[(n + 1) % UNROLL], (it + (n + 1) // UNROLL) * 16 + 16)
                    share_of(m + 1, (n + 1) % UNROLL, it + 1 + (n + 1) // UNROLL)
                finish(m, n, e)

            rounds = BLOCKS // UNROLL
            for n in range(UNROLL):
                expert_block(n, n, 0, True, True)
            with dve.Fori(1, rounds - 1) as it:
                for n in range(UNROLL):
                    expert_block(it * UNROLL + n, n, it, True, False)
            for n in range(UNROLL):
                expert_block((rounds - 1) * UNROLL + n, n, rounds - 1, n < UNROLL - 1, False)

        @block.scalar
        def _(act):
            act.wait_ge(dve_step, REDUCED)
            act.activation(sine[:, :, :], turned[:, :, :].rearrange("p t f -> p f t"), ACT.Sin).then_inc(trig_done, 1)
            act.wait_ge(dve_step, REDUCED + 1)
            act.activation(cosine[:, :, :], folded[:, :, :].rearrange("p t f -> p f t"), ACT.Sin,
                           bias=half_pi[:, 0:1], scale=-1.0).then_inc(trig_done, 1)

            def evt_copy(b):
                act.wait_ge(evt_done, b + 1)
                act.copy(ev_t[:, :], b2[:, 0:P]).then_inc(evt_copied, 1)

            def xt_copy(b):
                act.wait_ge(xt_done, b + 1)
                act.copy(xt0[:, :], b2[:, :])
                act.copy(xt1[0:D1, :], b3[0:D1, :]).then_inc(xt_copied, 1)

            def tq_copy(b):
                act.wait_ge(tq_done, b + 1)
                act.copy(tq0[:, :], b2[:, :])
                act.copy(tq1[:, :], b3[0:K1, :]).then_inc(tq_copied, 1)

            def softmax(b, s):
                i = b * TILES + s
                act.wait_ge(max_done, i + 1)
                if not (isinstance(b, int) and b == 0 and s < 2):
                    act.wait_ge(h2_done, i - 1)
                act.activation(prob[:, s % 2, :], (b4, b5)[s % 2][:, :], ACT.Exp, bias=nmax[:, s % 2:s % 2 + 1],
                               accum_out=rsum[:, s % 2:s % 2 + 1]).then_inc(exp_done, 1)

            def x2t_copy(b, s):
                act.wait_ge(x2t_done, b * TILES + s + 1)
                act.copy(x2t0[:, :], b1[:, 0:P])
                act.copy(x2t1[:, :], b1[0:D1, P:2 * P]).then_inc(x2t_copied, 1)

            def gap_exponent(b):
                act.wait_ge(gap_done, b + 1)
                act.activation(gap_e[:, :], gap[:, :], ACT.Exp).then_inc(gap_exp, 1)

            evt_copy(0)
            xt_copy(0)
            tq_copy(0)

            def batch(b, first=False, last=False):
                softmax(b, 0)
                if not last:
                    evt_copy(b + 1)
                if not first:
                    x2t_copy(b - 1, TILES - 1)
                softmax(b, 1)
                x2t_copy(b, 0)
                softmax(b, 2)
                if not first:
                    gap_exponent(b - 1)
                x2t_copy(b, 1)
                if not last:
                    xt_copy(b + 1)
                softmax(b, 3)
                if not last:
                    tq_copy(b + 1)
                x2t_copy(b, 2)

            batch(0, first=True)
            with act.Fori(0, (BATCHES - 2) // ROWS_KEPT) as i:
                for k in range(ROWS_KEPT):
                    batch(ROWS_KEPT * i + k + 1)
            batch(BATCHES - 1, last=True)
            x2t_copy(BATCHES - 1, TILES - 1)
            gap_exponent(BATCHES - 1)

            def xbt_copy(m):
                act.wait_ge(xbt_done, m + 1)
                act.copy(xbt0[:, :], b0[:, 0:P])
                act.copy(xbt1[0:D1, :], b0[0:D1, P:2 * P]).then_inc(xbt_copied, 1)

            def gelu(m, n):
                act.wait_ge(up_done, m + 1)
                act.activation(hid[:, n % 2, :], (b1, b2)[n % 2][:, 0:HID], ACT.Gelu).then_inc(gelu_done, 1)

            xbt_copy(0)
            with act.Fori(0, BLOCKS // UNROLL - 1) as it:
                for n in range(UNROLL):
                    gelu(it * UNROLL + n, n)
                    xbt_copy(it * UNROLL + n + 1)
            for n in range(UNROLL):
                gelu(BLOCKS - UNROLL + n, n)
                if n < UNROLL - 1:
                    xbt_copy(BLOCKS - UNROLL + n + 1)

        @block.tensor
        def _(pe):
            pe.wait_ge(const_done, 2)
            pe.wait_ge(small_in, 16 * 5)
            for i in range(2):
                cols = slice(i * D, i * D + P), slice(i * D + P, (i + 1) * D)
                for c, dst in enumerate(((b4, b5), (b6, b7))[i]):
                    rows = (P, D1)[c]
                    pe.transpose(dst[0:rows, 0:P], wqkv0[:, cols[c]], ident[:, :])
                    pe.transpose(dst[0:rows, P:D + 1], wqkv1[:, cols[c]], ident[0:K1, 0:K1]).then_inc(wt_done, 1)
            pe.wait_ge(wt_copied, 4)
            for dst, cols in ((b0, slice(0, P)), (b1, slice(P, D + 1))):
                m = cols.stop - cols.start
                pe.matmul(dst[0:m, 0:D + 1], wqk_t0[:, 0, cols], wqk_t0[:, 1, :], start=True, stop=False)
                pe.matmul(dst[0:m, 0:D + 1], wqk_t1[:, 0, cols], wqk_t1[:, 1, :], start=False, stop=True
                          ).then_inc(sw_done, 1)
            pe.wait_ge(wt_copied, 5)

            def ev_transpose(b):
                pe.wait_ge(ev_copied, b + 1)
                if not (isinstance(b, int) and b == 0):
                    pe.wait_ge(tq_copied, b)
                pe.transpose(b2[:, 0:P], ev_b[:, :], ident[:, :]).then_inc(evt_done, 1)

            def embed(b, half):
                if half == 0:
                    pe.wait_ge(evt_copied, b + 1)
                    if not (isinstance(b, int) and b == 0):
                        pe.wait_ge(val_copied, 2 * b)
                else:
                    pe.wait_ge(emb_copied, 2 * b + 1)
                for j in range(2):
                    mm = pe.matmul(b0[:, j * D:(j + 1) * D], ev_t[:, :], wz[:, 2 * half + j, :], start=True, stop=True)
                mm.then_inc(emb_done, 1)

            def x_transposes(b):
                pe.wait_ge(x1_done, b + 1)
                for j in range(TILES):
                    pe.transpose(b2[:, j * P:(j + 1) * P], x1[:, j, 0:P], ident[:, :])
                    mm = pe.transpose(b3[0:D1, j * P:(j + 1) * P], x1[:, j, P:D], ident[:, :])
                mm.then_inc(xt_done, 1)

            def score_factor(b):
                pe.wait_ge(xt_copied, b + 1)
                for dst, cols in ((b2, slice(0, P)), (b3, slice(P, D + 1))):
                    m = cols.stop - cols.start
                    pe.matmul(dst[0:m, :], score_w0[:, cols], xt0[:, :], start=True, stop=False)
                    mm = pe.matmul(dst[0:m, :], score_w1[:, cols], xt1[:, :], start=False, stop=True)
                mm.then_inc(tq_done, 1)

            def values(b, half):
                if half == 0:
                    pe.wait_ge(emb_copied, 2 * b + 2)
                else:
                    pe.wait_ge(val_copied, 2 * b + 1)
                for j in range(2):
                    t = slice((2 * half + j) * P, (2 * half + j + 1) * P)
                    pe.matmul(b0[:, j * D:(j + 1) * D], xt0[:, t], wqkv0[:, 2 * D:3 * D], start=True, stop=False)
                    mm = pe.matmul(b0[:, j * D:(j + 1) * D], xt1[:, t], wqkv1[:, 2 * D:3 * D], start=False, stop=True)
                mm.then_inc(val_done, 1)

            def scores(b, s):
                i = b * TILES + s
                if s == 0:
                    pe.wait_ge(tq_copied, b + 1)
                if not (isinstance(b, int) and b == 0 and s < 2):
                    pe.wait_ge(exp_done, i - 1)
                t = slice(s * P, (s + 1) * P)
                dst = (b4, b5)[s % 2]
                pe.matmul(dst[:, :], tq0[:, t], xt0[:, :], start=True, stop=False)
                pe.matmul(dst[:, :], tq1[:, t], xt1[:, :], start=False, stop=True).then_inc(score_done, 1)

            def p_transposes(b, s):
                i = b * TILES + s
                pe.wait_ge(exp_done, i + 1)
                if not (isinstance(b, int) and b == 0 and s == 0):
                    pe.wait_ge(pt_copied, i)
                for k in range(TILES):
                    mm = pe.transpose(b6[:, k * P:(k + 1) * P], prob[:, s % 2, k * P:(k + 1) * P], ident[:, :])
                mm.then_inc(pt_done, 1)

            def context(b, s):
                i = b * TILES + s
                if s == 0:
                    pe.wait_ge(val_copied, 2 * b + 2)
                pe.wait_ge(pt_copied, i + 1)
                if not (isinstance(b, int) and b == 0 and s == 0):
                    pe.wait_ge(h2_done, i)
                for k in range(TILES):
                    mm = pe.matmul(b7[:, 0:D], prob_t[:, s % 2, k * P:(k + 1) * P], val[:, k, :],
                                   start=(k == 0), stop=(k == TILES - 1))
                mm.then_inc(pv_done, 1)

            def x2_transposes(b, kept, s):
                pe.wait_ge(x2_done, b * TILES + s + 1)
                if s == 0 and not (isinstance(b, int) and b == 0):
                    pe.wait_ge(logit_copied, b)
                if s == 1 and not (isinstance(b, int) and b == 0):
                    pe.wait_ge(rank_copied, b)
                pe.transpose(b1[:, 0:P], x2[:, kept, s, 0:P], ident[:, :])
                pe.transpose(b1[0:D1, P:2 * P], x2[:, kept, s, P:D], ident[:, :]).then_inc(x2t_done, 1)

            def gate(b, s):
                pe.wait_ge(x2t_copied, b * TILES + s + 1)
                dst = b1[:, 256 + s * E:256 + (s + 1) * E]
                pe.matmul(dst, x2t0[:, :], wg0[:, :], start=True, stop=False)
                pe.matmul(dst, x2t1[:, :], wg1[:, :], start=False, stop=True).then_inc(logit_done, 1)

            def ranks(b):
                pe.wait_ge(mask_done, b + 1)
                pe.matmul(b1[:, 288:288 + E], before[:, :], here_b[:, :], start=True, stop=False)
                pe.matmul(b1[:, 288:288 + E], ones_b[:, :], so_far[:, :], start=False, stop=True).then_inc(rank_done, 1)

            ev_transpose(0)
            embed(0, 0)
            embed(0, 1)
            x_transposes(0)
            score_factor(0)
            values(0, 0)
            scores(0, 0)
            values(0, 1)

            def batch(b, kept, first=False, last=False):
                scores(b, 1)
                if not last:
                    ev_transpose(b + 1)
                p_transposes(b, 0)
                if not first:
                    x2_transposes(b - 1, (kept - 1) % ROWS_KEPT, TILES - 1)
                if not last:
                    embed(b + 1, 0)
                context(b, 0)
                if not first:
                    gate(b - 1, TILES - 1)
                scores(b, 2)
                if not last:
                    embed(b + 1, 1)
                p_transposes(b, 1)
                x2_transposes(b, kept, 0)
                context(b, 1)
                gate(b, 0)
                scores(b, 3)
                if not first:
                    ranks(b - 1)
                p_transposes(b, 2)
                x2_transposes(b, kept, 1)
                if not last:
                    x_transposes(b + 1)
                context(b, 2)
                gate(b, 1)
                p_transposes(b, 3)
                if not last:
                    score_factor(b + 1)
                x2_transposes(b, kept, 2)
                context(b, 3)
                if not last:
                    values(b + 1, 0)
                gate(b, 2)
                if not last:
                    scores(b + 1, 0)
                    values(b + 1, 1)

            batch(0, 0, first=True)
            with pe.Fori(0, (BATCHES - 2) // ROWS_KEPT) as i:
                for k in range(ROWS_KEPT):
                    batch(ROWS_KEPT * i + k + 1, (k + 1) % ROWS_KEPT)
            batch(BATCHES - 1, (BATCHES - 1) % ROWS_KEPT, last=True)
            x2_transposes(BATCHES - 1, (BATCHES - 1) % ROWS_KEPT, TILES - 1)
            gate(BATCHES - 1, TILES - 1)
            ranks(BATCHES - 1)
            pe.wait_ge(slot_done, BATCHES)
            pe.matmul(b1[:, 304:304 + E], ones_b[:, :], so_far[:, :], start=True, stop=True).then_inc(count_done, 1)

            def block_transposes(m, n, round_of):
                pe.wait_ge(block_in[n], round_of * 16)
                pe.transpose(b0[:, 0:P], xb[:, n, 0:P], ident[:, :])
                pe.transpose(b0[0:D1, P:2 * P], xb[:, n, P:D], ident[:, :]).then_inc(xbt_done, 1)

            def up_proj(m, n):
                e = pe.value_load(t_i[0:1, 0, bass.ds(m, 1)], min_val=0, max_val=E - 1)
                pe.wait_ge(xbt_copied, m + 1)
                dst = (b1, b2)[n % 2][:, 0:HID]
                pe.matmul(dst, xbt0[:, :], up0[:, bass.ds(e * HID, HID)], start=True, stop=False)
                pe.matmul(dst, xbt1[:, :], up1[:, bass.ds(e * HID, HID)], start=False, stop=True).then_inc(up_done, 1)

            def hid_transposes(m, n):
                pe.wait_ge(gelu_done, m + 1)
                for c in range(HC):
                    mm = pe.transpose(b3[:, c * P:(c + 1) * P], hid[:, n % 2, c * P:(c + 1) * P], ident[:, :])
                mm.then_inc(ht_done, 1)

            def down_proj(m, n, first):
                e = pe.value_load(t_i[0:1, 0, bass.ds(m, 1)], min_val=0, max_val=E - 1)
                pe.wait_ge(ht_copied, m + 1)
                if not (first and n < 2):
                    pe.wait_ge(y_read, m - 1)
                for c in range(HC):
                    mm = pe.matmul((b5, b6)[n % 2][:, 0:D], hid_t[:, c * P:(c + 1) * P],
                                   down[:, bass.ds(e * (HC * D) + c * D, D)], start=(c == 0), stop=(c == HC - 1))
                mm.then_inc(y_mm, 1)

            pe.wait_ge(up_in, 32)
            pe.wait_ge(down_in, 32)
            pe.wait_ge(table_done, 1)
            block_transposes(0, 0, 1)
            up_proj(0, 0)
            block_transposes(1, 1, 1)

            def expert_block(m, n, it, ahead1, ahead2, first):
                hid_transposes(m, n)
                if ahead1:
                    up_proj(m + 1, n + 1)
                if ahead2:
                    block_transposes(m + 2, (n + 2) % UNROLL, it + 1 + (n + 2) // UNROLL)
                down_proj(m, n, first)

            rounds = BLOCKS // UNROLL
            for n in range(UNROLL):
                expert_block(n, n, 0, True, True, True)
            with pe.Fori(1, rounds - 1) as it:
                for n in range(UNROLL):
                    expert_block(it * UNROLL + n, n, it, True, True, False)
            for n in range(UNROLL):
                expert_block((rounds - 1) * UNROLL + n, n, rounds - 1, n < UNROLL - 1, n < UNROLL - 2, False)


def kernel(x, L0_tok_quantum_params, L0_tok_post_w, L0_tok_post_b, L0_attn_W_qkv, L0_attn_b_qkv, L0_ffn_Wg,
           L0_ffn_W1, L0_ffn_b1, L0_ffn_W2, L0_ffn_b2):
    import concourse.bacc as bacc
    from concourse.bass_utils import run_bass_kernel_spmd

    x = np.ascontiguousarray(x)
    vocab = L0_tok_quantum_params.shape[0]
    embed = L0_tok_post_w.shape[0]
    experts, _, hidden = L0_ffn_W1.shape
    tiles = x.shape[1] // 128
    emb_w = np.zeros((tiles, 128 // tiles, tiles, embed), np.float32)
    for j in range(tiles):
        emb_w[j, 0:QUBITS, j] = np.asarray(L0_tok_post_w).T
        emb_w[j, QUBITS, j] = L0_tok_post_b
    arrays = {
        "token_ids": x,
        "angles": np.ascontiguousarray(L0_tok_quantum_params).reshape(vocab, ANGLES),
        "emb_w": emb_w.reshape(128, tiles * embed),
        "qkv_w": np.concatenate([L0_attn_W_qkv, np.asarray(L0_attn_b_qkv)[None]], 0),
        "gate_w": np.ascontiguousarray(L0_ffn_Wg),
        "up_w": np.concatenate([L0_ffn_W1, np.asarray(L0_ffn_b1)[:, None]], 1).transpose(1, 0, 2).reshape(
            embed + 1, experts * hidden),
        "down_w": np.asarray(L0_ffn_W2).reshape(experts, hidden // 128, 128, embed).transpose(2, 0, 1, 3).reshape(
            128, experts * hidden // 128 * embed),
        "down_b": np.ascontiguousarray(L0_ffn_b2).reshape(experts * embed),
    }
    nc = bacc.Bacc("TRN2", target_bir_lowering=False, num_devices=1)
    aps = []
    for name in arrays:
        arrays[name] = np.ascontiguousarray(arrays[name])
        aps.append(nc.dram_tensor(name, arrays[name].shape, mybir.dt.from_np(arrays[name].dtype),
                                  kind="ExternalInput").ap())
    out = nc.dram_tensor("out", (x.shape[0], x.shape[1], embed), F32, kind="ExternalOutput").ap()
    build(nc, *aps, out)
    result = run_bass_kernel_spmd(nc, [arrays], core_ids=[0])
    return result.results[0]["out"]
```

```python
import itertools
import math
from contextlib import ExitStack

import numpy as np
import concourse.bass as bass
from concourse import mybir

ALU = mybir.AluOpType
ACT = mybir.ActivationFunctionType
AX = mybir.AxisListType
F32 = mybir.dt.float32
I32 = mybir.dt.int32
U32 = mybir.dt.uint32
BF16 = mybir.dt.bfloat16

QUBITS = 6
LAYERS = 3
ANGLES = LAYERS * QUBITS * 2
EPS = 1e-5
ROUNDER = 1.5 * 2.0 ** 23
TWO_PI_HIGH = 6.28125
TWO_PI_LOW = 2 * math.pi - TWO_PI_HIGH
PI_BELOW = 3.1415925
REDUCED = 10
TABLES_READY = 24
X_DONE = 52
CHAIN = 43


Z_SUPPORT = [list(range(1, QUBITS))] + [list(range(q + 1)) for q in range(1, QUBITS)]
X_SUPPORT = [[q, q + 1] for q in range(QUBITS - 1)] + [[QUBITS - 1, 0, 1]]
PAULI_CODE = {"I": 0, "Z": 1, "X": 2, "Y": 3}


def pauli_string(choice):
    x_all, z_all, phase = 0, 0, 0
    for j, name in choice:
        x = sum(1 << k for k in X_SUPPORT[j]) if name in "XY" else 0
        z = sum(1 << k for k in Z_SUPPORT[j]) if name in "ZY" else 0
        phase += (name == "Y") + 2 * bin(z_all & x).count("1")
        x_all, z_all = x_all ^ x, z_all ^ z
    names = ""
    for k in range(QUBITS):
        xk, zk = x_all >> k & 1, z_all >> k & 1
        names += "IXZY"[xk + 2 * zk]
        phase -= xk and zk
    assert phase % 2 == 0
    return names, 1 - phase % 4


def table_place(choice):
    names, sign = pauli_string(choice)
    low = sum(PAULI_CODE[names[k]] * 4 ** k for k in range(3))
    high = sum(PAULI_CODE[names[3 + k]] * 4 ** k for k in range(3))
    return low + (0 if sign > 0 else 64), high


def boxes(shape, place, most=3):
    left = set(itertools.product(*[range(s) for s in shape]))
    kinds = []
    for k in range(most, -1, -1):
        for dims in itertools.combinations(range(len(shape)), k):
            runs = [[(s, n, t) for t in (1, 2) for s in range(shape[d]) for n in range(shape[d], 1, -1)
                     if s + (n - 1) * t < shape[d]] for d in dims]
            for run in itertools.product(*runs):
                kinds.append((int(np.prod([n for _, n, _ in run])), dims, run))
    kinds.sort(key=lambda kind: -kind[0])
    found = []
    for size, dims, run in kinds:
        for base in sorted(left):
            if base not in left or any(base[d] != r[0] for d, r in zip(dims, run)):
                continue
            points = {}
            for step in itertools.product(*[range(r[1]) for r in run]):
                p = list(base)
                for d, r, o in zip(dims, run, step):
                    p[d] += r[2] * o
                points[step] = tuple(p)
            if not all(p in left for p in points.values()):
                continue
            origin = place(base)
            units = [tuple(int(j == i) for j in range(len(dims))) for i in range(len(dims))]
            slope = [tuple(a - b for a, b in zip(place(points[u]), origin)) for u in units]
            if all(place(p) == tuple(origin[h] + sum(o * s[h] for o, s in zip(step, slope)) for h in (0, 1))
                   for step, p in points.items()):
                found.append((base, [(d, r[1], r[2]) for d, r in zip(dims, run)], origin, slope))
                left -= set(points.values())
    assert not left
    return found


Z_BLOCK, at = {}, 0
for _q in list(range(1, QUBITS)) + [0]:
    Z_BLOCK[_q] = at
    at += 2 ** len(Z_SUPPORT[_q])
Z_STRINGS = at
PAIRS = QUBITS - 1
X_STRINGS = 9 * PAIRS + 27


def gather_products(eng, out, tables, n, shape, names, support, base, strides, log):
    def place(index):
        return table_place([(j, names[i]) for j, i in zip(support, index)])

    for first, dims, (low, high), slope in boxes(shape, place):
        at = base + sum(i * s for i, s in zip(first, strides))
        part_out, part_tab = out.ap[0][0], tables.ap[0][0]
        run = [(strides[d] * step, count) for d, count, step in dims]
        o = bass.AP(out.tensor, out.offset + at * n, [[part_out, 128]] + [[s * n, c] for s, c in run] + [[1, n]])
        a = bass.AP(tables.tensor, tables.offset + low * n,
                    [[part_tab, 128]] + [[s[0] * n, c] for s, (_, c) in zip(slope, run)] + [[1, n]])
        b = bass.AP(tables.tensor, tables.offset + (128 + high) * n,
                    [[part_tab, 128]] + [[s[1] * n, c] for s, (_, c) in zip(slope, run)] + [[1, n]])
        log(eng.tensor_tensor(o, a, b, ALU.mult))


def build(nc, token_ids, angles, emb_w, qkv_w, gate_w, up_w, down_w, down_b, out):
    P = 128
    TOKENS = token_ids.shape[0] * token_ids.shape[1]
    BATCHES, SEQ = token_ids.shape
    D = qkv_w.shape[1] // 3
    D0, D1 = P, D - P
    K1 = D1 + 1
    TILES = SEQ // P
    T = TOKENS // P
    E = gate_w.shape[1]
    HID = up_w.shape[1] // E
    HC = HID // P
    SCALE = 1.0 / math.sqrt(D)
    REGION = TOKENS + P
    PAD_ROW = E * REGION
    WIDTH = D + 5
    NO_TOKEN = 1.0e6
    UNROLL = 4
    ROWS_KEPT = 3
    BLOCKS = -(-(2 * TOKENS // P + E - 1) // UNROLL) * UNROLL
    EV_STRIDE = P // TILES

    routed = nc.dram_tensor("routed", (PAD_ROW + P, WIDTH), F32, kind="Internal").ap()
    ids_view = token_ids.rearrange("b (p j) -> p b j", j=TILES)
    out_rows = out.rearrange("b s d -> (b s) d")
    out_view = out.rearrange("b (p j) d -> b p (j d)", j=TILES)

    ctx = ExitStack()
    with ctx:
        def sb(name, shape, dt=F32):
            return ctx.enter_context(nc.sbuf_tensor(name, shape, dt))

        def bank(name):
            return ctx.enter_context(nc.psum_tensor(name, [P, 512], F32))

        def sem(name):
            return ctx.enter_context(nc.semaphore(name))

        ids = sb("ids", [P, BATCHES, TILES], I32)
        angle_stages = sb("angle_stages", [P, 4, T, ANGLES])
        theta, turns, turned, folded = [angle_stages[:, i] for i in range(4)]
        sine = sb("sine", [P, ANGLES, T])
        cosine = sb("cosine", [P, ANGLES, T])
        half_pi = sb("half_pi", [P, 1])
        bloch = sb("bloch", [P, QUBITS, 4, T])
        pair = sb("pair", [P, 2, 16, T])
        tables = sb("tables", [P, 192, T])
        ry = sb("ry", [P, QUBITS, 2, T])
        rzy = sb("rzy", [P, QUBITS, 3, T])
        z_both = sb("z_both", [P, 2, Z_STRINGS, T])
        z_coef = z_both[:, 0]
        z_str = z_both[:, 1]
        z_part = sb("z_part", [P, 28, T])
        x_str = sb("x_str", [P, X_STRINGS, T])
        x_sum = sb("x_sum", [P, X_STRINGS // 3, T])
        x_sum2 = sb("x_sum2", [P, X_STRINGS // 9, T])
        z_exp = sb("z_exp", [P, QUBITS, T])
        x_exp = sb("x_exp", [P, QUBITS, T])
        ev = sb("ev", [P, T + TILES, EV_STRIDE])
        ident = sb("ident", [P, P])
        ones = sb("ones", [P, P])
        before_f = sb("before_f", [P, P])
        before = sb("before", [P, P], BF16)
        ones_b = sb("ones_b", [P, P], BF16)
        minus_half = sb("minus_half", [P, TILES])
        tok_i = sb("tok_i", [P, T], I32)
        tok = sb("tok", [P, T])
        blk_i = sb("blk_i", [P, BLOCKS], I32)
        blk = sb("blk", [P, BLOCKS])
        exp_i = sb("exp_i", [P, E], I32)
        exp_f = sb("exp_f", [P, E])
        region_f = sb("region_f", [P, E])
        pad_rows = sb("pad_rows", [P, WIDTH])
        wz = sb("wz", [P, TILES, D])
        wqkv0 = sb("wqkv0", [P, 3 * D])
        wqkv1 = sb("wqkv1", [K1, 3 * D])
        wg0 = sb("wg0", [P, E])
        wg1 = sb("wg1", [D1, E])
        wqk_t0 = sb("wqk_t0", [P, 2, D + 1])
        wqk_t1 = sb("wqk_t1", [D1, 2, D + 1])
        score_w0 = sb("score_w0", [P, D + 1])
        score_w1 = sb("score_w1", [K1, D + 1])
        up0 = sb("up0", [P, E * HID])
        up1 = sb("up1", [K1, E * HID])
        spare = tables[:, :, :].rearrange("p f t -> p (f t)")
        down = spare[:, 0:E * HC * D]
        down_bias = spare[:, E * HC * D:E * HC * D + E * D]
        string_room = [z_both[:, :, :, :].rearrange("p a k t -> p (a k t)"), 0]
        angle_room = [angle_stages[:, :, :, :].rearrange("p a t f -> p (a t f)"), 0]

        def behind(room, pattern, **sizes):
            size = int(np.prod(list(sizes.values())))
            room[1] += size
            return room[0][:, room[1] - size:room[1]].rearrange(pattern, **sizes)

        hres = behind(string_room, "p (t d) -> p t d", t=T + TILES // 2, d=D)
        ev_b = sb("ev_b", [P, P])
        ev_t = sb("ev_t", [P, P])
        bn1 = sb("bn1", [P, TILES, 6])
        mv1 = sb("mv1", [P, TILES, 2])
        ve1 = sb("ve1", [P, TILES])
        rs1 = sb("rs1", [P, TILES])
        x1 = behind(string_room, "p (j d) -> p j d", j=TILES, d=D)
        xt0 = sb("xt0", [P, ROWS_KEPT, SEQ])
        xt1 = sb("xt1", [K1, ROWS_KEPT, SEQ])
        tq0 = sb("tq0", [P, SEQ])
        tq1 = sb("tq1", [K1, SEQ])
        val = behind(string_room, "p (j d) -> p j d", j=TILES, d=D)
        nmax = sb("nmax", [P, 2])
        rsum = sb("rsum", [P, TILES])
        rinv = sb("rinv", [P, TILES])
        prob = behind(string_room, "p (c k) -> p c k", c=2, k=SEQ)
        prob_t = behind(angle_room, "p (c k) -> p c k", c=2, k=SEQ)
        bn2 = sb("bn2", [P, 2, 6])
        mv2 = sb("mv2", [P, 2, 2])
        ve2 = sb("ve2", [P, 2])
        rs2 = sb("rs2", [P, 2])
        x2 = sb("x2", [P, ROWS_KEPT, TILES, WIDTH])
        x2t0 = sb("x2t0", [P, P])
        x2t1 = sb("x2t1", [D1, P])
        logit = sb("logit", [P, TILES, E])
        top = sb("top", [P, TILES, E])
        top_i = sb("top_i", [P, TILES, E], U32)
        gap = sb("gap", [P, TILES])
        gap_e = sb("gap_e", [P, TILES])
        gap_1 = sb("gap_1", [P, TILES])
        mask = sb("mask", [P, 2, TILES, E])
        both = sb("both", [P, TILES, E])
        ahead = sb("ahead", [P, TILES, E])
        here = sb("here", [P, E])
        here_b = sb("here_b", [P, E], BF16)
        so_far = sb("so_far", [P, E], BF16)
        rank = sb("rank", [P, E])
        place = sb("place", [P, TILES, E])
        slot_e = sb("slot_e", [P, 2, TILES, E])
        slot_f = sb("slot_f", [P, 2, TILES])
        slot = sb("slot", [P, ROWS_KEPT, 2, TILES], I32)
        count = sb("count", [P, E])
        count_i = sb("count_i", [P, E], I32)
        nblk_i = sb("nblk_i", [P, E], I32)
        nblk = sb("nblk", [P, E])
        cum = sb("cum", [P, 2, E])
        skip = sb("skip", [P, E])
        ge = behind(angle_room, "p (e m) -> p e m", e=E, m=BLOCKS)
        ge_w = behind(angle_room, "p (e m) -> p e m", e=E - 1, m=BLOCKS)
        t_exp = sb("t_exp", [P, BLOCKS])
        t_row = sb("t_row", [P, BLOCKS])
        t_first = sb("t_first", [P, BLOCKS])
        t_i = sb("t_i", [P, 3, BLOCKS], I32)
        xb = behind(angle_room, "p (n d) -> p n d", n=UNROLL, d=WIDTH)
        xbt0 = sb("xbt0", [P, P])
        xbt1 = sb("xbt1", [K1, P])
        hid = behind(angle_room, "p (n h) -> p n h", n=2, h=HID)
        up_now0 = behind(angle_room, "p (n h) -> p n h", n=2, h=HID)
        up_now1 = sb("up_now1", [K1, 2, HID])
        share = sb("share", [P, UNROLL])
        share_w = sb("share_w", [P, UNROLL, 2])
        dest = sb("dest", [P, UNROLL], I32)
        y_raw = sb("y_raw", [P, 2, D])
        y = sb("y", [P, UNROLL, D])

        b0, b1, b2, b3, b4, b5, b6, b7 = [bank(f"bank{i}") for i in range(8)]

        ids_in = sem("ids_in")
        angles_in = sem("angles_in")
        small_in = sem("small_in")
        up_in = sem("up_in")
        down_in = sem("down_in")
        const_done = sem("const_done")
        dve_step = sem("dve_step")
        trig_done = sem("trig_done")
        x_step = sem("x_step")
        pool_step = sem("pool_step")
        wt_done = sem("wt_done")
        wt_copied = sem("wt_copied")
        sw_done = sem("sw_done")
        ev_done = sem("ev_done")
        ev_copied = sem("ev_copied")
        evt_done = sem("evt_done")
        evt_copied = sem("evt_copied")
        emb_done = sem("emb_done")
        emb_copied = sem("emb_copied")
        var1_done = sem("var1_done")
        x1_done = sem("x1_done")
        rs1_done = sem("rs1_done")
        rs2_done = sem("rs2_done")
        rows_free = sem("rows_free")
        xt_done = sem("xt_done")
        xt_copied = sem("xt_copied")
        tq_done = sem("tq_done")
        tq_copied = sem("tq_copied")
        val_done = sem("val_done")
        val_copied = sem("val_copied")
        score_done = sem("score_done")
        max_done = sem("max_done")
        exp_done = sem("exp_done")
        pt_done = sem("pt_done")
        pt_copied = sem("pt_copied")
        pv_done = sem("pv_done")
        h2_done = sem("h2_done")
        var2_done = sem("var2_done")
        x2_done = sem("x2_done")
        x2t_done = sem("x2t_done")
        x2t_copied = sem("x2t_copied")
        logit_done = sem("logit_done")
        logit_copied = sem("logit_copied")
        gap_done = sem("gap_done")
        gap_exp = sem("gap_exp")
        mask_done = sem("mask_done")
        rank_done = sem("rank_done")
        rank_copied = sem("rank_copied")
        slot_done = sem("slot_done")
        scattered = sem("scattered")
        h2_out = sem("h2_out")
        count_done = sem("count_done")
        count_copied = sem("count_copied")
        table_done = sem("table_done")
        pads_out = sem("pads_out")
        block_in = [sem(f"block_in{i}") for i in range(UNROLL)]
        xbt_done = sem("xbt_done")
        xbt_copied = sem("xbt_copied")
        up_done = sem("up_done")
        gelu_done = sem("gelu_done")
        up0_copied = sem("up0_copied")
        up1_copied = sem("up1_copied")
        share_done = sem("share_done")
        y_mm = sem("y_mm")
        y_read = sem("y_read")
        y_done = sem("y_done")
        added = [sem(f"added{i}") for i in range(UNROLL)]
        passed = sem("passed")

        def hold(eng):
            eng.sem_inc(passed, 1)

        block = ctx.enter_context(nc.Block())

        @block.sync
        def _(sp):
            sp.dma_start(ids[:, :, :], ids_view).then_inc(ids_in, 16)
            sp.dma_start(wqkv0[:, :], qkv_w[0:P, :]).then_inc(small_in, 16)
            sp.dma_start(wqkv1[:, :], qkv_w[P:D + 1, :]).then_inc(small_in, 16)
            sp.dma_start(wz[:, :, :], emb_w.rearrange("p (j d) -> p j d", j=TILES)).then_inc(small_in, 16)
            sp.dma_start(wg0[:, :], gate_w[0:P, :]).then_inc(small_in, 16)
            sp.dma_start(wg1[:, :], gate_w[P:D, :]).then_inc(small_in, 16)
            sp.dma_start(up0[:, :], up_w[0:P, :]).then_inc(up_in, 16)
            sp.dma_start(up1[:, :], up_w[P:D + 1, :]).then_inc(up_in, 16)
            sp.wait_ge(const_done, 1)
            sp.dma_start(routed[PAD_ROW:PAD_ROW + P, :], pad_rows[:, :]).then_inc(pads_out, 16)
            sp.wait_ge(ev_done, 1)
            sp.dma_start(down, down_w).then_inc(down_in, 16)
            sp.dma_start(down_bias, down_b.partition_broadcast(P)).then_inc(down_in, 16)
            with sp.Fori(0, BATCHES) as b:
                sp.wait_ge(h2_done, b * TILES + TILES)
                sp.dma_start(out_view[bass.ds(b, 1)].rearrange("o p f -> (o p) f"),
                             hres[:, bass.ds(b * TILES, TILES), :].rearrange("p j d -> p (j d)")).then_inc(h2_out, 16)
            sp.wait_ge(count_copied, 2)
            for e in range(E):
                rows = sp.value_load(count_i[0:1, e:e + 1], min_val=0, max_val=TOKENS)
                sp.dma_start(routed[bass.ds(rows + e * REGION, P), :], pad_rows[:, :]).then_inc(pads_out, 16)
            sp.wait_ge(pads_out, 16 * E + 16)
            sp.wait_ge(scattered, 16 * 2 * (T + TILES))
            sp.wait_ge(table_done, 1)
            for n in range(UNROLL):
                row = sp.value_load(t_i[0:1, 1, n:n + 1], min_val=0, max_val=PAD_ROW)
                sp.dma_start(xb[:, n, :], routed[bass.ds(row, P), :]).then_inc(block_in[n], 16)
            with sp.Fori(0, BLOCKS // UNROLL - 1) as it:
                for n in range(UNROLL):
                    row = sp.value_load(t_i[0:1, 1, bass.ds((it + 1) * UNROLL + n, 1)], min_val=0, max_val=PAD_ROW)
                    sp.wait_ge(xbt_done, it * UNROLL + n + 1)
                    sp.wait_ge(share_done, (it * UNROLL + n) * 2 + 2)
                    sp.dma_start(xb[:, n, :], routed[bass.ds(row, P), :]).then_inc(block_in[n], 16)
            sp.wait_ge(h2_out, 16 * BATCHES)
            for n in range(UNROLL):
                sp.wait_ge(added[n], 16 * (BLOCKS // UNROLL) + 16)

        @block.gpsimd
        def _(pool):
            steps = [0]

            def step(instruction):
                steps[0] += 1
                instruction.then_inc(pool_step, 1)

            def join():
                pool.wait_ge(pool_step, steps[0])

            step(pool.memset(pad_rows[:, :], 0.0))
            join()
            pool.memset(pad_rows[:, WIDTH - 1:WIDTH], NO_TOKEN).then_inc(const_done, 1)
            pool.wait_ge(ids_in, 16)
            for t in range(T):
                b, j = divmod(t, TILES)
                pool.indirect_dma_start(out=theta[:, t, :], out_offset=None, in_=angles,
                                        in_offset=bass.IndirectOffsetOnAxis(ids[:, b, j:j + 1], 0)
                                        ).then_inc(angles_in, 16)
            step(pool.memset(ident[:, :], 0.0))
            step(pool.memset(ones[:, :], 1.0))
            step(pool.memset(minus_half[:, :], -0.5))
            step(pool.memset(ones_b[:, :], 1.0))
            step(pool.memset(so_far[:, :], 0.0))
            step(pool.iota(tok_i[:, :], [[SEQ, BATCHES], [1, TILES]], base=0, channel_multiplier=TILES))
            step(pool.iota(blk_i[:, :], [[1, BLOCKS]], base=0, channel_multiplier=0))
            step(pool.iota(exp_i[:, :], [[1, E]], base=0, channel_multiplier=0))
            join()
            step(pool.affine_select(out=ident[:, :], in_=ident[:, :], compare_op=ALU.not_equal, fill=1.0, base=0,
                                    pattern=[[-1, P]], channel_multiplier=1))
            step(pool.affine_select(out=before_f[:, :], in_=ones[:, :], compare_op=ALU.is_gt, fill=0.0, base=0,
                                    pattern=[[1, P]], channel_multiplier=-1))
            step(pool.tensor_copy(tok[:, :], tok_i[:, :]))
            step(pool.tensor_copy(blk[:, :], blk_i[:, :]))
            step(pool.tensor_copy(exp_f[:, :], exp_i[:, :]))
            join()
            step(pool.tensor_copy(before[:, :], before_f[:, :]))
            step(pool.tensor_scalar(region_f[:, :], exp_f[:, :], float(REGION), None, ALU.mult))
            join()
            pool.tensor_copy(exp_f[:, :], exp_i[:, :]).then_inc(const_done, 1)

            xsteps = [0]

            def xstep(instruction):
                xsteps[0] += 1
                instruction.then_inc(x_step, 1)

            def xjoin():
                pool.wait_ge(x_step, xsteps[0])

            pool.wait_ge(dve_step, TABLES_READY)
            for q in range(PAIRS):
                gather_products(pool, x_str[:, :, :], tables[:, :, :], T, [3, 3], "XYZ", X_SUPPORT[q], 9 * q, [3, 1],
                                xstep)
            gather_products(pool, x_str[:, :, :], tables[:, :, :], T, [3, 3, 3], "XYZ", X_SUPPORT[PAIRS], 9 * PAIRS,
                            [9, 3, 1], xstep)
            xjoin()
            pairs = x_str[:, 0:9 * PAIRS].rearrange("p (q a b) t -> p q a b t", q=PAIRS, a=3)
            for q in range(PAIRS):
                xstep(pool.tensor_tensor(pairs[:, q], pairs[:, q],
                                         rzy[:, q + 1].unsqueeze(1).to_broadcast([P, 3, 3, T]), ALU.mult))
            triple = x_str[:, 9 * PAIRS:X_STRINGS].rearrange("p (a b) t -> p a b t", b=3)
            xstep(pool.tensor_tensor(triple, triple, rzy[:, 1].unsqueeze(1).to_broadcast([P, 9, 3, T]), ALU.mult))
            xjoin()
            by3 = x_str[:, :, :].rearrange("p (a b) t -> p a b t", b=3)
            xstep(pool.tensor_tensor(x_sum[:, :, :], by3[:, :, 0], by3[:, :, 1], ALU.add))
            xjoin()
            xstep(pool.tensor_tensor(x_sum[:, :, :], x_sum[:, :, :], by3[:, :, 2], ALU.add))
            xjoin()
            xstep(pool.tensor_tensor(x_sum[:, 0:3 * PAIRS], x_sum[:, 0:3 * PAIRS],
                                     rzy[:, 0:PAIRS].rearrange("p q a t -> p (q a) t"), ALU.mult))
            triple2 = x_sum[:, 3 * PAIRS:].rearrange("p (a b) t -> p a b t", b=3)
            xstep(pool.tensor_tensor(triple2, triple2, rzy[:, 0].unsqueeze(1).to_broadcast([P, 3, 3, T]), ALU.mult))
            xjoin()
            sum_by3 = x_sum[:, :, :].rearrange("p (a b) t -> p a b t", b=3)
            xstep(pool.tensor_tensor(x_sum2[:, :, :], sum_by3[:, :, 0], sum_by3[:, :, 1], ALU.add))
            xjoin()
            xstep(pool.tensor_tensor(x_sum2[:, :, :], x_sum2[:, :, :], sum_by3[:, :, 2], ALU.add))
            xjoin()
            xstep(pool.tensor_copy(x_exp[:, 0:PAIRS], x_sum2[:, 0:PAIRS]))
            xstep(pool.tensor_tensor(x_sum2[:, PAIRS:], x_sum2[:, PAIRS:], rzy[:, PAIRS], ALU.mult))
            xjoin()
            xstep(pool.tensor_tensor(x_exp[:, PAIRS], x_sum2[:, PAIRS], x_sum2[:, PAIRS + 1], ALU.add))
            xjoin()
            xstep(pool.tensor_tensor(x_exp[:, PAIRS], x_exp[:, PAIRS], x_sum2[:, PAIRS + 2], ALU.add))
            assert xsteps[0] == X_DONE, xsteps

            def copy_ev(b):
                if not (isinstance(b, int) and b == 0):
                    pool.wait_ge(evt_done, b)
                pool.tensor_copy(ev_b[:, :], ev[:, bass.ds(b * TILES, TILES), :].rearrange("p j e -> p (j e)")
                                 ).then_inc(ev_copied, 1)

            def rstd1(b):
                pool.wait_ge(var1_done, b + 1)
                pool.tensor_tensor(rs1[:, :], ve1[:, :], minus_half[:, :], ALU.pow).then_inc(rs1_done, 1)

            def rstd2(b, s):
                pool.wait_ge(var2_done, b * TILES + s + 1)
                pool.tensor_tensor(rs2[:, s % 2:s % 2 + 1], ve2[:, s % 2:s % 2 + 1], minus_half[:, 0:1], ALU.pow
                                   ).then_inc(rs2_done, 1)

            def scatter(b, kept, j):
                if j == 0:
                    pool.wait_ge(slot_done, b + 2)
                    hold(pool)
                for k in range(2):
                    pool.indirect_dma_start(out=routed, out_offset=bass.IndirectOffsetOnAxis(
                        slot[:, kept, k, j:j + 1], 0), in_=x2[:, kept, j, :], in_offset=None,
                        bounds_check=PAD_ROW - 1, oob_is_err=False).then_inc(scattered, 16)

            def free_rows(b):
                pool.wait_ge(scattered, b * (16 * 2 * TILES) + 2 * (16 * 2 * TILES))
                pool.sem_inc(rows_free, 1)

            step(pool.memset(dest[:, :], TOKENS))
            step(pool.memset(y[:, :, :], 0.0))
            join()
            for n in range(UNROLL):
                pool.indirect_dma_start(out=out_rows, out_offset=bass.IndirectOffsetOnAxis(dest[:, n:n + 1], 0),
                                        in_=y[:, n, :], in_offset=None, bounds_check=TOKENS - 1,
                                        oob_is_err=False, compute_op=ALU.add).then_inc(added[n], 16)
            pool.sem_inc(rows_free, 1)
            pool.wait_ge(ev_done, 1)
            copy_ev(0)
            rstd1(0)
            copy_ev(1)

            def batch(b, kept, first=False, last=False):
                older = (kept - 2) % ROWS_KEPT
                if not first:
                    rstd2(b - 1, 3)
                if not last:
                    rstd1(b + 1)
                if not first:
                    scatter(b - 2, older, 0)
                rstd2(b, 0)
                if not first:
                    scatter(b - 2, older, 1)
                rstd2(b, 1)
                if not last:
                    copy_ev(b + 2)
                if not first:
                    scatter(b - 2, older, 2)
                rstd2(b, 2)
                if not first:
                    scatter(b - 2, older, 3)
                    free_rows(b - 2)

            batch(0, 0, first=True)
            with pool.Fori(0, (BATCHES - 2) // ROWS_KEPT) as i:
                for k in range(ROWS_KEPT):
                    batch(ROWS_KEPT * i + k + 1, (k + 1) % ROWS_KEPT)
            batch(BATCHES - 1, (BATCHES - 1) % ROWS_KEPT, last=True)
            rstd2(BATCHES - 1, 3)
            for b in (BATCHES - 2, BATCHES - 1):
                for j in range(TILES):
                    scatter(b, b % ROWS_KEPT, j)

            pool.wait_ge(h2_out, 16 * BATCHES)
            pool.wait_ge(table_done, 1)
            with pool.Fori(0, BLOCKS // UNROLL) as it:
                for n in range(UNROLL):
                    m = it * UNROLL + n
                    first_of_expert = pool.value_load(t_i[0:1, 2, bass.ds(m, 1)], min_val=0, max_val=BLOCKS)
                    pool.wait_ge(y_done, m + 1)
                    for k in range(UNROLL):
                        pool.wait_ge(added[k], (first_of_expert + (UNROLL - 1 - k)) // UNROLL * 16 + 16)
                    hold(pool)
                    pool.indirect_dma_start(out=out_rows, out_offset=bass.IndirectOffsetOnAxis(dest[:, n:n + 1], 0),
                                            in_=y[:, n, :], in_offset=None, bounds_check=TOKENS - 1,
                                            oob_is_err=False, compute_op=ALU.add).then_inc(added[n], 16)

        @block.vector
        def _(dve):
            steps = [0]

            def step(instruction):
                steps[0] += 1
                instruction.then_inc(dve_step, 1)

            def join():
                dve.wait_ge(dve_step, steps[0])

            step(dve.memset(ev[:, :, :], 0.0))
            step(dve.memset(half_pi[:, :], math.pi / 2))
            dve.memset(xt1[D1:K1, :, :], 1.0)
            dve.memset(xbt1[D1:K1, :], 1.0)
            step(dve.memset(bloch[:, :, 0, :], 1.0))
            join()
            step(dve.memset(ev[:, :, QUBITS:QUBITS + 1], 1.0))
            dve.wait_ge(angles_in, 16 * T)
            step(dve.tensor_scalar(turns[:, :, :], theta[:, :, :], 1 / (2 * math.pi), ROUNDER, ALU.mult, ALU.add))
            join()
            step(dve.tensor_scalar(turned[:, :, :], turns[:, :, :], ROUNDER, TWO_PI_HIGH, ALU.subtract, ALU.mult))
            step(dve.tensor_scalar(folded[:, :, :], turns[:, :, :], ROUNDER, TWO_PI_LOW, ALU.subtract, ALU.mult))
            join()
            step(dve.tensor_tensor(theta[:, :, :], theta[:, :, :], turned[:, :, :], ALU.subtract))
            join()
            step(dve.tensor_tensor(theta[:, :, :], theta[:, :, :], folded[:, :, :], ALU.subtract))
            join()
            step(dve.tensor_scalar(turned[:, :, :], theta[:, :, :], PI_BELOW, -PI_BELOW, ALU.min, ALU.max))
            join()
            assert steps[0] == REDUCED
            step(dve.scalar_tensor_tensor(folded[:, :, :], turned[:, :, :], -1.0, turned[:, :, :], ALU.mult, ALU.max))

            def sin_of(layer, gate):
                first = (layer * QUBITS * 2) + gate
                return sine[:, first:first + 2 * QUBITS - 1:2, :]

            def cos_of(layer, gate):
                first = (layer * QUBITS * 2) + gate
                return cosine[:, first:first + 2 * QUBITS - 1:2, :]

            dve.wait_ge(trig_done, 2)
            step(dve.tensor_copy(bloch[:, :, 1, :], cos_of(0, 0)))
            step(dve.tensor_tensor(bloch[:, :, 2, :], sin_of(0, 0), cos_of(0, 1), ALU.mult))
            step(dve.tensor_tensor(bloch[:, :, 3, :], sin_of(0, 0), sin_of(0, 1), ALU.mult))
            step(dve.tensor_copy(ry[:, :, 0, :], cos_of(1, 0)))
            step(dve.tensor_scalar(ry[:, :, 1, :], sin_of(1, 0), -1.0, None, ALU.mult))
            step(dve.tensor_tensor(rzy[:, :, 0, :], cos_of(1, 1), cos_of(1, 0), ALU.mult))
            step(dve.tensor_scalar(rzy[:, :, 1, :], sin_of(1, 1), -1.0, None, ALU.mult))
            step(dve.tensor_tensor(rzy[:, :, 2, :], cos_of(1, 1), sin_of(1, 0), ALU.mult))
            join()
            for h in range(2):
                step(dve.tensor_tensor(pair[:, h].rearrange("p (a b) t -> p a b t", a=4),
                                       bloch[:, 3 * h + 1].unsqueeze(2).to_broadcast([P, 4, 4, T]),
                                       bloch[:, 3 * h].unsqueeze(1).to_broadcast([P, 4, 4, T]), ALU.mult))
            join()
            for h, at in ((0, 0), (1, 128)):
                step(dve.tensor_tensor(tables[:, at:at + 64].rearrange("p (a b) t -> p a b t", a=4),
                                       bloch[:, 3 * h + 2].unsqueeze(2).to_broadcast([P, 4, 16, T]),
                                       pair[:, h].unsqueeze(1).to_broadcast([P, 4, 16, T]), ALU.mult))
            join()
            step(dve.tensor_scalar(tables[:, 64:128], tables[:, 0:64], -1.0, None, ALU.mult))
            join()
            assert steps[0] == TABLES_READY, steps

            def times_qubit(result, at, q, factors, first, n):
                step(dve.tensor_tensor(result[:, at:at + 2 * n].rearrange("p (a b) t -> p a b t", a=2),
                                       ry[:, q].unsqueeze(2).to_broadcast([P, 2, n, T]),
                                       factors[:, first:first + n].unsqueeze(1).to_broadcast([P, 2, n, T]), ALU.mult))

            times_qubit(z_coef, Z_BLOCK[1], 1, ry[:, 0], 0, 2)
            times_qubit(z_part, 0, 2, ry[:, 1], 0, 2)
            join()
            times_qubit(z_coef, Z_BLOCK[2], 2, z_coef, Z_BLOCK[1], 4)
            times_qubit(z_part, 4, 3, z_part, 0, 4)
            join()
            times_qubit(z_coef, Z_BLOCK[3], 3, z_coef, Z_BLOCK[2], 8)
            times_qubit(z_part, 12, 4, z_part, 4, 8)
            join()
            times_qubit(z_coef, Z_BLOCK[4], 4, z_coef, Z_BLOCK[3], 16)
            times_qubit(z_coef, Z_BLOCK[0], 5, z_part, 12, 16)
            join()
            times_qubit(z_coef, Z_BLOCK[5], 5, z_coef, Z_BLOCK[4], 32)
            for q in range(QUBITS):
                k = len(Z_SUPPORT[q])
                gather_products(dve, z_str[:, :, :], tables[:, :, :], T, [2] * k, "ZX", Z_SUPPORT[q], Z_BLOCK[q],
                                [2 ** i for i in range(k)], step)
            join()
            step(dve.tensor_tensor(z_str[:, :, :], z_str[:, :, :], z_coef[:, :, :], ALU.mult))
            join()
            for q in range(QUBITS):
                k = 2 ** len(Z_SUPPORT[q])
                step(dve.tensor_reduce(z_exp[:, q], z_str[:, Z_BLOCK[q]:Z_BLOCK[q] + k].rearrange("p k t -> p t k"),
                                       AX.X, ALU.add))
            join()
            step(dve.tensor_tensor(z_exp[:, :, :], z_exp[:, :, :], cos_of(2, 0), ALU.mult))
            dve.wait_ge(x_step, X_DONE)
            step(dve.tensor_tensor(x_exp[:, :, :], x_exp[:, :, :], sin_of(2, 0), ALU.mult))
            join()
            dve.tensor_tensor(ev[:, 0:T, 0:QUBITS].rearrange("p t q -> p q t"), z_exp[:, :, :], x_exp[:, :, :],
                              ALU.subtract).then_inc(ev_done, 1)

            for i in range(4):
                dve.wait_ge(wt_done, i + 1)
                src, dst = [(b4, wqk_t0), (b5, wqk_t1), (b6, wqk_t0), (b7, wqk_t1)][i]
                rows = P if i % 2 == 0 else D1
                dve.tensor_copy(dst[0:rows, i // 2, :], src[0:rows, 0:D + 1]).then_inc(wt_copied, 1)
            dve.wait_ge(sw_done, 2)
            dve.tensor_scalar(score_w0[:, :], b0[:, 0:D + 1], SCALE, None, ALU.mult)
            dve.tensor_scalar(score_w1[:, :], b1[0:K1, 0:D + 1], SCALE, None, ALU.mult).then_inc(wt_copied, 1)

            base = steps[0]

            class Chain:
                def __init__(self, per):
                    self.per, self.start, self.n = per, 0, 0

                def begin(self, b):
                    self.start, self.n = b * self.per + base, 0

                def step(self, instruction):
                    self.n += 1
                    instruction.then_inc(dve_step, 1)

                def join(self):
                    dve.wait_ge(dve_step, self.start + self.n)

                def join_held(self):
                    self.join()
                    hold(dve)

                def end(self):
                    assert self.n == self.per, self.n

            chain = Chain(CHAIN)

            def emb_copy(b, half):
                dve.wait_ge(emb_done, 2 * b + half + 1)
                dve.tensor_copy(hres[:, bass.ds(b * TILES + 2 * half, 2), :],
                                b0[:, 0:2 * D].rearrange("p (j d) -> p j d", j=2)).then_inc(emb_copied, 1)

            def stats1(b):
                dve.wait_ge(emb_copied, 2 * b + 2)
                hold(dve)
                for j in range(TILES):
                    chain.step(dve.bn_stats(bn1[:, j, :], hres[:, bass.ds(b * TILES + j, 1), :].rearrange("p o d -> p (o d)")))
                chain.join_held()
                for j in range(TILES):
                    chain.step(dve.bn_aggr(mv1[:, j, :], bn1[:, j, :]))
                chain.join()
                dve.tensor_scalar(ve1[:, :], mv1[:, :, 1], EPS, None, ALU.add).then_inc(var1_done, 1)

            def norm1(b):
                dve.wait_ge(rs1_done, b + 1)
                if not (isinstance(b, int) and b == 0):
                    dve.wait_ge(xt_done, b)
                for j in range(TILES):
                    last = dve.tensor_scalar(x1[:, j, :], hres[:, bass.ds(b * TILES + j, 1), :].rearrange(
                        "p o d -> p (o d)"), mv1[:, j, 0:1], rs1[:, j:j + 1], ALU.subtract, ALU.mult)
                last.then_inc(x1_done, 1)

            def norm2(b, kept, s):
                i = b * TILES + s
                dve.wait_ge(rs2_done, i + 1)
                dve.tensor_scalar(x2[:, kept, s, 0:D], hres[:, bass.ds(i, 1), :].rearrange("p o d -> p (o d)"),
                                  mv2[:, s % 2, 0:1], rs2[:, s % 2:s % 2 + 1], ALU.subtract, ALU.mult
                                  ).then_inc(x2_done, 1)

            def val_copy(b, half):
                dve.wait_ge(val_done, 2 * b + half + 1)
                dve.tensor_copy(val[:, 2 * half:2 * half + 2, :],
                                (b2, b3)[half][:, 0:2 * D].rearrange("p (j d) -> p j d", j=2)).then_inc(val_copied, 1)

            def row_max(b, s):
                i = b * TILES + s
                dve.wait_ge(score_done, i + 1)
                if not (isinstance(b, int) and b == 0 and s < 2):
                    dve.wait_ge(exp_done, i - 1)
                dve.tensor_reduce(nmax[:, s % 2:s % 2 + 1], (b4, b5)[s % 2][:, :], AX.X, ALU.max, negate=True
                                  ).then_inc(max_done, 1)

            def pt_copy(b, s):
                dve.wait_ge(pt_done, b * TILES + s + 1)
                dve.tensor_copy(prob_t[:, s % 2, :], b6[:, :]).then_inc(pt_copied, 1)

            def residual(b, s):
                i = b * TILES + s
                c = s % 2
                chain.step(dve.reciprocal(rinv[:, s:s + 1], rsum[:, s:s + 1]))
                dve.wait_ge(pv_done, i + 1)
                chain.join()
                row = hres[:, bass.ds(i, 1), :].rearrange("p o d -> p (o d)")
                dve.scalar_tensor_tensor(row, b7[:, 0:D], rinv[:, s:s + 1], row, ALU.mult, ALU.add).then_inc(h2_done, 1)
                dve.wait_ge(h2_done, i + 1)
                hold(dve)
                chain.step(dve.bn_stats(bn2[:, c, :], row))
                chain.join_held()
                chain.step(dve.bn_aggr(mv2[:, c, :], bn2[:, c, :]))
                chain.join()
                dve.tensor_scalar(ve2[:, c:c + 1], mv2[:, c, 1:2], EPS, None, ALU.add).then_inc(var2_done, 1)

            def logit_copy(b):
                dve.wait_ge(logit_done, b * TILES + TILES)
                dve.tensor_copy(logit[:, :, :].rearrange("p j e -> p (j e)"),
                                b1[:, 256:256 + TILES * E]).then_inc(logit_copied, 1)

            def route_a(b, par):
                dve.wait_ge(logit_copied, b + 1)
                hold(dve)
                for j in range(TILES):
                    chain.step(dve.max(top[:, j, :], logit[:, j, :]))
                chain.join_held()
                for j in range(TILES):
                    chain.step(dve.max_index(top_i[:, j, :], top[:, j, :], logit[:, j, :]))
                dve.tensor_tensor(gap[:, :], top[:, :, 1], top[:, :, 0], ALU.subtract).then_inc(gap_done, 1)
                chain.join()
                chain.step(dve.tensor_copy(x2[:, par, :, D:D + 2], top_i[:, :, 0:2]))
                chain.step(dve.tensor_copy(x2[:, par, :, D + 4], tok[:, bass.ds(b * TILES, TILES)]))
                chain.join()
                chain.step(dve.tensor_tensor(
                    mask[:, :, :, :], x2[:, par, :, D:D + 2].rearrange("p j k -> p k j").unsqueeze(3).to_broadcast([P, 2, TILES, E]),
                    exp_f[:, :].unsqueeze(1).unsqueeze(1).to_broadcast([P, 2, TILES, E]), ALU.is_equal))
                chain.join()
                chain.step(dve.tensor_tensor(both[:, :, :], mask[:, 0], mask[:, 1], ALU.add))
                chain.join()
                chain.step(dve.tensor_copy(ahead[:, 1, :], both[:, 0, :]))
                chain.step(dve.tensor_tensor(ahead[:, 2, :], both[:, 0, :], both[:, 1, :], ALU.add))
                chain.join()
                chain.step(dve.tensor_tensor(ahead[:, 3, :], ahead[:, 2, :], both[:, 2, :], ALU.add))
                chain.join()
                chain.step(dve.tensor_tensor(here[:, :], ahead[:, 3, :], both[:, 3, :], ALU.add))
                chain.join()
                dve.tensor_copy(here_b[:, :], here[:, :]).then_inc(mask_done, 1)

            def rank_copy(b):
                dve.wait_ge(rank_done, b + 1)
                dve.tensor_tensor(rank[:, :], b1[:, 288:288 + E], region_f[:, :], ALU.add).then_inc(rank_copied, 1)

            def route_b(b, par):
                dve.wait_ge(gap_exp, b + 1)
                chain.step(dve.tensor_scalar(gap_1[:, :], gap_e[:, :], 1.0, None, ALU.add))
                chain.join()
                chain.step(dve.reciprocal(x2[:, par, :, D + 2], gap_1[:, :]))
                chain.join()
                chain.step(dve.tensor_tensor(x2[:, par, :, D + 3], x2[:, par, :, D + 2], gap_e[:, :], ALU.mult))
                chain.step(dve.tensor_tensor(so_far[:, :], so_far[:, :], here[:, :], ALU.add))
                dve.wait_ge(rank_copied, b + 1)
                chain.step(dve.tensor_tensor(place[:, :, :], ahead[:, :, :],
                                             rank[:, :].unsqueeze(1).to_broadcast([P, TILES, E]), ALU.add))
                chain.join()
                chain.step(dve.tensor_tensor(slot_e[:, :, :, :], mask[:, :, :, :],
                                             place[:, :, :].unsqueeze(1).to_broadcast([P, 2, TILES, E]), ALU.mult))
                chain.join()
                chain.step(dve.tensor_reduce(slot_f[:, :, :], slot_e[:, :, :, :], AX.X, ALU.add))
                chain.join()
                dve.tensor_copy(slot[:, par, :, :], slot_f[:, :, :]).then_inc(slot_done, 1)

            dve.memset(x2[:, ROWS_KEPT - 1, :, :], 0.0)
            dve.memset(slot[:, ROWS_KEPT - 1, :, :], PAD_ROW + P).then_inc(slot_done, 1)
            dve.memset(ahead[:, 0, :], 0.0).then_inc(const_done, 1)
            dve.wait_ge(const_done, 3)
            dve.wait_ge(slot_done, 1)
            chain.begin(0)
            emb_copy(0, 0)
            emb_copy(0, 1)
            stats1(0)
            norm1(0)
            base = base + chain.n
            emb_copy(1, 0)
            row_max(0, 0)

            def batch(b, kept, first=False, last=False):
                before_kept = (kept - 1) % ROWS_KEPT
                chain.begin(b)
                if not first:
                    norm2(b - 1, before_kept, 2)
                row_max(b, 1)
                if not last:
                    emb_copy(b + 1, 1)
                pt_copy(b, 0)
                if not first:
                    residual(b - 1, 3)
                val_copy(b, 0)
                val_copy(b, 1)
                if not last:
                    stats1(b + 1)
                if not first:
                    norm2(b - 1, before_kept, 3)
                row_max(b, 2)
                pt_copy(b, 1)
                if not last:
                    norm1(b + 1)
                residual(b, 0)
                if not first:
                    logit_copy(b - 1)
                    dve.wait_ge(rows_free, b)
                norm2(b, kept, 0)
                row_max(b, 3)
                pt_copy(b, 2)
                residual(b, 1)
                if not first:
                    route_a(b - 1, before_kept)
                norm2(b, kept, 1)
                if not last:
                    row_max(b + 1, 0)
                if not first:
                    rank_copy(b - 1)
                if not last:
                    emb_copy(b + 2, 0)
                pt_copy(b, 3)
                residual(b, 2)
                if not first:
                    route_b(b - 1, before_kept)

            batch(0, 0, first=True)
            base = base + chain.n - CHAIN
            with dve.Fori(0, (BATCHES - 2) // ROWS_KEPT) as i:
                for k in range(ROWS_KEPT):
                    batch(ROWS_KEPT * i + k + 1, (k + 1) % ROWS_KEPT)
                    chain.end()
            batch(BATCHES - 1, (BATCHES - 1) % ROWS_KEPT, last=True)
            final, final_kept = BATCHES - 1, (BATCHES - 1) % ROWS_KEPT
            norm2(final, final_kept, 2)
            residual(final, 3)
            norm2(final, final_kept, 3)
            logit_copy(final)
            route_a(final, final_kept)
            rank_copy(final)
            route_b(final, final_kept)

            dve.wait_ge(count_done, 1)
            dve.tensor_copy(count[:, :], b1[:, 304:304 + E]).then_inc(count_copied, 1)
            dve.tensor_copy(count_i[:, :], b1[:, 304:304 + E]).then_inc(count_copied, 1)
            dve.wait_ge(count_copied, 2)
            chain.step(dve.tensor_scalar(count[:, :], count[:, :], float(P - 1), None, ALU.add))
            chain.join()
            chain.step(dve.tensor_copy(nblk_i[:, :], count[:, :]))
            chain.join()
            chain.step(dve.tensor_scalar(nblk_i[:, :], nblk_i[:, :], 7, None, ALU.arith_shift_right))
            chain.join()
            chain.step(dve.tensor_copy(nblk[:, :], nblk_i[:, :]))
            chain.join()
            chain.step(dve.tensor_copy(cum[:, 0, :], nblk[:, :]))
            chain.step(dve.tensor_scalar(skip[:, :], nblk[:, :], -float(P), float(REGION), ALU.mult, ALU.add))
            chain.join()
            c = 0
            for shift in (1, 2, 4):
                chain.step(dve.tensor_copy(cum[:, 1 - c, 0:shift], cum[:, c, 0:shift]))
                chain.step(dve.tensor_tensor(cum[:, 1 - c, shift:E], cum[:, c, shift:E], cum[:, c, 0:E - shift], ALU.add))
                chain.join()
                c = 1 - c
            chain.step(dve.tensor_tensor(ge[:, :, :], blk[:, :].unsqueeze(1).to_broadcast([P, E, BLOCKS]),
                                         cum[:, c, :].unsqueeze(2).to_broadcast([P, E, BLOCKS]), ALU.is_ge))
            chain.join()
            past = ge[:, 0:E - 1, :]
            chain.step(dve.tensor_reduce(t_exp[:, :], past.rearrange("p e m -> p m e"), AX.X, ALU.add))
            for values, result in ((skip, t_row), (nblk, t_first)):
                chain.step(dve.tensor_tensor(ge_w[:, :, :], past, values[:, 0:E - 1].unsqueeze(2).to_broadcast(
                    [P, E - 1, BLOCKS]), ALU.mult))
                chain.join()
                chain.step(dve.tensor_reduce(result[:, :], ge_w[:, :, :].rearrange("p e m -> p m e"), AX.X, ALU.add))
                chain.join()
            chain.step(dve.scalar_tensor_tensor(t_row[:, :], blk[:, :], float(P), t_row[:, :], ALU.mult, ALU.add))
            chain.join()
            chain.step(dve.tensor_scalar(t_row[:, :], t_row[:, :], -float(PAD_ROW), None, ALU.add))
            chain.join()
            chain.step(dve.tensor_tensor(ge_w[:, 0, :], t_row[:, :], ge[:, E - 1, :], ALU.mult))
            chain.join()
            chain.step(dve.tensor_tensor(t_row[:, :], t_row[:, :], ge_w[:, 0, :], ALU.subtract))
            chain.join()
            chain.step(dve.tensor_scalar(t_row[:, :], t_row[:, :], float(PAD_ROW), None, ALU.add))
            chain.join()
            dve.tensor_copy(t_i[:, 0, :], t_exp[:, :])
            dve.tensor_copy(t_i[:, 2, :], t_first[:, :])
            dve.tensor_copy(t_i[:, 1, :], t_row[:, :]).then_inc(table_done, 1)

            def share_of(m, n, round_of):
                dve.wait_ge(block_in[n], round_of * 16)
                dve.scalar_tensor_tensor(share_w[:, n, :], xb[:, n, D:D + 2], t_exp[:, bass.ds(m, 1)],
                                         xb[:, n, D + 2:D + 4], ALU.is_equal, ALU.mult,
                                         accum_out=share[:, n:n + 1]).then_inc(share_done, 1)
                dve.tensor_copy(dest[:, n:n + 1], xb[:, n, D + 4:D + 5]).then_inc(share_done, 1)

            def up_copy(m, n, free):
                e = dve.value_load(t_i[0:1, 0, bass.ds(m, 1)], min_val=0, max_val=E - 1)
                if free:
                    dve.wait_ge(up_done, m - 1)
                dve.tensor_copy(up_now0[:, n % 2, :], up0[:, bass.ds(e * HID, HID)]).then_inc(up0_copied, 1)
                return e

            def finish(m, n, e):
                dve.wait_ge(y_mm, m + 1)
                dve.tensor_tensor(y_raw[:, n % 2, :], (b5, b6)[n % 2][:, 0:D],
                                  down_bias[:, bass.ds(e * D, D)], ALU.add).then_inc(y_read, 1)
                dve.wait_ge(y_read, m + 1)
                dve.wait_ge(share_done, m * 2 + 2)
                dve.tensor_scalar(y[:, n, :], y_raw[:, n % 2, :], share[:, n:n + 1], None, ALU.mult
                                  ).then_inc(y_done, 1)

            dve.wait_ge(down_in, 32)
            dve.wait_ge(table_done, 1)
            dve.wait_ge(added[0], 16)
            share_of(0, 0, 1)
            up_copy(0, 0, False)
            up_copy(1, 1, False)

            def expert_block(m, n, it, more, more2):
                if more2:
                    up_copy(m + 2, n, True)
                if more:
                    dve.wait_ge(added[(n + 1) % UNROLL], (it + (n + 1) // UNROLL) * 16 + 16)
                    share_of(m + 1, (n + 1) % UNROLL, it + 1 + (n + 1) // UNROLL)
                e = dve.value_load(t_i[0:1, 0, bass.ds(m, 1)], min_val=0, max_val=E - 1)
                finish(m, n, e)

            rounds = BLOCKS // UNROLL
            for n in range(UNROLL):
                expert_block(n, n, 0, True, True)
            with dve.Fori(1, rounds - 1) as it:
                for n in range(UNROLL):
                    expert_block(it * UNROLL + n, n, it, True, True)
            for n in range(UNROLL):
                expert_block((rounds - 1) * UNROLL + n, n, rounds - 1, n < UNROLL - 1, n < UNROLL - 2)

        @block.scalar
        def _(act):
            act.wait_ge(dve_step, REDUCED)
            act.activation(sine[:, :, :], turned[:, :, :].rearrange("p t f -> p f t"), ACT.Sin).then_inc(trig_done, 1)
            act.wait_ge(dve_step, REDUCED + 1)
            act.activation(cosine[:, :, :], folded[:, :, :].rearrange("p t f -> p f t"), ACT.Sin,
                           bias=half_pi[:, 0:1], scale=-1.0).then_inc(trig_done, 1)

            def evt_copy(b):
                act.wait_ge(evt_done, b + 1)
                act.copy(ev_t[:, :], b2[:, 0:P]).then_inc(evt_copied, 1)

            def xt_copy(b, kept):
                act.wait_ge(xt_done, b + 1)
                act.copy(xt0[:, kept, :], b2[:, :])
                act.copy(xt1[0:D1, kept, :], b3[0:D1, :]).then_inc(xt_copied, 1)

            def tq_copy(b):
                act.wait_ge(tq_done, b + 1)
                act.copy(tq0[:, :], b2[:, :])
                act.copy(tq1[:, :], b3[0:K1, :]).then_inc(tq_copied, 1)

            def softmax(b, s):
                i = b * TILES + s
                act.wait_ge(max_done, i + 1)
                if not (isinstance(b, int) and b == 0 and s < 2):
                    act.wait_ge(pt_done, i - 1)
                if not (isinstance(b, int) and b == 0):
                    act.wait_ge(h2_done, i - 3)
                act.activation(prob[:, s % 2, :], (b4, b5)[s % 2][:, :], ACT.Exp, bias=nmax[:, s % 2:s % 2 + 1],
                               accum_out=rsum[:, s:s + 1]).then_inc(exp_done, 1)

            def x2t_copy(b, s):
                act.wait_ge(x2t_done, b * TILES + s + 1)
                act.copy(x2t0[:, :], b1[:, 0:P])
                act.copy(x2t1[:, :], b1[0:D1, P:2 * P]).then_inc(x2t_copied, 1)

            def gap_exponent(b):
                act.wait_ge(gap_done, b + 1)
                act.activation(gap_e[:, :], gap[:, :], ACT.Exp).then_inc(gap_exp, 1)

            evt_copy(0)
            xt_copy(0, 0)
            tq_copy(0)
            evt_copy(1)
            softmax(0, 0)

            def batch(b, kept, first=False, last=False):
                softmax(b, 1)
                if not first:
                    x2t_copy(b - 1, 2)
                softmax(b, 2)
                if not first:
                    x2t_copy(b - 1, 3)
                if not last:
                    xt_copy(b + 1, (kept + 1) % ROWS_KEPT)
                softmax(b, 3)
                if not last:
                    tq_copy(b + 1)
                x2t_copy(b, 0)
                if not last:
                    evt_copy(b + 2)
                    softmax(b + 1, 0)
                x2t_copy(b, 1)
                if not first:
                    gap_exponent(b - 1)

            batch(0, 0, first=True)
            with act.Fori(0, (BATCHES - 2) // ROWS_KEPT) as i:
                for k in range(ROWS_KEPT):
                    batch(ROWS_KEPT * i + k + 1, (k + 1) % ROWS_KEPT)
            batch(BATCHES - 1, (BATCHES - 1) % ROWS_KEPT, last=True)
            x2t_copy(BATCHES - 1, 2)
            x2t_copy(BATCHES - 1, 3)
            gap_exponent(BATCHES - 1)

            def xbt_copy(m):
                act.wait_ge(xbt_done, m + 1)
                act.copy(xbt0[:, :], b0[:, 0:P])
                act.copy(xbt1[0:D1, :], b0[0:D1, P:2 * P]).then_inc(xbt_copied, 1)

            def gelu(m, n):
                act.wait_ge(up_done, m + 1)
                act.activation(hid[:, n % 2, :], (b1, b2)[n % 2][:, 0:HID], ACT.Gelu).then_inc(gelu_done, 1)

            def up_copy(m, n):
                e = act.value_load(t_i[0:1, 0, bass.ds(m, 1)], min_val=0, max_val=E - 1)
                act.copy(up_now1[:, n % 2, :], up1[:, bass.ds(e * HID, HID)]).then_inc(up1_copied, 1)

            act.wait_ge(up_in, 32)
            act.wait_ge(table_done, 1)
            up_copy(0, 0)
            up_copy(1, 1)
            xbt_copy(0)
            xbt_copy(1)
            with act.Fori(0, BLOCKS // UNROLL - 1) as it:
                for n in range(UNROLL):
                    gelu(it * UNROLL + n, n)
                    up_copy(it * UNROLL + n + 2, n)
                    xbt_copy(it * UNROLL + n + 2)
            for n in range(UNROLL):
                gelu(BLOCKS - UNROLL + n, n)
                if n < UNROLL - 2:
                    up_copy(BLOCKS - UNROLL + n + 2, n)
                    xbt_copy(BLOCKS - UNROLL + n + 2)

        @block.tensor
        def _(pe):
            pe.wait_ge(const_done, 2)
            pe.wait_ge(small_in, 16 * 5)
            for i in range(2):
                cols = slice(i * D, i * D + P), slice(i * D + P, (i + 1) * D)
                for c, dst in enumerate(((b4, b5), (b6, b7))[i]):
                    rows = (P, D1)[c]
                    pe.transpose(dst[0:rows, 0:P], wqkv0[:, cols[c]], ident[:, :])
                    pe.transpose(dst[0:rows, P:D + 1], wqkv1[:, cols[c]], ident[0:K1, 0:K1]).then_inc(wt_done, 1)
            pe.wait_ge(wt_copied, 4)
            for dst, cols in ((b0, slice(0, P)), (b1, slice(P, D + 1))):
                m = cols.stop - cols.start
                pe.matmul(dst[0:m, 0:D + 1], wqk_t0[:, 0, cols], wqk_t0[:, 1, :], start=True, stop=False)
                pe.matmul(dst[0:m, 0:D + 1], wqk_t1[:, 0, cols], wqk_t1[:, 1, :], start=False, stop=True
                          ).then_inc(sw_done, 1)
            pe.wait_ge(wt_copied, 5)

            def ev_transpose(b):
                pe.wait_ge(ev_copied, b + 1)
                if not (isinstance(b, int) and b == 0):
                    pe.wait_ge(tq_copied, b)
                pe.transpose(b2[:, 0:P], ev_b[:, :], ident[:, :]).then_inc(evt_done, 1)

            def embed(b, half):
                if half == 0:
                    pe.wait_ge(evt_copied, b + 1)
                    if not (isinstance(b, int) and b == 0):
                        pe.wait_ge(emb_copied, 2 * b)
                else:
                    pe.wait_ge(emb_copied, 2 * b + 1)
                for j in range(2):
                    mm = pe.matmul(b0[:, j * D:(j + 1) * D], ev_t[:, :], wz[:, 2 * half + j, :], start=True, stop=True)
                mm.then_inc(emb_done, 1)

            def x_transposes(b):
                pe.wait_ge(x1_done, b + 1)
                if not (isinstance(b, int) and b == 0):
                    pe.wait_ge(val_copied, 2 * b)
                for j in range(TILES):
                    pe.transpose(b2[:, j * P:(j + 1) * P], x1[:, j, 0:P], ident[:, :])
                    mm = pe.transpose(b3[0:D1, j * P:(j + 1) * P], x1[:, j, P:D], ident[:, :])
                mm.then_inc(xt_done, 1)

            def score_factor(b, kept):
                pe.wait_ge(xt_copied, b + 1)
                for dst, cols in ((b2, slice(0, P)), (b3, slice(P, D + 1))):
                    m = cols.stop - cols.start
                    pe.matmul(dst[0:m, :], score_w0[:, cols], xt0[:, kept, :], start=True, stop=False)
                    mm = pe.matmul(dst[0:m, :], score_w1[:, cols], xt1[:, kept, :], start=False, stop=True)
                mm.then_inc(tq_done, 1)

            def values(b, kept, half):
                dst = (b2, b3)[half]
                for j in range(2):
                    t = slice((2 * half + j) * P, (2 * half + j + 1) * P)
                    pe.matmul(dst[:, j * D:(j + 1) * D], xt0[:, kept, t], wqkv0[:, 2 * D:3 * D], start=True, stop=False)
                    mm = pe.matmul(dst[:, j * D:(j + 1) * D], xt1[:, kept, t], wqkv1[:, 2 * D:3 * D],
                                   start=False, stop=True)
                mm.then_inc(val_done, 1)

            def scores(b, kept, s):
                i = b * TILES + s
                if s == 0:
                    pe.wait_ge(tq_copied, b + 1)
                if not (isinstance(b, int) and b == 0 and s < 2):
                    pe.wait_ge(exp_done, i - 1)
                t = slice(s * P, (s + 1) * P)
                dst = (b4, b5)[s % 2]
                pe.matmul(dst[:, :], tq0[:, t], xt0[:, kept, :], start=True, stop=False)
                pe.matmul(dst[:, :], tq1[:, t], xt1[:, kept, :], start=False, stop=True).then_inc(score_done, 1)

            def p_transposes(b, s):
                i = b * TILES + s
                pe.wait_ge(exp_done, i + 1)
                if not (isinstance(b, int) and b == 0 and s == 0):
                    pe.wait_ge(pt_copied, i)
                for k in range(TILES):
                    mm = pe.transpose(b6[:, k * P:(k + 1) * P], prob[:, s % 2, k * P:(k + 1) * P], ident[:, :])
                mm.then_inc(pt_done, 1)

            def context(b, s):
                i = b * TILES + s
                if s == 0:
                    pe.wait_ge(val_copied, 2 * b + 2)
                pe.wait_ge(pt_copied, i + 1)
                if not (isinstance(b, int) and b == 0 and s == 0):
                    pe.wait_ge(h2_done, i)
                for k in range(TILES):
                    mm = pe.matmul(b7[:, 0:D], prob_t[:, s % 2, k * P:(k + 1) * P], val[:, k, :],
                                   start=(k == 0), stop=(k == TILES - 1))
                mm.then_inc(pv_done, 1)

            def x2_transposes(b, kept, s):
                pe.wait_ge(x2_done, b * TILES + s + 1)
                if s == 0 and not (isinstance(b, int) and b == 0):
                    pe.wait_ge(logit_copied, b)
                if s == 1 and not (isinstance(b, int) and b == 0):
                    pe.wait_ge(rank_copied, b)
                pe.transpose(b1[:, 0:P], x2[:, kept, s, 0:P], ident[:, :])
                pe.transpose(b1[0:D1, P:2 * P], x2[:, kept, s, P:D], ident[:, :]).then_inc(x2t_done, 1)

            def gate(b, s):
                pe.wait_ge(x2t_copied, b * TILES + s + 1)
                dst = b1[:, 256 + s * E:256 + (s + 1) * E]
                pe.matmul(dst, x2t0[:, :], wg0[:, :], start=True, stop=False)
                pe.matmul(dst, x2t1[:, :], wg1[:, :], start=False, stop=True).then_inc(logit_done, 1)

            def ranks(b):
                pe.wait_ge(mask_done, b + 1)
                pe.matmul(b1[:, 288:288 + E], before[:, :], here_b[:, :], start=True, stop=False)
                pe.matmul(b1[:, 288:288 + E], ones_b[:, :], so_far[:, :], start=False, stop=True).then_inc(rank_done, 1)

            ev_transpose(0)
            embed(0, 0)
            embed(0, 1)
            x_transposes(0)
            score_factor(0, 0)
            scores(0, 0, 0)
            ev_transpose(1)
            embed(1, 0)

            def batch(b, kept, first=False, last=False):
                before_kept, next_kept = (kept - 1) % ROWS_KEPT, (kept + 1) % ROWS_KEPT
                scores(b, kept, 1)
                if not last:
                    embed(b + 1, 1)
                p_transposes(b, 0)
                if not first:
                    x2_transposes(b - 1, before_kept, 2)
                    context(b - 1, 3)
                values(b, kept, 0)
                values(b, kept, 1)
                if not first:
                    gate(b - 1, 2)
                scores(b, kept, 2)
                p_transposes(b, 1)
                if not first:
                    x2_transposes(b - 1, before_kept, 3)
                context(b, 0)
                if not first:
                    gate(b - 1, 3)
                if not last:
                    x_transposes(b + 1)
                scores(b, kept, 3)
                p_transposes(b, 2)
                if not last:
                    score_factor(b + 1, next_kept)
                x2_transposes(b, kept, 0)
                context(b, 1)
                gate(b, 0)
                if not last:
                    scores(b + 1, next_kept, 0)
                if not first:
                    ranks(b - 1)
                if not last:
                    ev_transpose(b + 2)
                p_transposes(b, 3)
                x2_transposes(b, kept, 1)
                if not last:
                    embed(b + 2, 0)
                context(b, 2)
                gate(b, 1)

            batch(0, 0, first=True)
            with pe.Fori(0, (BATCHES - 2) // ROWS_KEPT) as i:
                for k in range(ROWS_KEPT):
                    batch(ROWS_KEPT * i + k + 1, (k + 1) % ROWS_KEPT)
            batch(BATCHES - 1, (BATCHES - 1) % ROWS_KEPT, last=True)
            final, final_kept = BATCHES - 1, (BATCHES - 1) % ROWS_KEPT
            x2_transposes(final, final_kept, 2)
            context(final, 3)
            gate(final, 2)
            x2_transposes(final, final_kept, 3)
            gate(final, 3)
            ranks(final)
            pe.wait_ge(slot_done, BATCHES + 1)
            pe.matmul(b1[:, 304:304 + E], ones_b[:, :], so_far[:, :], start=True, stop=True).then_inc(count_done, 1)

            def block_transposes(m, n, round_of):
                pe.wait_ge(block_in[n], round_of * 16)
                pe.transpose(b0[:, 0:P], xb[:, n, 0:P], ident[:, :])
                pe.transpose(b0[0:D1, P:2 * P], xb[:, n, P:D], ident[:, :]).then_inc(xbt_done, 1)

            def up_proj(m, n):
                pe.wait_ge(xbt_copied, m + 1)
                pe.wait_ge(up0_copied, m + 1)
                pe.wait_ge(up1_copied, m + 1)
                for c in range(HC):
                    dst, cols = (b1, b2)[n % 2][:, c * P:(c + 1) * P], slice(c * P, (c + 1) * P)
                    pe.matmul(dst, up_now0[:, n % 2, cols], xbt0[:, :], start=True, stop=False)
                    mm = pe.matmul(dst, up_now1[:, n % 2, cols], xbt1[:, :], start=False, stop=True)
                mm.then_inc(up_done, 1)

            def down_proj(m, n, e, first):
                pe.wait_ge(gelu_done, m + 1)
                if not (first and n < 2):
                    pe.wait_ge(y_read, m - 1)
                for c in range(HC):
                    mm = pe.matmul((b5, b6)[n % 2][:, 0:D], hid[:, n % 2, c * P:(c + 1) * P],
                                   down[:, bass.ds(e * (HC * D) + c * D, D)], start=(c == 0), stop=(c == HC - 1))
                mm.then_inc(y_mm, 1)

            pe.wait_ge(up_in, 32)
            pe.wait_ge(down_in, 32)
            pe.wait_ge(table_done, 1)
            block_transposes(0, 0, 1)
            up_proj(0, 0)
            block_transposes(1, 1, 1)

            def expert_block(m, n, it, ahead1, ahead2, first):
                e = pe.value_load(t_i[0:1, 0, bass.ds(m, 1)], min_val=0, max_val=E - 1)
                if ahead1:
                    up_proj(m + 1, n + 1)
                if ahead2:
                    block_transposes(m + 2, (n + 2) % UNROLL, it + 1 + (n + 2) // UNROLL)
                down_proj(m, n, e, first)

            rounds = BLOCKS // UNROLL
            for n in range(UNROLL):
                expert_block(n, n, 0, True, True, True)
            with pe.Fori(1, rounds - 1) as it:
                for n in range(UNROLL):
                    expert_block(it * UNROLL + n, n, it, True, True, False)
            for n in range(UNROLL):
                expert_block((rounds - 1) * UNROLL + n, n, rounds - 1, n < UNROLL - 1, n < UNROLL - 2, False)


def kernel(x, L0_tok_quantum_params, L0_tok_post_w, L0_tok_post_b, L0_attn_W_qkv, L0_attn_b_qkv, L0_ffn_Wg,
           L0_ffn_W1, L0_ffn_b1, L0_ffn_W2, L0_ffn_b2):
    import concourse.bacc as bacc
    from concourse.bass_utils import run_bass_kernel_spmd

    x = np.ascontiguousarray(x)
    vocab = L0_tok_quantum_params.shape[0]
    embed = L0_tok_post_w.shape[0]
    experts, _, hidden = L0_ffn_W1.shape
    tiles = x.shape[1] // 128
    emb_w = np.zeros((tiles, 128 // tiles, tiles, embed), np.float32)
    for j in range(tiles):
        emb_w[j, 0:QUBITS, j] = np.asarray(L0_tok_post_w).T
        emb_w[j, QUBITS, j] = L0_tok_post_b
    arrays = {
        "token_ids": x,
        "angles": np.ascontiguousarray(L0_tok_quantum_params).reshape(vocab, ANGLES),
        "emb_w": emb_w.reshape(128, tiles * embed),
        "qkv_w": np.concatenate([L0_attn_W_qkv, np.asarray(L0_attn_b_qkv)[None]], 0),
        "gate_w": np.ascontiguousarray(L0_ffn_Wg),
        "up_w": np.concatenate([L0_ffn_W1, np.asarray(L0_ffn_b1)[:, None]], 1).transpose(1, 0, 2).reshape(
            embed + 1, experts * hidden),
        "down_w": np.asarray(L0_ffn_W2).reshape(experts, hidden // 128, 128, embed).transpose(2, 0, 1, 3).reshape(
            128, experts * hidden // 128 * embed),
        "down_b": np.ascontiguousarray(L0_ffn_b2).reshape(experts * embed),
    }
    nc = bacc.Bacc("TRN2", target_bir_lowering=False, num_devices=1)
    aps = []
    for name in arrays:
        arrays[name] = np.ascontiguousarray(arrays[name])
        aps.append(nc.dram_tensor(name, arrays[name].shape, mybir.dt.from_np(arrays[name].dtype),
                                  kind="ExternalInput").ap())
    out = nc.dram_tensor("out", (x.shape[0], x.shape[1], embed), F32, kind="ExternalOutput").ap()
    build(nc, *aps, out)
    result = run_bass_kernel_spmd(nc, [arrays], core_ids=[0])
    return result.results[0]["out"]
```

```python
import itertools
import math
from contextlib import ExitStack

import numpy as np
import concourse.bass as bass
from concourse import mybir

ALU = mybir.AluOpType
ACT = mybir.ActivationFunctionType
AX = mybir.AxisListType
F32 = mybir.dt.float32
I32 = mybir.dt.int32
U32 = mybir.dt.uint32
BF16 = mybir.dt.bfloat16

QUBITS = 6
LAYERS = 3
ANGLES = LAYERS * QUBITS * 2
EPS = 1e-5
ROUNDER = 1.5 * 2.0 ** 23
TWO_PI_HIGH = 6.28125
TWO_PI_LOW = 2 * math.pi - TWO_PI_HIGH
PI_BELOW = 3.1415925
HALF_PI_READY = 2
REDUCED = 6
TABLES_READY = 20
CIRCUIT_STEPS = 116
X_DONE = 52
CHAIN = 43


Z_SUPPORT = [list(range(1, QUBITS))] + [list(range(q + 1)) for q in range(1, QUBITS)]
X_SUPPORT = [[q, q + 1] for q in range(QUBITS - 1)] + [[QUBITS - 1, 0, 1]]
PAULI_CODE = {"I": 0, "Z": 1, "X": 2, "Y": 3}


def pauli_string(choice):
    x_all, z_all, phase = 0, 0, 0
    for j, name in choice:
        x = sum(1 << k for k in X_SUPPORT[j]) if name in "XY" else 0
        z = sum(1 << k for k in Z_SUPPORT[j]) if name in "ZY" else 0
        phase += (name == "Y") + 2 * bin(z_all & x).count("1")
        x_all, z_all = x_all ^ x, z_all ^ z
    names = ""
    for k in range(QUBITS):
        xk, zk = x_all >> k & 1, z_all >> k & 1
        names += "IXZY"[xk + 2 * zk]
        phase -= xk and zk
    assert phase % 2 == 0
    return names, 1 - phase % 4


def table_place(choice):
    names, sign = pauli_string(choice)
    low = sum(PAULI_CODE[names[k]] * 4 ** k for k in range(3))
    high = sum(PAULI_CODE[names[3 + k]] * 4 ** k for k in range(3))
    return low + (0 if sign > 0 else 64), high


def boxes(shape, place, most=3):
    left = set(itertools.product(*[range(s) for s in shape]))
    kinds = []
    for k in range(most, -1, -1):
        for dims in itertools.combinations(range(len(shape)), k):
            runs = [[(s, n, t) for t in (1, 2) for s in range(shape[d]) for n in range(shape[d], 1, -1)
                     if s + (n - 1) * t < shape[d]] for d in dims]
            for run in itertools.product(*runs):
                kinds.append((int(np.prod([n for _, n, _ in run])), dims, run))
    kinds.sort(key=lambda kind: -kind[0])
    found = []
    for size, dims, run in kinds:
        for base in sorted(left):
            if base not in left or any(base[d] != r[0] for d, r in zip(dims, run)):
                continue
            points = {}
            for step in itertools.product(*[range(r[1]) for r in run]):
                p = list(base)
                for d, r, o in zip(dims, run, step):
                    p[d] += r[2] * o
                points[step] = tuple(p)
            if not all(p in left for p in points.values()):
                continue
            origin = place(base)
            units = [tuple(int(j == i) for j in range(len(dims))) for i in range(len(dims))]
            slope = [tuple(a - b for a, b in zip(place(points[u]), origin)) for u in units]
            if all(place(p) == tuple(origin[h] + sum(o * s[h] for o, s in zip(step, slope)) for h in (0, 1))
                   for step, p in points.items()):
                found.append((base, [(d, r[1], r[2]) for d, r in zip(dims, run)], origin, slope))
                left -= set(points.values())
    assert not left
    return found


Z_BLOCK, at = {}, 0
for _q in list(range(1, QUBITS)) + [0]:
    Z_BLOCK[_q] = at
    at += 2 ** len(Z_SUPPORT[_q])
Z_STRINGS = at
PAIRS = QUBITS - 1
X_STRINGS = 9 * PAIRS + 27


def gather_products(eng, out, tables, n, shape, names, support, base, strides, log):
    def place(index):
        return table_place([(j, names[i]) for j, i in zip(support, index)])

    for first, dims, (low, high), slope in boxes(shape, place):
        at = base + sum(i * s for i, s in zip(first, strides))
        part_out, part_tab = out.ap[0][0], tables.ap[0][0]
        run = [(strides[d] * step, count) for d, count, step in dims]
        o = bass.AP(out.tensor, out.offset + at * n, [[part_out, 128]] + [[s * n, c] for s, c in run] + [[1, n]])
        a = bass.AP(tables.tensor, tables.offset + low * n,
                    [[part_tab, 128]] + [[s[0] * n, c] for s, (_, c) in zip(slope, run)] + [[1, n]])
        b = bass.AP(tables.tensor, tables.offset + (128 + high) * n,
                    [[part_tab, 128]] + [[s[1] * n, c] for s, (_, c) in zip(slope, run)] + [[1, n]])
        log(eng.tensor_tensor(o, a, b, ALU.mult))


def build(nc, token_ids, angles, emb_w, emb_rows, qkv_w, gate_w, up_w, down_w, down_b, out):
    P = 128
    TOKENS = token_ids.shape[0] * token_ids.shape[1]
    BATCHES, SEQ = token_ids.shape
    D = qkv_w.shape[1] // 3
    D0, D1 = P, D - P
    K1 = D1 + 1
    TILES = SEQ // P
    T = TOKENS // P
    E = gate_w.shape[1]
    HID = up_w.shape[1] // E
    HC = HID // P
    SCALE = 1.0 / math.sqrt(D)
    REGION = TOKENS + P
    PAD_ROW = E * REGION
    WIDTH = D + 5
    NO_TOKEN = 1.0e6
    UNROLL = 4
    AHEAD = 3
    KEPT = 2
    CHUNKS = 2
    CT = T // CHUNKS
    GATHERED_LATE = 6
    BLOCKS = -(-(2 * TOKENS // P + E - 1) // UNROLL) * UNROLL
    FEATURES = QUBITS + 2
    EV_STRIDE = P // TILES

    routed = nc.dram_tensor("routed", (PAD_ROW + P, WIDTH), F32, kind="Internal").ap()
    ids_view = token_ids.rearrange("b (p j) -> p b j", j=TILES)
    out_rows = out.rearrange("b s d -> (b s) d")
    out_view = out.rearrange("b (p j) d -> b p (j d)", j=TILES)

    ctx = ExitStack()
    with ctx:
        def sb(name, shape, dt=F32):
            return ctx.enter_context(nc.sbuf_tensor(name, shape, dt))

        def bank(name):
            return ctx.enter_context(nc.psum_tensor(name, [P, 512], F32))

        def sem(name):
            return ctx.enter_context(nc.semaphore(name))

        ids = sb("ids", [P, BATCHES, TILES], I32)
        theta_all = sb("theta_all", [P, T, ANGLES])
        angle_stages = sb("angle_stages", [P, 3, CT, ANGLES])
        turns, turned, folded = [angle_stages[:, i] for i in range(3)]
        sine = sb("sine", [P, ANGLES, CT])
        cosine = sb("cosine", [P, ANGLES, CT])
        half_pi = sb("half_pi", [P, 1])
        bloch = sb("bloch", [P, QUBITS, 4, CT])
        pair = sb("pair", [P, 2, 16, CT])
        string_stages = sb("string_stages", [P, 192 + 2 * Z_STRINGS, CT])
        tables = string_stages[:, 0:192]
        z_coef = string_stages[:, 192:192 + Z_STRINGS]
        z_str = string_stages[:, 192 + Z_STRINGS:192 + 2 * Z_STRINGS]
        ry = sb("ry", [P, QUBITS, 2, CT])
        rzy = sb("rzy", [P, QUBITS, 3, CT])
        z_part = sb("z_part", [P, 28, CT])
        x_str = sb("x_str", [P, X_STRINGS, CT])
        x_sum = sb("x_sum", [P, X_STRINGS // 3, CT])
        x_sum2 = sb("x_sum2", [P, X_STRINGS // 9, CT])
        z_exp = sb("z_exp", [P, QUBITS, CT])
        x_exp = sb("x_exp", [P, QUBITS, CT])
        ev = sb("ev", [P, T + TILES, EV_STRIDE])
        ident = sb("ident", [P, P])
        ones = sb("ones", [P, P])
        before_f = sb("before_f", [P, P])
        before = sb("before", [P, P], BF16)
        ones_b = sb("ones_b", [P, P], BF16)
        minus_half = sb("minus_half", [P, TILES])
        tok_i = sb("tok_i", [P, T], I32)
        tok = sb("tok", [P, T])
        blk_i = sb("blk_i", [P, BLOCKS], I32)
        blk = sb("blk", [P, BLOCKS])
        exp_i = sb("exp_i", [P, E], I32)
        exp_f = sb("exp_f", [P, E])
        region_f = sb("region_f", [P, E])
        pad_rows = sb("pad_rows", [P, WIDTH])
        wz = sb("wz", [P, TILES, D])
        wqkv0 = sb("wqkv0", [P, 3 * D])
        wqkv1 = sb("wqkv1", [K1, 3 * D])
        wg0 = sb("wg0", [P, E])
        wg1 = sb("wg1", [D1, E])
        gelu_ahead = sb("gelu_ahead", [P, 1])
        lift = sb("lift", [P, D + 1])
        lift_sum = sb("lift_sum", [P, 1])
        lift_mean = sb("lift_mean", [P, 1])
        lift_t0 = sb("lift_t0", [P, P])
        lift_t1 = sb("lift_t1", [K1, P])
        lifted_qk0 = sb("lifted_qk0", [P, 2, P])
        lifted_qk1 = sb("lifted_qk1", [D1, 2, P])
        lifted_v = sb("lifted_v", [P, D])
        score_w = sb("score_w", [P, P])
        up0 = sb("up0", [P, E * HID])
        up1 = sb("up1", [K1, E * HID])
        string_room = [string_stages[:, :, :].rearrange("p k t -> p (k t)"), 0]
        angle_room = [angle_stages[:, :, :, :].rearrange("p a t f -> p (a t f)"), 0]

        def behind(room, pattern, **sizes):
            size = int(np.prod(list(sizes.values())))
            room[1] += size
            return room[0][:, room[1] - size:room[1]].rearrange(pattern, **sizes)

        down = behind(string_room, "p (k d) -> p (k d)", k=E * HC, d=D)
        down_bias = behind(string_room, "p (e d) -> p (e d)", e=E, d=D)
        hres = sb("hres", [P, T + TILES // 2, D])
        ev_b = sb("ev_b", [P, P])
        ev_t = sb("ev_t", [P, P])
        bn1 = sb("bn1", [P, TILES, 6])
        mv1 = sb("mv1", [P, TILES, 2])
        ve1 = sb("ve1", [P, TILES])
        rs1 = sb("rs1", [P, TILES])
        u_b = sb("u_b", [P, TILES, EV_STRIDE])
        ut = sb("ut", [P, KEPT, SEQ])
        tq = sb("tq", [P, SEQ])
        val = sb("val", [P, TILES, D])
        nmax = sb("nmax", [P, 2])
        rsum = sb("rsum", [P, TILES])
        rinv = sb("rinv", [P, TILES])
        prob = sb("prob", [P, 2, SEQ])
        prob_t = sb("prob_t", [P, 2, SEQ])
        bn2 = sb("bn2", [P, 2, 6])
        mv2 = sb("mv2", [P, 2, 2])
        ve2 = sb("ve2", [P, 2])
        rs2 = sb("rs2", [P, 2])
        x2 = sb("x2", [P, KEPT, TILES, WIDTH])
        x2t0 = sb("x2t0", [P, P])
        x2t1 = sb("x2t1", [D1, P])
        logit = sb("logit", [P, TILES, E])
        top = sb("top", [P, TILES, E])
        top_i = sb("top_i", [P, TILES, E], U32)
        gap = sb("gap", [P, TILES])
        gap_e = sb("gap_e", [P, TILES])
        gap_1 = sb("gap_1", [P, TILES])
        mask = sb("mask", [P, 2, TILES, E])
        both = sb("both", [P, TILES, E])
        ahead = sb("ahead", [P, TILES, E])
        here = sb("here", [P, E])
        here_b = sb("here_b", [P, E], BF16)
        so_far = sb("so_far", [P, E], BF16)
        rank = sb("rank", [P, E])
        place = sb("place", [P, TILES, E])
        slot_e = sb("slot_e", [P, 2, TILES, E])
        slot_f = sb("slot_f", [P, 2, TILES])
        slot = sb("slot", [P, KEPT, 2, TILES], I32)
        count = sb("count", [P, E])
        count_i = sb("count_i", [P, E], I32)
        nblk_i = sb("nblk_i", [P, E], I32)
        nblk = sb("nblk", [P, E])
        cum = sb("cum", [P, 2, E])
        skip = sb("skip", [P, E])
        ge = behind(angle_room, "p (e m) -> p e m", e=E, m=BLOCKS)
        ge_w = behind(angle_room, "p (e m) -> p e m", e=E - 1, m=BLOCKS)
        t_exp = sb("t_exp", [P, BLOCKS])
        t_row = sb("t_row", [P, BLOCKS])
        t_first = sb("t_first", [P, BLOCKS])
        t_i = sb("t_i", [P, 4, BLOCKS], I32)
        t_pair = sb("t_pair", [P, BLOCKS])
        xb = behind(string_room, "p (n d) -> p n d", n=UNROLL, d=WIDTH)
        xbt0 = sb("xbt0", [P, 2, P])
        xbt1 = sb("xbt1", [K1, 2, P])
        hid = behind(string_room, "p (n h) -> p n h", n=2, h=HID)
        up_now0 = sb("up_now0", [P, UNROLL, HID])
        up_now1 = sb("up_now1", [K1, UNROLL, HID])
        share = sb("share", [P, UNROLL])
        share_w = sb("share_w", [P, UNROLL, 2])
        dest = sb("dest", [P, UNROLL], I32)
        y_raw = sb("y_raw", [P, 2, D])
        y = sb("y", [P, UNROLL, D])

        b0, b1, b2, b3, b4, b5, b6, b7 = [bank(f"bank{i}") for i in range(8)]

        ids_in = sem("ids_in")
        angles_in = [sem(f"angles_in{c}") for c in range(CHUNKS)]
        small_in = sem("small_in")
        up_in = sem("up_in")
        down_in = sem("down_in")
        pads_done = sem("pads_done")
        const_done = sem("const_done")
        dve_step = sem("dve_step")
        circuit_step = sem("circuit_step")
        ident_done = sem("ident_done")
        trig_done = sem("trig_done")
        x_step = sem("x_step")
        pool_step = sem("pool_step")
        lift_done = sem("lift_done")
        centered = sem("centered")
        lift_copied = sem("lift_copied")
        lifted_done = sem("lifted_done")
        ev_done = sem("ev_done")
        ev_copied = sem("ev_copied")
        evt_done = sem("evt_done")
        evt_copied = sem("evt_copied")
        emb_done = sem("emb_done")
        emb_copied = sem("emb_copied")
        var1_done = sem("var1_done")
        u_done = sem("u_done")
        rs1_done = sem("rs1_done")
        rs2_done = sem("rs2_done")
        ut_done = sem("ut_done")
        ut_copied = sem("ut_copied")
        tq_done = sem("tq_done")
        tq_copied = sem("tq_copied")
        val_done = sem("val_done")
        val_copied = sem("val_copied")
        score_done = sem("score_done")
        max_done = sem("max_done")
        exp_done = sem("exp_done")
        pt_done = sem("pt_done")
        pt_copied = sem("pt_copied")
        pv_done = sem("pv_done")
        h2_done = sem("h2_done")
        var2_done = sem("var2_done")
        x2_done = sem("x2_done")
        x2t_done = sem("x2t_done")
        x2t_copied = sem("x2t_copied")
        logit_done = sem("logit_done")
        logit_copied = sem("logit_copied")
        gap_done = sem("gap_done")
        gap_exp = sem("gap_exp")
        mask_done = sem("mask_done")
        rank_done = sem("rank_done")
        rank_copied = sem("rank_copied")
        slot_done = sem("slot_done")
        scattered = sem("scattered")
        h2_out = sem("h2_out")
        count_done = sem("count_done")
        count_copied = sem("count_copied")
        table_done = sem("table_done")
        pads_out = sem("pads_out")
        block_in = [sem(f"block_in{i}") for i in range(UNROLL)]
        xbt_done = sem("xbt_done")
        xbt_copied = sem("xbt_copied")
        up_done = sem("up_done")
        gelu_done = sem("gelu_done")
        up0_copied = sem("up0_copied")
        up1_copied = sem("up1_copied")
        share_done = sem("share_done")
        y_mm = sem("y_mm")
        y_read = sem("y_read")
        y_done = sem("y_done")
        added = [sem(f"added{i}") for i in range(UNROLL)]
        passed = sem("passed")

        def emb_bank(b, half):
            return b1 if isinstance(b, int) and b == 0 and half == 1 else b0

        def hold(eng):
            eng.sem_inc(passed, 1)

        block = ctx.enter_context(nc.Block())

        @block.sync
        def _(sp):
            sp.dma_start(ids[:, :, :], ids_view).then_inc(ids_in, 16)
            sp.dma_start(lift[:, :], emb_rows).then_inc(small_in, 16)
            sp.dma_start(wqkv0[:, :], qkv_w[0:P, :]).then_inc(small_in, 16)
            sp.dma_start(wqkv1[:, :], qkv_w[P:D + 1, :]).then_inc(small_in, 16)
            sp.dma_start(wz[:, :, :], emb_w.rearrange("p (j d) -> p j d", j=TILES)).then_inc(small_in, 16)
            sp.dma_start(wg0[:, :], gate_w[0:P, :]).then_inc(small_in, 16)
            sp.dma_start(wg1[:, :], gate_w[P:D, :]).then_inc(small_in, 16)
            sp.dma_start(up0[:, :], up_w[0:P, :]).then_inc(up_in, 16)
            sp.dma_start(up1[:, :], up_w[P:D + 1, :]).then_inc(up_in, 16)
            sp.wait_ge(pads_done, 1)
            sp.dma_start(routed[PAD_ROW:PAD_ROW + P, :], pad_rows[:, :]).then_inc(pads_out, 16)
            def rows_out(b):
                sp.dma_start(out_view[bass.ds(b, 1)].rearrange("o p f -> (o p) f"),
                             hres[:, bass.ds(b * TILES, TILES), :].rearrange("p j d -> p (j d)")).then_inc(h2_out, 16)

            sp.wait_ge(h2_done, TILES)
            rows_out(0)
            sp.wait_ge(ev_done, CHUNKS)
            sp.dma_start(down_bias, down_b.partition_broadcast(P)).then_inc(down_in, 16)
            share_cols = E * HC * D // (BATCHES - 2)
            with sp.Fori(0, BATCHES - 2) as i:
                sp.wait_ge(h2_done, i * TILES + 2 * TILES + TILES // 2)
                rows_out(i + 1)
                sp.dma_start(down[:, bass.ds(i * share_cols, share_cols)], down_w[:, bass.ds(i * share_cols, share_cols)]
                             ).then_inc(down_in, 16)
            sp.wait_ge(h2_done, T)
            rows_out(BATCHES - 1)
            sp.wait_ge(count_copied, 2)
            for e in range(E):
                rows = sp.value_load(count_i[0:1, e:e + 1], min_val=0, max_val=TOKENS)
                sp.dma_start(routed[bass.ds(rows + e * REGION, P), :], pad_rows[:, :]).then_inc(pads_out, 16)
            sp.wait_ge(pads_out, 16 * E + 16)
            sp.wait_ge(scattered, 16 * 2 * T)
            sp.wait_ge(table_done, 1)
            for n in range(UNROLL):
                row = sp.value_load(t_i[0:1, 1, n:n + 1], min_val=0, max_val=PAD_ROW)
                sp.dma_start(xb[:, n, :], routed[bass.ds(row, P), :]).then_inc(block_in[n], 16)
            with sp.Fori(0, BLOCKS // UNROLL - 1) as it:
                for n in range(UNROLL):
                    row = sp.value_load(t_i[0:1, 1, bass.ds((it + 1) * UNROLL + n, 1)], min_val=0, max_val=PAD_ROW)
                    sp.wait_ge(xbt_done, it * UNROLL + n + 1)
                    sp.wait_ge(share_done, (it * UNROLL + n) * 2 + 2)
                    sp.dma_start(xb[:, n, :], routed[bass.ds(row, P), :]).then_inc(block_in[n], 16)
            sp.wait_ge(h2_out, 16 * BATCHES)
            for n in range(UNROLL):
                sp.wait_ge(added[n], 16 * (BLOCKS // UNROLL) + 16)

        @block.gpsimd
        def _(pool):
            steps = [0]

            def step(instruction):
                steps[0] += 1
                instruction.then_inc(pool_step, 1)

            def join():
                pool.wait_ge(pool_step, steps[0])

            step(pool.memset(pad_rows[:, :], 0.0))
            join()
            pool.memset(pad_rows[:, WIDTH - 1:WIDTH], NO_TOKEN).then_inc(pads_done, 1)
            step(pool.memset(ident[:, :], 0.0))
            join()
            pool.affine_select(out=ident[:, :], in_=ident[:, :], compare_op=ALU.not_equal, fill=1.0, base=0,
                               pattern=[[-1, P]], channel_multiplier=1).then_inc(ident_done, 1)

            def gather_angles(first, last):
                for t in range(first, last):
                    b, j = divmod(t, TILES)
                    pool.indirect_dma_start(out=theta_all[:, t, :], out_offset=None, in_=angles,
                                            in_offset=bass.IndirectOffsetOnAxis(ids[:, b, j:j + 1], 0)
                                            ).then_inc(angles_in[t // CT], 16)

            pool.wait_ge(ids_in, 16)
            gather_angles(0, CT)
            step(pool.memset(ones[:, :], 1.0))
            step(pool.memset(minus_half[:, :], -0.5))
            step(pool.memset(ones_b[:, :], 1.0))
            step(pool.memset(so_far[:, :], 0.0))
            step(pool.iota(tok_i[:, :], [[SEQ, BATCHES], [1, TILES]], base=0, channel_multiplier=TILES))
            step(pool.iota(blk_i[:, :], [[1, BLOCKS]], base=0, channel_multiplier=0))
            step(pool.iota(exp_i[:, :], [[1, E]], base=0, channel_multiplier=0))
            join()
            step(pool.affine_select(out=before_f[:, :], in_=ones[:, :], compare_op=ALU.is_gt, fill=0.0, base=0,
                                    pattern=[[1, P]], channel_multiplier=-1))
            step(pool.tensor_copy(tok[:, :], tok_i[:, :]))
            step(pool.tensor_copy(blk[:, :], blk_i[:, :]))
            step(pool.tensor_copy(exp_f[:, :], exp_i[:, :]))
            join()
            step(pool.tensor_copy(before[:, :], before_f[:, :]))
            join()
            pool.tensor_scalar(region_f[:, :], exp_f[:, :], float(REGION), None, ALU.mult).then_inc(const_done, 1)

            xsteps = [0]

            def xstep(instruction):
                xsteps[0] += 1
                instruction.then_inc(x_step, 1)

            def xjoin():
                pool.wait_ge(x_step, xsteps[0])

            def x_strings_low(c):
                pool.wait_ge(circuit_step, c * CIRCUIT_STEPS + TABLES_READY)
                for q in range(PAIRS // 2):
                    gather_products(pool, x_str[:, :, :], tables, CT, [3, 3], "XYZ", X_SUPPORT[q], 9 * q,
                                    [3, 1], xstep)

            def x_strings_high(c):
                for q in range(PAIRS // 2, PAIRS):
                    gather_products(pool, x_str[:, :, :], tables, CT, [3, 3], "XYZ", X_SUPPORT[q], 9 * q,
                                    [3, 1], xstep)

            def x_strings_last(c):
                gather_products(pool, x_str[:, :, :], tables, CT, [3, 3, 3], "XYZ", X_SUPPORT[PAIRS],
                                9 * PAIRS, [9, 3, 1], xstep)

            def x_weights(c):
                xjoin()
                pairs = x_str[:, 0:9 * PAIRS].rearrange("p (q a b) t -> p q a b t", q=PAIRS, a=3)
                for q in range(PAIRS):
                    xstep(pool.tensor_tensor(pairs[:, q], pairs[:, q],
                                             rzy[:, q + 1].unsqueeze(1).to_broadcast([P, 3, 3, CT]), ALU.mult))
                triple = x_str[:, 9 * PAIRS:X_STRINGS].rearrange("p (a b) t -> p a b t", b=3)
                xstep(pool.tensor_tensor(triple, triple, rzy[:, 1].unsqueeze(1).to_broadcast([P, 9, 3, CT]), ALU.mult))
                xjoin()
                by3 = x_str[:, :, :].rearrange("p (a b) t -> p a b t", b=3)
                xstep(pool.tensor_tensor(x_sum[:, :, :], by3[:, :, 0], by3[:, :, 1], ALU.add))
                xjoin()
                xstep(pool.tensor_tensor(x_sum[:, :, :], x_sum[:, :, :], by3[:, :, 2], ALU.add))

            def x_sums(c):
                xjoin()
                xstep(pool.tensor_tensor(x_sum[:, 0:3 * PAIRS], x_sum[:, 0:3 * PAIRS],
                                         rzy[:, 0:PAIRS].rearrange("p q a t -> p (q a) t"), ALU.mult))
                triple2 = x_sum[:, 3 * PAIRS:].rearrange("p (a b) t -> p a b t", b=3)
                xstep(pool.tensor_tensor(triple2, triple2, rzy[:, 0].unsqueeze(1).to_broadcast([P, 3, 3, CT]), ALU.mult))
                xjoin()
                sum_by3 = x_sum[:, :, :].rearrange("p (a b) t -> p a b t", b=3)
                xstep(pool.tensor_tensor(x_sum2[:, :, :], sum_by3[:, :, 0], sum_by3[:, :, 1], ALU.add))
                xjoin()
                xstep(pool.tensor_tensor(x_sum2[:, :, :], x_sum2[:, :, :], sum_by3[:, :, 2], ALU.add))
                xjoin()
                xstep(pool.tensor_copy(x_exp[:, 0:PAIRS], x_sum2[:, 0:PAIRS]))
                xstep(pool.tensor_tensor(x_sum2[:, PAIRS:], x_sum2[:, PAIRS:], rzy[:, PAIRS], ALU.mult))
                xjoin()
                xstep(pool.tensor_tensor(x_exp[:, PAIRS], x_sum2[:, PAIRS], x_sum2[:, PAIRS + 1], ALU.add))
                xjoin()
                xstep(pool.tensor_tensor(x_exp[:, PAIRS], x_exp[:, PAIRS], x_sum2[:, PAIRS + 2], ALU.add))
                assert xsteps[0] == (c + 1) * X_DONE, xsteps

            gather_angles(CT, T - GATHERED_LATE)
            for part in (x_strings_low, x_strings_high, x_strings_last, x_weights, x_sums):
                part(0)

            def copy_ev(b):
                if isinstance(b, int) and b % (BATCHES // CHUNKS) == 0:
                    pool.wait_ge(ev_done, b // (BATCHES // CHUNKS) + 1)
                if not (isinstance(b, int) and b == 0):
                    pool.wait_ge(evt_done, b)
                pool.tensor_copy(ev_b[:, :], ev[:, bass.ds(b * TILES, TILES), :].rearrange("p j e -> p (j e)")
                                 ).then_inc(ev_copied, 1)

            def rstd1(b):
                pool.wait_ge(var1_done, b + 1)
                pool.tensor_tensor(rs1[:, :], ve1[:, :], minus_half[:, :], ALU.pow).then_inc(rs1_done, 1)

            def rstd2(b, s):
                pool.wait_ge(var2_done, b * TILES + s + 1)
                pool.tensor_tensor(rs2[:, s % 2:s % 2 + 1], ve2[:, s % 2:s % 2 + 1], minus_half[:, 0:1], ALU.pow
                                   ).then_inc(rs2_done, 1)

            def scatter(b, kept, j):
                if j == 0:
                    pool.wait_ge(slot_done, b + 1)
                    hold(pool)
                for k in range(2):
                    pool.indirect_dma_start(out=routed, out_offset=bass.IndirectOffsetOnAxis(
                        slot[:, kept, k, j:j + 1], 0), in_=x2[:, kept, j, :], in_offset=None).then_inc(scattered, 16)

            def add_nothing(c):
                step(pool.memset(dest[:, :], TOKENS))
                step(pool.memset(y[:, :, :], 0.0))
                join()
                for n in range(UNROLL):
                    pool.indirect_dma_start(out=out_rows, out_offset=bass.IndirectOffsetOnAxis(dest[:, n:n + 1], 0),
                                            in_=y[:, n, :], in_offset=None, bounds_check=TOKENS - 1,
                                            oob_is_err=False, compute_op=ALU.add).then_inc(added[n], 16)

            copy_ev(0)
            gather_angles(T - GATHERED_LATE, T - GATHERED_LATE // 2)
            rstd1(0)
            copy_ev(1)
            gather_angles(T - GATHERED_LATE // 2, T)

            def batch(b, kept, first=False, routed_before=True, last=False, parts=((), (), (), ())):
                if not last:
                    rstd1(b + 1)
                if not first:
                    rstd2(b - 1, 3)
                if routed_before:
                    scatter(b - 2, kept, 2)
                    scatter(b - 2, kept, 3)
                for part in parts[0]:
                    part(1)
                rstd2(b, 0)
                if not last:
                    copy_ev(b + 2)
                for part in parts[1]:
                    part(1)
                rstd2(b, 1)
                for part in parts[2]:
                    part(1)
                rstd2(b, 2)
                for part in parts[3]:
                    part(1)
                if not first:
                    scatter(b - 1, 1 - kept, 0)
                    scatter(b - 1, 1 - kept, 1)

            batch(0, 0, first=True, routed_before=False,
                  parts=((), (x_strings_low,), (x_strings_high,), (x_strings_last,)))
            batch(1, 1, routed_before=False, parts=((x_weights,), (x_sums,), (), ()))
            batch(2, 0, parts=((), (), (add_nothing,), ()))
            with pool.Fori(0, (BATCHES - 4) // KEPT) as i:
                for k in range(KEPT):
                    batch(KEPT * i + k + 3, (k + 3) % KEPT)
            batch(BATCHES - 1, (BATCHES - 1) % KEPT, last=True)
            rstd2(BATCHES - 1, 3)
            scatter(BATCHES - 2, (BATCHES - 2) % KEPT, 2)
            scatter(BATCHES - 2, (BATCHES - 2) % KEPT, 3)
            for j in range(TILES):
                scatter(BATCHES - 1, (BATCHES - 1) % KEPT, j)

            pool.wait_ge(h2_out, 16 * BATCHES)
            pool.wait_ge(table_done, 1)
            with pool.Fori(0, BLOCKS // UNROLL) as it:
                for n in range(UNROLL):
                    m = it * UNROLL + n
                    first_of_expert = pool.value_load(t_i[0:1, 2, bass.ds(m, 1)], min_val=0, max_val=BLOCKS)
                    pool.wait_ge(y_done, m + 1)
                    for k in range(UNROLL):
                        pool.wait_ge(added[k], (first_of_expert + (UNROLL - 1 - k)) // UNROLL * 16 + 16)
                    hold(pool)
                    pool.indirect_dma_start(out=out_rows, out_offset=bass.IndirectOffsetOnAxis(dest[:, n:n + 1], 0),
                                            in_=y[:, n, :], in_offset=None, bounds_check=TOKENS - 1,
                                            oob_is_err=False, compute_op=ALU.add).then_inc(added[n], 16)

        @block.vector
        def _(dve):
            steps = [0]

            def step(instruction):
                steps[0] += 1
                instruction.then_inc(dve_step, 1)

            def join():
                dve.wait_ge(dve_step, steps[0])

            dve.memset(xbt1[D1:K1, :, :], 1.0)
            step(dve.memset(ev[:, :, :], 0.0))
            step(dve.memset(half_pi[:, :], math.pi / 2))
            step(dve.memset(bloch[:, :, 0, :], 1.0))
            step(dve.memset(ahead[:, 0, :], 0.0))
            join()
            step(dve.memset(ev[:, :, QUBITS:QUBITS + 1], 1.0))

            step(dve.memset(ut[:, :, :], 0.0))
            step(dve.memset(u_b[:, :, :], 0.0))
            join()
            step(dve.memset(u_b[:, :, FEATURES - 1:FEATURES], 1.0))
            dve.wait_ge(small_in, 16 * 6)
            step(dve.tensor_reduce(lift_sum[:, :], lift[:, 0:D], AX.X, ALU.add))
            join()
            step(dve.tensor_scalar(lift_mean[:, :], lift_sum[:, :], 1.0 / D, None, ALU.mult))
            join()
            dve.tensor_scalar(lift[:, 0:D], lift[:, 0:D], lift_mean[:, 0:1], None, ALU.subtract).then_inc(centered, 1)
            dve.wait_ge(lift_done, 1)
            dve.tensor_copy(lift_t0[:, :], b4[:, 0:P])
            dve.tensor_copy(lift_t1[:, :], b4[0:K1, P:2 * P]).then_inc(lift_copied, 1)
            dve.wait_ge(lifted_done, 1)
            dve.tensor_copy(lifted_v[:, :], b5[:, 0:D])
            for i, src in enumerate((b6, b7)):
                dve.tensor_copy(lifted_qk0[:, i, :], src[:, 0:P])
                copied = dve.tensor_copy(lifted_qk1[:, i, :], src[0:D1, P:2 * P])
            copied.then_inc(lift_copied, 1)
            dve.wait_ge(lifted_done, 2)
            dve.tensor_scalar(score_w[:, :], b4[:, 0:P], SCALE, None, ALU.mult).then_inc(lift_copied, 1)

            csteps = [0]

            def cstep(instruction):
                csteps[0] += 1
                instruction.then_inc(circuit_step, 1)

            def cjoin():
                dve.wait_ge(circuit_step, csteps[0])

            def sin_of(layer, gate):
                first = (layer * QUBITS * 2) + gate
                return sine[:, first:first + 2 * QUBITS - 1:2, :]

            def cos_of(layer, gate):
                first = (layer * QUBITS * 2) + gate
                return cosine[:, first:first + 2 * QUBITS - 1:2, :]

            def reduce_angles(c):
                theta = theta_all[:, c * CT:(c + 1) * CT, :]
                dve.wait_ge(angles_in[c], 16 * CT)
                cstep(dve.tensor_scalar(turns, theta, 1 / (2 * math.pi), ROUNDER, ALU.mult, ALU.add))
                cjoin()
                cstep(dve.tensor_scalar(turned, turns, ROUNDER, TWO_PI_HIGH, ALU.subtract, ALU.mult))
                cstep(dve.tensor_scalar(folded, turns, ROUNDER, TWO_PI_LOW, ALU.subtract, ALU.mult))
                cjoin()
                cstep(dve.tensor_tensor(theta, theta, turned, ALU.subtract))
                cjoin()
                cstep(dve.tensor_tensor(theta, theta, folded, ALU.subtract))
                cjoin()
                cstep(dve.tensor_scalar(turned, theta, PI_BELOW, -PI_BELOW, ALU.min, ALU.max))
                cjoin()
                assert csteps[0] == c * CIRCUIT_STEPS + REDUCED
                cstep(dve.scalar_tensor_tensor(folded, turned, -1.0, turned, ALU.mult, ALU.max))

            def rotations(c):
                dve.wait_ge(trig_done, 2 * c + 2)
                cstep(dve.tensor_copy(bloch[:, :, 1, :], cos_of(0, 0)))
                cstep(dve.tensor_tensor(bloch[:, :, 2, :], sin_of(0, 0), cos_of(0, 1), ALU.mult))
                cstep(dve.tensor_tensor(bloch[:, :, 3, :], sin_of(0, 0), sin_of(0, 1), ALU.mult))
                cstep(dve.tensor_copy(ry[:, :, 0, :], cos_of(1, 0)))
                cstep(dve.tensor_scalar(ry[:, :, 1, :], sin_of(1, 0), -1.0, None, ALU.mult))
                cstep(dve.tensor_tensor(rzy[:, :, 0, :], cos_of(1, 1), cos_of(1, 0), ALU.mult))
                cstep(dve.tensor_scalar(rzy[:, :, 1, :], sin_of(1, 1), -1.0, None, ALU.mult))
                cstep(dve.tensor_tensor(rzy[:, :, 2, :], cos_of(1, 1), sin_of(1, 0), ALU.mult))

            def bloch_tables(c):
                cjoin()
                for h in range(2):
                    cstep(dve.tensor_tensor(pair[:, h].rearrange("p (a b) t -> p a b t", a=4),
                                            bloch[:, 3 * h + 1].unsqueeze(2).to_broadcast([P, 4, 4, CT]),
                                            bloch[:, 3 * h].unsqueeze(1).to_broadcast([P, 4, 4, CT]), ALU.mult))
                cjoin()
                for h, at in ((0, 0), (1, 128)):
                    cstep(dve.tensor_tensor(tables[:, at:at + 64].rearrange("p (a b) t -> p a b t", a=4),
                                            bloch[:, 3 * h + 2].unsqueeze(2).to_broadcast([P, 4, 16, CT]),
                                            pair[:, h].unsqueeze(1).to_broadcast([P, 4, 16, CT]), ALU.mult))
                cjoin()
                cstep(dve.tensor_scalar(tables[:, 64:128], tables[:, 0:64], -1.0, None, ALU.mult))
                assert csteps[0] == c * CIRCUIT_STEPS + TABLES_READY, csteps

            def z_coefficients(c):
                def times_qubit(result, at, q, factors, first, n):
                    cstep(dve.tensor_tensor(result[:, at:at + 2 * n].rearrange("p (a b) t -> p a b t", a=2),
                                            ry[:, q].unsqueeze(2).to_broadcast([P, 2, n, CT]),
                                            factors[:, first:first + n].unsqueeze(1).to_broadcast([P, 2, n, CT]),
                                            ALU.mult))

                times_qubit(z_coef, Z_BLOCK[1], 1, ry[:, 0], 0, 2)
                times_qubit(z_part, 0, 2, ry[:, 1], 0, 2)
                cjoin()
                times_qubit(z_coef, Z_BLOCK[2], 2, z_coef, Z_BLOCK[1], 4)
                times_qubit(z_part, 4, 3, z_part, 0, 4)
                cjoin()
                times_qubit(z_coef, Z_BLOCK[3], 3, z_coef, Z_BLOCK[2], 8)
                times_qubit(z_part, 12, 4, z_part, 4, 8)
                cjoin()
                times_qubit(z_coef, Z_BLOCK[4], 4, z_coef, Z_BLOCK[3], 16)
                times_qubit(z_coef, Z_BLOCK[0], 5, z_part, 12, 16)
                cjoin()
                times_qubit(z_coef, Z_BLOCK[5], 5, z_coef, Z_BLOCK[4], 32)

            def z_strings(qubits):
                def part(c):
                    for q in qubits:
                        k = len(Z_SUPPORT[q])
                        gather_products(dve, z_str, tables, CT, [2] * k, "ZX", Z_SUPPORT[q], Z_BLOCK[q],
                                        [2 ** i for i in range(k)], cstep)
                return part

            def z_weights(c):
                cjoin()
                cstep(dve.tensor_tensor(z_str, z_str, z_coef, ALU.mult))

            def z_sums(c):
                cjoin()
                for q in range(QUBITS):
                    k = 2 ** len(Z_SUPPORT[q])
                    cstep(dve.tensor_reduce(z_exp[:, q], z_str[:, Z_BLOCK[q]:Z_BLOCK[q] + k].rearrange("p k t -> p t k"),
                                            AX.X, ALU.add))

            def expectations(c):
                cjoin()
                cstep(dve.tensor_tensor(z_exp[:, :, :], z_exp[:, :, :], cos_of(2, 0), ALU.mult))
                dve.wait_ge(x_step, (c + 1) * X_DONE)
                cstep(dve.tensor_tensor(x_exp[:, :, :], x_exp[:, :, :], sin_of(2, 0), ALU.mult))
                cjoin()
                assert csteps[0] == (c + 1) * CIRCUIT_STEPS, csteps
                dve.tensor_tensor(ev[:, c * CT:(c + 1) * CT, 0:QUBITS].rearrange("p t q -> p q t"), z_exp[:, :, :],
                                  x_exp[:, :, :], ALU.subtract).then_inc(ev_done, 1)

            z_strings_low, z_strings_0, z_strings_5 = z_strings(range(1, QUBITS - 1)), z_strings([0]), z_strings([5])
            for part in (reduce_angles, rotations, bloch_tables, z_coefficients, z_strings_low, z_strings_0,
                         z_strings_5, z_weights, z_sums, expectations):
                part(0)

            base = steps[0]

            class Chain:
                def __init__(self, per):
                    self.per, self.start, self.n = per, 0, 0

                def begin(self, b):
                    self.start, self.n = b * self.per + base, 0

                def step(self, instruction):
                    self.n += 1
                    instruction.then_inc(dve_step, 1)

                def join(self):
                    dve.wait_ge(dve_step, self.start + self.n)

                def join_held(self):
                    self.join()
                    hold(dve)

                def end(self):
                    assert self.n == self.per, self.n

            chain = Chain(CHAIN)

            def stats1(b):
                dve.wait_ge(emb_copied, 2 * b + 2)
                hold(dve)
                for j in range(TILES):
                    chain.step(dve.bn_stats(bn1[:, j, :], hres[:, bass.ds(b * TILES + j, 1), :].rearrange("p o d -> p (o d)")))
                chain.join_held()
                for j in range(TILES):
                    chain.step(dve.bn_aggr(mv1[:, j, :], bn1[:, j, :]))
                chain.join()
                dve.tensor_scalar(ve1[:, :], mv1[:, :, 1], EPS, None, ALU.add).then_inc(var1_done, 1)

            def features(b):
                dve.wait_ge(rs1_done, b + 1)
                if not (isinstance(b, int) and b == 0):
                    dve.wait_ge(ut_done, b)
                dve.tensor_tensor(u_b[:, :, 0:FEATURES - 1], ev[:, bass.ds(b * TILES, TILES), 0:FEATURES - 1],
                                  rs1[:, :].unsqueeze(2).to_broadcast([P, TILES, FEATURES - 1]), ALU.mult
                                  ).then_inc(u_done, 1)

            def norm2(b, kept, s):
                i = b * TILES + s
                dve.wait_ge(rs2_done, i + 1)
                dve.tensor_scalar(x2[:, kept, s, 0:D], hres[:, bass.ds(i, 1), :].rearrange("p o d -> p (o d)"),
                                  mv2[:, s % 2, 0:1], rs2[:, s % 2:s % 2 + 1], ALU.subtract, ALU.mult
                                  ).then_inc(x2_done, 1)

            def row_max(b, s):
                i = b * TILES + s
                dve.wait_ge(score_done, i + 1)
                if not (isinstance(b, int) and b == 0 and s < 2):
                    dve.wait_ge(exp_done, i - 1)
                dve.tensor_reduce(nmax[:, s % 2:s % 2 + 1], (b4, b5)[s % 2][:, :], AX.X, ALU.max, negate=True
                                  ).then_inc(max_done, 1)

            def residual(b, s):
                i = b * TILES + s
                c = s % 2
                chain.step(dve.reciprocal(rinv[:, s:s + 1], rsum[:, s:s + 1]))
                dve.wait_ge(pv_done, i + 1)
                chain.join()
                row = hres[:, bass.ds(i, 1), :].rearrange("p o d -> p (o d)")
                dve.scalar_tensor_tensor(row, b7[:, 0:D], rinv[:, s:s + 1], row, ALU.mult, ALU.add).then_inc(h2_done, 1)
                dve.wait_ge(h2_done, i + 1)
                hold(dve)
                chain.step(dve.bn_stats(bn2[:, c, :], row))
                chain.join_held()
                chain.step(dve.bn_aggr(mv2[:, c, :], bn2[:, c, :]))
                chain.join()
                dve.tensor_scalar(ve2[:, c:c + 1], mv2[:, c, 1:2], EPS, None, ALU.add).then_inc(var2_done, 1)

            def logit_copy(b):
                dve.wait_ge(logit_done, b * TILES + TILES)
                dve.tensor_copy(logit[:, :, :].rearrange("p j e -> p (j e)"),
                                b1[:, 256:256 + TILES * E]).then_inc(logit_copied, 1)

            def route_a(b, par):
                dve.wait_ge(logit_copied, b + 1)
                hold(dve)
                for j in range(TILES):
                    chain.step(dve.max(top[:, j, :], logit[:, j, :]))
                chain.join_held()
                for j in range(TILES):
                    chain.step(dve.max_index(top_i[:, j, :], top[:, j, :], logit[:, j, :]))
                dve.tensor_tensor(gap[:, :], top[:, :, 1], top[:, :, 0], ALU.subtract).then_inc(gap_done, 1)
                chain.join()
                chain.step(dve.tensor_copy(x2[:, par, :, D:D + 2], top_i[:, :, 0:2]))
                chain.step(dve.tensor_copy(x2[:, par, :, D + 4], tok[:, bass.ds(b * TILES, TILES)]))
                chain.join()
                chain.step(dve.tensor_tensor(
                    mask[:, :, :, :], x2[:, par, :, D:D + 2].rearrange("p j k -> p k j").unsqueeze(3).to_broadcast([P, 2, TILES, E]),
                    exp_f[:, :].unsqueeze(1).unsqueeze(1).to_broadcast([P, 2, TILES, E]), ALU.is_equal))
                chain.join()
                chain.step(dve.tensor_tensor(both[:, :, :], mask[:, 0], mask[:, 1], ALU.add))
                chain.join()
                chain.step(dve.tensor_copy(ahead[:, 1, :], both[:, 0, :]))
                chain.step(dve.tensor_tensor(ahead[:, 2, :], both[:, 0, :], both[:, 1, :], ALU.add))
                chain.join()
                chain.step(dve.tensor_tensor(ahead[:, 3, :], ahead[:, 2, :], both[:, 2, :], ALU.add))
                chain.join()
                chain.step(dve.tensor_tensor(here[:, :], ahead[:, 3, :], both[:, 3, :], ALU.add))
                chain.join()
                dve.tensor_copy(here_b[:, :], here[:, :]).then_inc(mask_done, 1)

            def rank_copy(b):
                dve.wait_ge(rank_done, b + 1)
                dve.tensor_tensor(rank[:, :], b1[:, 288:288 + E], region_f[:, :], ALU.add).then_inc(rank_copied, 1)

            def route_b(b, par):
                dve.wait_ge(gap_exp, b + 1)
                chain.step(dve.tensor_scalar(gap_1[:, :], gap_e[:, :], 1.0, None, ALU.add))
                chain.join()
                chain.step(dve.reciprocal(x2[:, par, :, D + 2], gap_1[:, :]))
                chain.join()
                chain.step(dve.tensor_tensor(x2[:, par, :, D + 3], x2[:, par, :, D + 2], gap_e[:, :], ALU.mult))
                chain.step(dve.tensor_tensor(so_far[:, :], so_far[:, :], here[:, :], ALU.add))
                dve.wait_ge(rank_copied, b + 1)
                chain.step(dve.tensor_tensor(place[:, :, :], ahead[:, :, :],
                                             rank[:, :].unsqueeze(1).to_broadcast([P, TILES, E]), ALU.add))
                chain.join()
                chain.step(dve.tensor_tensor(slot_e[:, :, :, :], mask[:, :, :, :],
                                             place[:, :, :].unsqueeze(1).to_broadcast([P, 2, TILES, E]), ALU.mult))
                chain.join()
                chain.step(dve.tensor_reduce(slot_f[:, :, :], slot_e[:, :, :, :], AX.X, ALU.add))
                chain.join()
                dve.tensor_copy(slot[:, par, :, :], slot_f[:, :, :]).then_inc(slot_done, 1)

            dve.wait_ge(const_done, 1)
            chain.begin(0)
            stats1(0)
            features(0)
            reduce_angles(1)
            base = base + chain.n
            row_max(0, 0)

            def batch(b, kept, first=False, scattered_before=True, last=False, parts=((), (), (), ())):
                before_kept = (kept - 1) % KEPT
                chain.begin(b)
                row_max(b, 1)
                if not first:
                    norm2(b - 1, before_kept, 2)
                if not last:
                    stats1(b + 1)
                if not first:
                    residual(b - 1, 3)
                for part in parts[0]:
                    part(1)
                row_max(b, 2)
                if not first:
                    norm2(b - 1, before_kept, 3)
                if not last:
                    features(b + 1)
                for part in parts[1]:
                    part(1)
                residual(b, 0)
                row_max(b, 3)
                if not first:
                    logit_copy(b - 1)
                if not first:
                    route_a(b - 1, before_kept)
                if scattered_before:
                    dve.wait_ge(scattered, b * (16 * 2 * TILES) - 16 * 2 * TILES)
                norm2(b, kept, 0)
                for part in parts[2]:
                    part(1)
                residual(b, 1)
                if not last:
                    row_max(b + 1, 0)
                norm2(b, kept, 1)
                if not first:
                    rank_copy(b - 1)
                    route_b(b - 1, before_kept)
                for part in parts[3]:
                    part(1)
                residual(b, 2)

            batch(0, 0, first=True, scattered_before=False,
                  parts=((rotations,), (bloch_tables,), (z_coefficients,), (z_strings_low,)))
            base = base + chain.n - CHAIN
            batch(1, 1, scattered_before=False,
                  parts=((z_strings_0,), (z_strings_5,), (z_weights,), (z_sums,)))
            batch(2, 0, parts=((expectations,), (), (), ()))
            with dve.Fori(0, (BATCHES - 4) // KEPT) as i:
                for k in range(KEPT):
                    batch(KEPT * i + k + 3, (k + 3) % KEPT)
                    chain.end()
            batch(BATCHES - 1, (BATCHES - 1) % KEPT, last=True)
            final, final_kept = BATCHES - 1, (BATCHES - 1) % KEPT
            norm2(final, final_kept, 2)
            residual(final, 3)
            norm2(final, final_kept, 3)
            logit_copy(final)
            route_a(final, final_kept)
            rank_copy(final)
            route_b(final, final_kept)

            dve.wait_ge(count_done, 1)
            dve.tensor_copy(count[:, :], b1[:, 304:304 + E]).then_inc(count_copied, 1)
            dve.tensor_copy(count_i[:, :], b1[:, 304:304 + E]).then_inc(count_copied, 1)
            dve.wait_ge(count_copied, 2)
            chain.step(dve.tensor_scalar(count[:, :], count[:, :], float(P - 1), None, ALU.add))
            chain.join()
            chain.step(dve.tensor_copy(nblk_i[:, :], count[:, :]))
            chain.join()
            chain.step(dve.tensor_scalar(nblk_i[:, :], nblk_i[:, :], 7, None, ALU.arith_shift_right))
            chain.join()
            chain.step(dve.tensor_copy(nblk[:, :], nblk_i[:, :]))
            chain.join()
            chain.step(dve.tensor_copy(cum[:, 0, :], nblk[:, :]))
            chain.step(dve.tensor_scalar(skip[:, :], nblk[:, :], -float(P), float(REGION), ALU.mult, ALU.add))
            chain.join()
            c = 0
            for shift in (1, 2, 4):
                chain.step(dve.tensor_copy(cum[:, 1 - c, 0:shift], cum[:, c, 0:shift]))
                chain.step(dve.tensor_tensor(cum[:, 1 - c, shift:E], cum[:, c, shift:E], cum[:, c, 0:E - shift], ALU.add))
                chain.join()
                c = 1 - c
            chain.step(dve.tensor_tensor(ge[:, :, :], blk[:, :].unsqueeze(1).to_broadcast([P, E, BLOCKS]),
                                         cum[:, c, :].unsqueeze(2).to_broadcast([P, E, BLOCKS]), ALU.is_ge))
            chain.join()
            past = ge[:, 0:E - 1, :]
            chain.step(dve.tensor_reduce(t_exp[:, :], past.rearrange("p e m -> p m e"), AX.X, ALU.add))
            chain.step(dve.memset(t_pair[:, :], 0.0))
            chain.join()
            chain.step(dve.tensor_scalar(t_pair[:, 0:BLOCKS - AHEAD], t_exp[:, AHEAD:BLOCKS], float(E), None, ALU.mult))
            chain.join()
            chain.step(dve.tensor_tensor(t_pair[:, :], t_pair[:, :], t_exp[:, :], ALU.add))
            for values, result in ((skip, t_row), (nblk, t_first)):
                chain.step(dve.tensor_tensor(ge_w[:, :, :], past, values[:, 0:E - 1].unsqueeze(2).to_broadcast(
                    [P, E - 1, BLOCKS]), ALU.mult))
                chain.join()
                chain.step(dve.tensor_reduce(result[:, :], ge_w[:, :, :].rearrange("p e m -> p m e"), AX.X, ALU.add))
                chain.join()
            chain.step(dve.scalar_tensor_tensor(t_row[:, :], blk[:, :], float(P), t_row[:, :], ALU.mult, ALU.add))
            chain.join()
            chain.step(dve.tensor_scalar(t_row[:, :], t_row[:, :], -float(PAD_ROW), None, ALU.add))
            chain.join()
            chain.step(dve.tensor_tensor(ge_w[:, 0, :], t_row[:, :], ge[:, E - 1, :], ALU.mult))
            chain.join()
            chain.step(dve.tensor_tensor(t_row[:, :], t_row[:, :], ge_w[:, 0, :], ALU.subtract))
            chain.join()
            chain.step(dve.tensor_scalar(t_row[:, :], t_row[:, :], float(PAD_ROW), None, ALU.add))
            chain.join()
            dve.tensor_copy(t_i[:, 0, :], t_exp[:, :])
            dve.tensor_copy(t_i[:, 2, :], t_first[:, :])
            dve.tensor_copy(t_i[:, 3, :], t_pair[:, :])
            dve.tensor_copy(t_i[:, 1, :], t_row[:, :]).then_inc(table_done, 1)

            def share_of(m, n, round_of):
                dve.wait_ge(block_in[n], round_of * 16)
                dve.scalar_tensor_tensor(share_w[:, n, :], xb[:, n, D:D + 2], t_exp[:, bass.ds(m, 1)],
                                         xb[:, n, D + 2:D + 4], ALU.is_equal, ALU.mult,
                                         accum_out=share[:, n:n + 1]).then_inc(share_done, 1)
                dve.tensor_copy(dest[:, n:n + 1], xb[:, n, D + 4:D + 5]).then_inc(share_done, 1)

            def up_copy(m, n, e, free):
                if free:
                    dve.wait_ge(up_done, m - 3)
                dve.tensor_copy(up_now0[:, n, :], up0[:, bass.ds(e * HID, HID)]).then_inc(up0_copied, 1)

            def biased(m, n, e):
                dve.wait_ge(y_mm, m + 1)
                dve.tensor_tensor(y_raw[:, n % 2, :], (b5, b6)[n % 2][:, 0:D],
                                  down_bias[:, bass.ds(e * D, D)], ALU.add).then_inc(y_read, 1)

            def weighted(m, n):
                dve.wait_ge(y_read, m + 1)
                dve.wait_ge(share_done, m * 2 + 2)
                dve.tensor_scalar(y[:, n, :], y_raw[:, n % 2, :], share[:, n:n + 1], None, ALU.mult
                                  ).then_inc(y_done, 1)

            dve.wait_ge(down_in, 16 * (BATCHES - 1))
            dve.wait_ge(table_done, 1)
            dve.wait_ge(added[0], 16)
            for m in range(AHEAD):
                up_copy(m, m, dve.value_load(t_i[0:1, 0, m:m + 1], min_val=0, max_val=E - 1), False)
            share_of(0, 0, 1)

            def expert_block(m, n, it, more, more_weights):
                experts = dve.value_load(t_i[0:1, 3, bass.ds(m, 1)], min_val=0, max_val=E * E - 1)
                e_ahead = experts // E
                if more_weights:
                    up_copy(m + AHEAD, (n + AHEAD) % UNROLL, e_ahead, not (isinstance(m, int) and m == 0))
                biased(m, n, experts % E)
                if more:
                    dve.wait_ge(added[(n + 1) % UNROLL], (it + (n + 1) // UNROLL) * 16 + 16)
                    share_of(m + 1, (n + 1) % UNROLL, it + 1 + (n + 1) // UNROLL)
                weighted(m, n)

            rounds = BLOCKS // UNROLL
            for n in range(UNROLL):
                expert_block(n, n, 0, True, True)
            with dve.Fori(1, rounds - 1) as it:
                for n in range(UNROLL):
                    expert_block(it * UNROLL + n, n, it, True, True)
            for n in range(UNROLL):
                expert_block((rounds - 1) * UNROLL + n, n, rounds - 1, n < UNROLL - 1, n < UNROLL - 3)

        @block.scalar
        def _(act):
            def trig(c):
                act.wait_ge(circuit_step, c * CIRCUIT_STEPS + REDUCED)
                act.activation(sine[:, :, :], turned.rearrange("p t f -> p f t"), ACT.Sin).then_inc(trig_done, 1)
                act.wait_ge(circuit_step, c * CIRCUIT_STEPS + REDUCED + 1)
                act.activation(cosine[:, :, :], folded.rearrange("p t f -> p f t"), ACT.Sin,
                               bias=half_pi[:, 0:1], scale=-1.0).then_inc(trig_done, 1)

            act.wait_ge(dve_step, HALF_PI_READY)
            trig(0)

            def evt_copy(b):
                act.wait_ge(evt_done, b + 1)
                act.copy(ev_t[:, :], b2[:, 0:P]).then_inc(evt_copied, 1)

            def emb_copy(b, half):
                act.wait_ge(emb_done, 2 * b + half + 1)
                hold(act)
                act.copy(hres[:, bass.ds(b * TILES + 2 * half, 2), :],
                         emb_bank(b, half)[:, 0:2 * D].rearrange("p (j d) -> p j d", j=2)).then_inc(emb_copied, 1)

            def val_copy(b, half):
                act.wait_ge(val_done, 2 * b + half + 1)
                if not (isinstance(b, int) and b == 0):
                    act.wait_ge(pv_done, b * TILES)
                act.copy(val[:, 2 * half:2 * half + 2, :],
                         (b2, b3)[half][:, 0:2 * D].rearrange("p (j d) -> p j d", j=2)).then_inc(val_copied, 1)

            def pt_copy(b, s):
                act.wait_ge(pt_done, b * TILES + s + 1)
                if not (isinstance(b, int) and b == 0 and s < 2):
                    act.wait_ge(pv_done, b * TILES + s - 1)
                act.copy(prob_t[:, s % 2, :], b6[:, :]).then_inc(pt_copied, 1)

            def ut_copy(b, kept):
                act.wait_ge(ut_done, b + 1)
                for j in range(TILES):
                    rows = slice(j * EV_STRIDE, (j + 1) * EV_STRIDE)
                    copied = act.copy(ut[rows, kept, j * P:(j + 1) * P], b3[rows, 0:P])
                copied.then_inc(ut_copied, 1)

            def tq_copy(b):
                act.wait_ge(tq_done, b + 1)
                act.copy(tq[:, :], b2[:, :]).then_inc(tq_copied, 1)

            def softmax(b, s):
                i = b * TILES + s
                act.wait_ge(max_done, i + 1)
                if not (isinstance(b, int) and b == 0 and s < 2):
                    act.wait_ge(pt_done, i - 1)
                if not (isinstance(b, int) and b == 0):
                    act.wait_ge(h2_done, i - 3)
                act.activation(prob[:, s % 2, :], (b4, b5)[s % 2][:, :], ACT.Exp, bias=nmax[:, s % 2:s % 2 + 1],
                               accum_out=rsum[:, s:s + 1]).then_inc(exp_done, 1)

            def x2t_copy(b, s):
                act.wait_ge(x2t_done, b * TILES + s + 1)
                act.copy(x2t0[:, :], b1[:, 0:P])
                act.copy(x2t1[:, :], b1[0:D1, P:2 * P]).then_inc(x2t_copied, 1)

            def gap_exponent(b):
                act.wait_ge(gap_done, b + 1)
                act.activation(gap_e[:, :], gap[:, :], ACT.Exp).then_inc(gap_exp, 1)

            evt_copy(0)
            emb_copy(0, 0)
            emb_copy(0, 1)
            ut_copy(0, 0)
            tq_copy(0)
            trig(1)
            evt_copy(1)
            softmax(0, 0)
            emb_copy(1, 0)

            def batch(b, kept, first=False, last=False):
                if not last:
                    emb_copy(b + 1, 1)
                softmax(b, 1)
                pt_copy(b, 0)
                if not first:
                    x2t_copy(b - 1, 2)
                val_copy(b, 0)
                val_copy(b, 1)
                softmax(b, 2)
                pt_copy(b, 1)
                if not first:
                    x2t_copy(b - 1, 3)
                if not last:
                    ut_copy(b + 1, (kept + 1) % KEPT)
                softmax(b, 3)
                pt_copy(b, 2)
                if not last:
                    tq_copy(b + 1)
                x2t_copy(b, 0)
                pt_copy(b, 3)
                if not last:
                    evt_copy(b + 2)
                    softmax(b + 1, 0)
                if not last:
                    emb_copy(b + 2, 0)
                x2t_copy(b, 1)
                if not first:
                    gap_exponent(b - 1)

            batch(0, 0, first=True)
            batch(1, 1)
            batch(2, 0)
            with act.Fori(0, (BATCHES - 4) // KEPT) as i:
                for k in range(KEPT):
                    batch(KEPT * i + k + 3, (k + 3) % KEPT)
            batch(BATCHES - 1, (BATCHES - 1) % KEPT, last=True)
            x2t_copy(BATCHES - 1, 2)
            x2t_copy(BATCHES - 1, 3)
            gap_exponent(BATCHES - 1)

            def xbt_copy(m, n):
                act.wait_ge(xbt_done, m + 1)
                act.copy(xbt0[:, n % 2, :], b0[:, 0:P])
                act.copy(xbt1[0:D1, n % 2, :], b0[0:D1, P:2 * P]).then_inc(xbt_copied, 1)

            def gelu(m, n):
                act.wait_ge(up_done, m + 1)
                act.activation(hid[:, n % 2, :], (b1, b2)[n % 2][:, 0:HID], ACT.Gelu).then_inc(gelu_done, 1)

            def up_copy(m, n):
                e = act.value_load(t_i[0:1, 0, bass.ds(m, 1)], min_val=0, max_val=E - 1)
                act.copy(up_now1[:, n, :], up1[:, bass.ds(e * HID, HID)]).then_inc(up1_copied, 1)

            act.activation(gelu_ahead[:, :], half_pi[:, 0:1], ACT.Gelu)
            act.wait_ge(up_in, 32)
            act.wait_ge(table_done, 1)
            up_copy(0, 0)
            up_copy(1, 1)
            xbt_copy(0, 0)
            xbt_copy(1, 1)
            gelu(0, 0)

            def expert_block(m, n, ahead):
                if ahead:
                    xbt_copy(m + 2, n)
                    up_copy(m + 2, (n + 2) % UNROLL)
                gelu(m + 1, n + 1)

            with act.Fori(0, BLOCKS // UNROLL - 1) as it:
                for n in range(UNROLL):
                    expert_block(it * UNROLL + n, n, True)
            for n in range(UNROLL - 1):
                expert_block(BLOCKS - UNROLL + n, n, n < UNROLL - 2)

        @block.tensor
        def _(pe):
            pe.wait_ge(ident_done, 1)
            pe.wait_ge(small_in, 16 * 6)
            pe.wait_ge(centered, 1)
            pe.transpose(b4[:, 0:P], lift[:, 0:P], ident[:, :])
            pe.transpose(b4[0:K1, P:2 * P], lift[:, P:D + 1], ident[:, :]).then_inc(lift_done, 1)
            pe.wait_ge(lift_copied, 1)
            pe.matmul(b5[:, 0:D], lift_t0[:, :], wqkv0[:, 2 * D:3 * D], start=True, stop=False)
            pe.matmul(b5[:, 0:D], lift_t1[:, :], wqkv1[:, 2 * D:3 * D], start=False, stop=True)
            for i, dst in enumerate((b6, b7)):
                for at, first, m in ((0, i * D, P), (P, i * D + P, D1)):
                    pe.matmul(dst[0:m, at:at + P], wqkv0[:, first:first + m], lift_t0[:, :], start=True, stop=False)
                    mm = pe.matmul(dst[0:m, at:at + P], wqkv1[:, first:first + m], lift_t1[:, :], start=False, stop=True)
            mm.then_inc(lifted_done, 1)
            pe.wait_ge(lift_copied, 2)
            pe.matmul(b4[:, 0:P], lifted_qk0[:, 0, :], lifted_qk0[:, 1, :], start=True, stop=False)
            pe.matmul(b4[:, 0:P], lifted_qk1[:, 0, :], lifted_qk1[:, 1, :], start=False, stop=True
                      ).then_inc(lifted_done, 1)
            pe.wait_ge(lift_copied, 3)

            def ev_transpose(b):
                pe.wait_ge(ev_copied, b + 1)
                if not (isinstance(b, int) and b == 0):
                    pe.wait_ge(tq_copied, b)
                pe.transpose(b2[:, 0:P], ev_b[:, :], ident[:, :]).then_inc(evt_done, 1)

            def embed(b, half):
                if half == 0:
                    pe.wait_ge(evt_copied, b + 1)
                    if not (isinstance(b, int) and b == 0):
                        pe.wait_ge(emb_copied, 2 * b)
                elif not (isinstance(b, int) and b == 0):
                    pe.wait_ge(emb_copied, 2 * b + 1)
                dst = emb_bank(b, half)
                for j in range(2):
                    mm = pe.matmul(dst[:, j * D:(j + 1) * D], ev_t[:, :], wz[:, 2 * half + j, :], start=True, stop=True)
                mm.then_inc(emb_done, 1)

            def feature_transpose(b):
                pe.wait_ge(u_done, b + 1)
                if not (isinstance(b, int) and b == 0):
                    pe.wait_ge(val_copied, 2 * b)
                pe.transpose(b3[:, 0:P], u_b[:, :, :].rearrange("p j e -> p (j e)"), ident[:, :]).then_inc(ut_done, 1)

            def score_factor(b, kept):
                pe.wait_ge(ut_copied, b + 1)
                pe.matmul(b2[:, :], score_w[:, :], ut[:, kept, :], start=True, stop=True).then_inc(tq_done, 1)

            def values(b, kept, half):
                dst = (b2, b3)[half]
                for j in range(2):
                    t = slice((2 * half + j) * P, (2 * half + j + 1) * P)
                    mm = pe.matmul(dst[:, j * D:(j + 1) * D], ut[:, kept, t], lifted_v[:, :], start=True, stop=True)
                mm.then_inc(val_done, 1)

            def scores(b, kept, s):
                i = b * TILES + s
                if s == 0:
                    pe.wait_ge(tq_copied, b + 1)
                if not (isinstance(b, int) and b == 0 and s < 2):
                    pe.wait_ge(exp_done, i - 1)
                pe.matmul((b4, b5)[s % 2][:, :], tq[:, s * P:(s + 1) * P], ut[:, kept, :], start=True, stop=True
                          ).then_inc(score_done, 1)

            def p_transposes(b, s):
                i = b * TILES + s
                pe.wait_ge(exp_done, i + 1)
                if not (isinstance(b, int) and b == 0 and s == 0):
                    pe.wait_ge(pt_copied, i)
                for k in range(TILES):
                    mm = pe.transpose(b6[:, k * P:(k + 1) * P], prob[:, s % 2, k * P:(k + 1) * P], ident[:, :])
                mm.then_inc(pt_done, 1)

            def context(b, s):
                i = b * TILES + s
                if s == 0:
                    pe.wait_ge(val_copied, 2 * b + 2)
                pe.wait_ge(pt_copied, i + 1)
                if not (isinstance(b, int) and b == 0 and s == 0):
                    pe.wait_ge(h2_done, i)
                for k in range(TILES):
                    mm = pe.matmul(b7[:, 0:D], prob_t[:, s % 2, k * P:(k + 1) * P], val[:, k, :],
                                   start=(k == 0), stop=(k == TILES - 1))
                mm.then_inc(pv_done, 1)

            def x2_transposes(b, kept, s):
                pe.wait_ge(x2_done, b * TILES + s + 1)
                if s == 0 and not (isinstance(b, int) and b == 0):
                    pe.wait_ge(logit_copied, b)
                if s == 1 and not (isinstance(b, int) and b == 0):
                    pe.wait_ge(rank_copied, b)
                pe.transpose(b1[:, 0:P], x2[:, kept, s, 0:P], ident[:, :])
                pe.transpose(b1[0:D1, P:2 * P], x2[:, kept, s, P:D], ident[:, :]).then_inc(x2t_done, 1)

            def gate(b, s):
                pe.wait_ge(x2t_copied, b * TILES + s + 1)
                dst = b1[:, 256 + s * E:256 + (s + 1) * E]
                pe.matmul(dst, x2t0[:, :], wg0[:, :], start=True, stop=False)
                pe.matmul(dst, x2t1[:, :], wg1[:, :], start=False, stop=True).then_inc(logit_done, 1)

            def ranks(b):
                if isinstance(b, int) and b == 0:
                    pe.wait_ge(const_done, 1)
                pe.wait_ge(mask_done, b + 1)
                pe.matmul(b1[:, 288:288 + E], before[:, :], here_b[:, :], start=True, stop=False)
                pe.matmul(b1[:, 288:288 + E], ones_b[:, :], so_far[:, :], start=False, stop=True).then_inc(rank_done, 1)

            ev_transpose(0)
            embed(0, 0)
            embed(0, 1)
            feature_transpose(0)
            score_factor(0, 0)
            scores(0, 0, 0)
            ev_transpose(1)
            embed(1, 0)

            def batch(b, kept, first=False, last=False):
                before_kept, next_kept = (kept - 1) % KEPT, (kept + 1) % KEPT
                scores(b, kept, 1)
                if not first:
                    gate(b - 1, 1)
                if not last:
                    embed(b + 1, 1)
                p_transposes(b, 0)
                if not first:
                    context(b - 1, 3)
                values(b, kept, 0)
                values(b, kept, 1)
                if not first:
                    x2_transposes(b - 1, before_kept, 2)
                scores(b, kept, 2)
                if not first:
                    gate(b - 1, 2)
                p_transposes(b, 1)
                context(b, 0)
                if not first:
                    x2_transposes(b - 1, before_kept, 3)
                scores(b, kept, 3)
                if not first:
                    gate(b - 1, 3)
                if not last:
                    feature_transpose(b + 1)
                p_transposes(b, 2)
                context(b, 1)
                if not last:
                    score_factor(b + 1, next_kept)
                x2_transposes(b, kept, 0)
                p_transposes(b, 3)
                if not last:
                    scores(b + 1, next_kept, 0)
                gate(b, 0)
                if not last:
                    ev_transpose(b + 2)
                if not first:
                    ranks(b - 1)
                if not last:
                    embed(b + 2, 0)
                context(b, 2)
                x2_transposes(b, kept, 1)

            batch(0, 0, first=True)
            batch(1, 1)
            batch(2, 0)
            with pe.Fori(0, (BATCHES - 4) // KEPT) as i:
                for k in range(KEPT):
                    batch(KEPT * i + k + 3, (k + 3) % KEPT)
            batch(BATCHES - 1, (BATCHES - 1) % KEPT, last=True)
            final, final_kept = BATCHES - 1, (BATCHES - 1) % KEPT
            gate(final, 1)
            context(final, 3)
            x2_transposes(final, final_kept, 2)
            gate(final, 2)
            x2_transposes(final, final_kept, 3)
            gate(final, 3)
            ranks(final)
            pe.wait_ge(slot_done, BATCHES)
            pe.matmul(b1[:, 304:304 + E], ones_b[:, :], so_far[:, :], start=True, stop=True).then_inc(count_done, 1)

            def block_transposes(m, n, round_of):
                pe.wait_ge(block_in[n], round_of * 16)
                if not (isinstance(m, int) and m == 0):
                    pe.wait_ge(xbt_copied, m)
                pe.transpose(b0[:, 0:P], xb[:, n, 0:P], ident[:, :])
                pe.transpose(b0[0:D1, P:2 * P], xb[:, n, P:D], ident[:, :]).then_inc(xbt_done, 1)

            def up_proj(m, n):
                pe.wait_ge(xbt_copied, m + 1)
                pe.wait_ge(up0_copied, m + 1)
                pe.wait_ge(up1_copied, m + 1)
                for c in range(HC):
                    dst, cols = (b1, b2)[n % 2][:, c * P:(c + 1) * P], slice(c * P, (c + 1) * P)
                    pe.matmul(dst, up_now0[:, n, cols], xbt0[:, n % 2, :], start=True, stop=False)
                    mm = pe.matmul(dst, up_now1[:, n, cols], xbt1[:, n % 2, :], start=False, stop=True)
                mm.then_inc(up_done, 1)

            def down_proj(m, n, e, first):
                pe.wait_ge(gelu_done, m + 1)
                if not (first and n < 2):
                    pe.wait_ge(y_read, m - 1)
                for c in range(HC):
                    mm = pe.matmul((b5, b6)[n % 2][:, 0:D], hid[:, n % 2, c * P:(c + 1) * P],
                                   down[:, bass.ds(e * (HC * D) + c * D, D)], start=(c == 0), stop=(c == HC - 1))
                mm.then_inc(y_mm, 1)

            pe.wait_ge(up_in, 32)
            pe.wait_ge(down_in, 16 * (BATCHES - 1))
            pe.wait_ge(table_done, 1)
            block_transposes(0, 0, 1)
            block_transposes(1, 1, 1)
            up_proj(0, 0)

            def expert_block(m, n, it, ahead1, ahead2, first):
                if ahead2:
                    block_transposes(m + 2, (n + 2) % UNROLL, it + 1 + (n + 2) // UNROLL)
                e = pe.value_load(t_i[0:1, 0, bass.ds(m, 1)], min_val=0, max_val=E - 1)
                if ahead1:
                    up_proj(m + 1, (n + 1) % UNROLL)
                down_proj(m, n, e, first)

            rounds = BLOCKS // UNROLL
            for n in range(UNROLL):
                expert_block(n, n, 0, True, True, True)
            with pe.Fori(1, rounds - 1) as it:
                for n in range(UNROLL):
                    expert_block(it * UNROLL + n, n, it, True, True, False)
            for n in range(UNROLL):
                expert_block((rounds - 1) * UNROLL + n, n, rounds - 1, n < UNROLL - 1, n < UNROLL - 2, False)


def kernel(x, L0_tok_quantum_params, L0_tok_post_w, L0_tok_post_b, L0_attn_W_qkv, L0_attn_b_qkv, L0_ffn_Wg,
           L0_ffn_W1, L0_ffn_b1, L0_ffn_W2, L0_ffn_b2):
    import concourse.bacc as bacc
    from concourse.bass_utils import run_bass_kernel_spmd

    x = np.ascontiguousarray(x)
    vocab = L0_tok_quantum_params.shape[0]
    embed = L0_tok_post_w.shape[0]
    experts, _, hidden = L0_ffn_W1.shape
    tiles = x.shape[1] // 128
    emb_w = np.zeros((tiles, 128 // tiles, tiles, embed), np.float32)
    for j in range(tiles):
        emb_w[j, 0:QUBITS, j] = np.asarray(L0_tok_post_w).T
        emb_w[j, QUBITS, j] = L0_tok_post_b
    emb_rows = np.zeros((tiles, 128 // tiles, embed + 1), np.float32)
    emb_rows[:, 0:QUBITS, 0:embed] = np.asarray(L0_tok_post_w).T
    emb_rows[:, QUBITS, 0:embed] = L0_tok_post_b
    emb_rows[:, QUBITS + 1, embed] = 1.0
    arrays = {
        "token_ids": x,
        "angles": np.ascontiguousarray(L0_tok_quantum_params).reshape(vocab, ANGLES),
        "emb_w": emb_w.reshape(128, tiles * embed),
        "emb_rows": emb_rows.reshape(128, embed + 1),
        "qkv_w": np.concatenate([L0_attn_W_qkv, np.asarray(L0_attn_b_qkv)[None]], 0),
        "gate_w": np.ascontiguousarray(L0_ffn_Wg),
        "up_w": np.concatenate([L0_ffn_W1, np.asarray(L0_ffn_b1)[:, None]], 1).transpose(1, 0, 2).reshape(
            embed + 1, experts * hidden),
        "down_w": np.asarray(L0_ffn_W2).reshape(experts, hidden // 128, 128, embed).transpose(2, 0, 1, 3).reshape(
            128, experts * hidden // 128 * embed),
        "down_b": np.ascontiguousarray(L0_ffn_b2).reshape(experts * embed),
    }
    nc = bacc.Bacc("TRN2", target_bir_lowering=False, num_devices=1)
    aps = []
    for name in arrays:
        arrays[name] = np.ascontiguousarray(arrays[name])
        aps.append(nc.dram_tensor(name, arrays[name].shape, mybir.dt.from_np(arrays[name].dtype),
                                  kind="ExternalInput").ap())
    out = nc.dram_tensor("out", (x.shape[0], x.shape[1], embed), F32, kind="ExternalOutput").ap()
    build(nc, *aps, out)
    result = run_bass_kernel_spmd(nc, [arrays], core_ids=[0])
    return result.results[0]["out"]
```
